# Optimizing a Trainium2 kernel written in Bass

```python
import numpy as np
import jax
import jax.numpy as jnp

def _softmax(x, axis=-1):
    return jax.nn.softmax(x, axis=axis)

def _gelu(x):
    return jax.nn.gelu(x, approximate=True)

def _silu(x):
    return jax.nn.silu(x)

def _sigmoid(x):
    return jax.nn.sigmoid(x)

def _layernorm(x, axis=-1, eps=1e-05):
    m = jnp.mean(x, axis=axis, keepdims=True)
    v = jnp.var(x, axis=axis, keepdims=True)
    return (x - m) / jnp.sqrt(v + eps)

def _scatter_add(tgt, idx, src, axis=0):
    return tgt.at[idx].add(src)

def _segment_sum(src, seg, n):
    return jax.ops.segment_sum(src, seg, n)
kernel_name = 'mk_perceiver_d1_seqx_r4_aa30f0'

def setup_inputs(seed: int=0):
    np.random.seed(seed)
    _w = jnp.asarray

    def _rec_inputs():
        import jax
        import jax.numpy as jnp
        _rk = jax.random.key(seed)
        x = 7.22e-05 + 1 * jax.random.normal(jax.random.fold_in(_rk, 1), (128, 32, 256), jnp.float32)
        _lenS = 32 - jax.random.randint(jax.random.fold_in(_rk, 7), (128,), 0, max(1, 32 // 4) + 1, jnp.int32)
        _lenS2 = 257 - jax.random.randint(jax.random.fold_in(_rk, 8), (128,), 0, max(1, 257 // 4) + 1, jnp.int32)
        _ctx_1024P = jax.random.normal(jax.random.fold_in(_rk, 11), (128, 16, 256), jnp.float32)
        _ctx_1024c = jax.random.dirichlet(jax.random.fold_in(_rk, 511), 0.3 * jnp.ones((16,), jnp.float32), (128, 257))
        _ctx_1024t = jnp.einsum('bsk,bkd->bsd', _ctx_1024c, _ctx_1024P)
        _ctx_1024t = _ctx_1024t * jax.lax.rsqrt(jnp.mean(jnp.square(_ctx_1024t)) + 1e-12) * 0.953939
        ctx_1024 = 4.13588e-05 + 0.999923 * (_ctx_1024t + 0.3 * jax.random.normal(jax.random.fold_in(_rk, 611), (128, 257, 256), jnp.float32))
        return (x, ctx_1024)
    x, ctx_1024 = _rec_inputs()

    def _L0_xattn_setup():
        import jax, jax.numpy as jnp
        import numpy as np
        D_MODEL = 256
        NUM_HEADS = 16
        D_K = D_MODEL // NUM_HEADS
        key = jax.random.key(seed)
        ks = jax.random.split(key, 11)
        B, S, D = (4, 512, D_MODEL)
        scale = 1.0 / np.sqrt(D)
        return {'Q': jax.random.normal(ks[0], (B, S, D), jnp.float32), 'K': jax.random.normal(ks[1], (B, S, D), jnp.float32), 'V': jax.random.normal(ks[2], (B, S, D), jnp.float32), 'Wq': jax.random.normal(ks[3], (D, D), jnp.float32) * scale, 'bq': jnp.zeros((D,), jnp.float32), 'Wk': jax.random.normal(ks[4], (D, D), jnp.float32) * scale, 'bk': jnp.zeros((D,), jnp.float32), 'Wv': jax.random.normal(ks[5], (D, D), jnp.float32) * scale, 'bv': jnp.zeros((D,), jnp.float32), 'Wo': jax.random.normal(ks[6], (D, D), jnp.float32) * scale, 'bo': jnp.zeros((D,), jnp.float32)}
    _L0_xattn_all = _L0_xattn_setup()
    _L0_xattn_in = {k: v for k, v in _L0_xattn_all.items() if k in ('Wq', 'bq', 'Wk', 'bk', 'Wv', 'bv', 'Wo', 'bo')}
    del _L0_xattn_all

    def _L0_attn_setup():
        import jax, jax.numpy as jnp
        import numpy as np
        B, L, D_MODEL, H, HD, FD = (1, 256, 256, 16, 64, 64)
        EPS = 1e-12

        def _heads(t):
            b, l, _ = t.shape
            return t.reshape(b, l, H, HD).transpose(0, 2, 1, 3)

        def _feature_map(t, K):
            f = jnp.einsum('hdf,bhld->bhlf', K, t)
            feats = jnp.concatenate([jax.nn.softmax(f, axis=-1), jax.nn.softmax(-f, axis=-1)], axis=-1)
            return jnp.maximum(feats, EPS)
        key = jax.random.key(seed)
        ks = jax.random.split(key, 7)
        s = 1.0 / np.sqrt(D_MODEL)
        return {'x': jax.random.normal(ks[0], (B, L, D_MODEL), jnp.float32), 'Wq': jax.random.normal(ks[1], (D_MODEL, H * HD), jnp.float32) * s, 'Wk': jax.random.normal(ks[2], (D_MODEL, H * HD), jnp.float32) * s, 'Wv': jax.random.normal(ks[3], (D_MODEL, H * HD), jnp.float32) * s, 'Wo': jax.random.normal(ks[4], (H * HD, D_MODEL), jnp.float32) * s, 'Kq': jax.random.normal(ks[5], (H, HD, FD), jnp.float32) * (1.0 / np.sqrt(HD)), 'Kk': jax.random.normal(ks[6], (H, HD, FD), jnp.float32) * (1.0 / np.sqrt(HD))}
    _L0_attn_all = _L0_attn_setup()
    _L0_attn_in = {k: v for k, v in _L0_attn_all.items() if k in ('Wq', 'Wk', 'Wv', 'Wo', 'Kq', 'Kk')}
    del _L0_attn_all

    def _L0_ffn_setup():
        import jax, jax.numpy as jnp
        import numpy as np
        D_MODEL = 256
        NUM_SLOTS = 64
        TOP_K = 8
        B, T = (4, 1024)

        def _forward(x, slot_init, slot_scale, w1, b1, w2, b2, gru_wih, gru_whh, gru_bih, gru_bhh, wv, bv, wo, bo, tau):
            Bn, Tn, D = x.shape
            Sn = slot_init.shape[0]
            S = jnp.broadcast_to((slot_init * slot_scale)[None], (Bn, Sn, D)).astype(x.dtype)
            slot_mean = S.mean(axis=1, keepdims=True)
            ctx = jnp.concatenate([x, jnp.broadcast_to(slot_mean, x.shape)], axis=-1)
            h = jax.nn.gelu(ctx @ w1.T + b1, approximate=False)
            route_logits = (h @ w2.T + b2) / (jnp.abs(tau) + 0.1)
            topk_vals, topk_idx = jax.lax.top_k(route_logits, TOP_K)
            topk_w = jax.nn.softmax(topk_vals, axis=-1)
            alpha = jnp.sum(topk_w[..., None] * jax.nn.one_hot(topk_idx, Sn, dtype=x.dtype), axis=-2)
            slot_input = jnp.einsum('bts,btd->bsd', alpha, x)
            slot_wsum = alpha.sum(axis=1) + 1e-08
            gi = (slot_input / slot_wsum[..., None]).reshape(Bn * Sn, D)
            hs = S.reshape(Bn * Sn, D)
            gx = gi @ gru_wih.T + gru_bih
            gh = hs @ gru_whh.T + gru_bhh
            xr, xz, xn = jnp.split(gx, 3, axis=-1)
            hr, hz, hn = jnp.split(gh, 3, axis=-1)
            r = jax.nn.sigmoid(xr + hr)
            z = jax.nn.sigmoid(xz + hz)
            n = jnp.tanh(xn + r * hn)
            h_new = (1.0 - z) * n + z * hs
            S_new = h_new.reshape(Bn, Sn, D)
            slot_values = S_new @ wv.T + bv
            out = jnp.einsum('bts,bsd->btd', alpha, slot_values)
            return out @ wo.T + bo
        key = jax.random.key(seed)
        ks = jax.random.split(key, 16)
        D, S = (D_MODEL, NUM_SLOTS)
        H = D // 2
        sc = lambda fan_in: 1.0 / np.sqrt(fan_in)
        inp = {'x': jax.random.normal(ks[0], (B, T, D), dtype=jnp.float32), 'slot_init': jax.random.normal(ks[1], (S, D), dtype=jnp.float32) * 0.1, 'slot_scale': jnp.ones((S, 1), dtype=jnp.float32), 'w1': jax.random.normal(ks[2], (H, 2 * D), dtype=jnp.float32) * sc(2 * D), 'b1': jnp.zeros((H,), dtype=jnp.float32), 'w2': jax.random.normal(ks[3], (S, H), dtype=jnp.float32) * sc(H), 'b2': jnp.zeros((S,), dtype=jnp.float32), 'gru_wih': jax.random.normal(ks[4], (3 * D, D), dtype=jnp.float32) * sc(D), 'gru_whh': jax.random.normal(ks[5], (3 * D, D), dtype=jnp.float32) * sc(D), 'gru_bih': jnp.zeros((3 * D,), dtype=jnp.float32), 'gru_bhh': jnp.zeros((3 * D,), dtype=jnp.float32), 'wv': jax.random.normal(ks[6], (D, D), dtype=jnp.float32) * sc(D), 'bv': jnp.zeros((D,), dtype=jnp.float32), 'wo': jax.random.normal(ks[7], (D, D), dtype=jnp.float32) * sc(D), 'bo': jnp.zeros((D,), dtype=jnp.float32), 'tau': jnp.ones((1,), dtype=jnp.float32)}
        return inp
    _L0_ffn_all = _L0_ffn_setup()
    _L0_ffn_in = {k: v for k, v in _L0_ffn_all.items() if k in ('slot_init', 'slot_scale', 'w1', 'b1', 'w2', 'b2', 'gru_wih', 'gru_whh', 'gru_bih', 'gru_bhh', 'wv', 'bv', 'wo', 'bo', 'tau')}
    del _L0_ffn_all
    return {'x': x, 'ctx_1024': ctx_1024, 'L0_xattn_Wq': _L0_xattn_in['Wq'], 'L0_xattn_bq': _L0_xattn_in['bq'], 'L0_xattn_Wk': _L0_xattn_in['Wk'], 'L0_xattn_bk': _L0_xattn_in['bk'], 'L0_xattn_Wv': _L0_xattn_in['Wv'], 'L0_xattn_bv': _L0_xattn_in['bv'], 'L0_xattn_Wo': _L0_xattn_in['Wo'], 'L0_xattn_bo': _L0_xattn_in['bo'], 'L0_attn_Wq': _L0_attn_in['Wq'], 'L0_attn_Wk': _L0_attn_in['Wk'], 'L0_attn_Wv': _L0_attn_in['Wv'], 'L0_attn_Wo': _L0_attn_in['Wo'], 'L0_attn_Kq': _L0_attn_in['Kq'], 'L0_attn_Kk': _L0_attn_in['Kk'], 'L0_ffn_slot_init': _L0_ffn_in['slot_init'], 'L0_ffn_slot_scale': _L0_ffn_in['slot_scale'], 'L0_ffn_w1': _L0_ffn_in['w1'], 'L0_ffn_b1': _L0_ffn_in['b1'], 'L0_ffn_w2': _L0_ffn_in['w2'], 'L0_ffn_b2': _L0_ffn_in['b2'], 'L0_ffn_gru_wih': _L0_ffn_in['gru_wih'], 'L0_ffn_gru_whh': _L0_ffn_in['gru_whh'], 'L0_ffn_gru_bih': _L0_ffn_in['gru_bih'], 'L0_ffn_gru_bhh': _L0_ffn_in['gru_bhh'], 'L0_ffn_wv': _L0_ffn_in['wv'], 'L0_ffn_bv': _L0_ffn_in['bv'], 'L0_ffn_wo': _L0_ffn_in['wo'], 'L0_ffn_bo': _L0_ffn_in['bo'], 'L0_ffn_tau': _L0_ffn_in['tau']}

def reference(x, ctx_1024, L0_xattn_Wq, L0_xattn_bq, L0_xattn_Wk, L0_xattn_bk, L0_xattn_Wv, L0_xattn_bv, L0_xattn_Wo, L0_xattn_bo, L0_attn_Wq, L0_attn_Wk, L0_attn_Wv, L0_attn_Wo, L0_attn_Kq, L0_attn_Kk, L0_ffn_slot_init, L0_ffn_slot_scale, L0_ffn_w1, L0_ffn_b1, L0_ffn_w2, L0_ffn_b2, L0_ffn_gru_wih, L0_ffn_gru_whh, L0_ffn_gru_bih, L0_ffn_gru_bhh, L0_ffn_wv, L0_ffn_bv, L0_ffn_wo, L0_ffn_bo, L0_ffn_tau):
    import jax
    import jax.numpy as jnp

    def _L0_xattn_ref(Q, K, V, Wq, bq, Wk, bk, Wv, bv, Wo, bo):
        import jax, jax.numpy as jnp
        import numpy as np
        D_MODEL = 256
        NUM_HEADS = 16
        D_K = D_MODEL // NUM_HEADS
        B, S, D = Q.shape
        H, Dk = (NUM_HEADS, D_K)

        def proj(x, W, b):
            y = jnp.einsum('bsd,de->bse', x, W.T) + b
            return y.reshape(B, -1, H, Dk).transpose(0, 2, 1, 3)
        q = proj(Q, Wq, bq)
        k = proj(K, Wk, bk)
        v = proj(V, Wv, bv)
        scores = jnp.einsum('bhqd,bhkd->bhqk', q, k) / np.sqrt(Dk)
        attn = jax.nn.softmax(scores, axis=-1)
        out = jnp.einsum('bhqk,bhkd->bhqd', attn, v)
        out = out.transpose(0, 2, 1, 3).reshape(B, -1, D)
        return jnp.einsum('bsd,de->bse', out, Wo.T) + bo

    def _L0_attn_ref(x, Wq, Wk, Wv, Wo, Kq, Kk):
        import jax, jax.numpy as jnp
        import numpy as np
        B, L, D_MODEL, H, HD, FD = (1, 256, 256, 16, 64, 64)
        EPS = 1e-12

        def _heads(t):
            b, l, _ = t.shape
            return t.reshape(b, l, H, HD).transpose(0, 2, 1, 3)

        def _feature_map(t, K):
            f = jnp.einsum('hdf,bhld->bhlf', K, t)
            feats = jnp.concatenate([jax.nn.softmax(f, axis=-1), jax.nn.softmax(-f, axis=-1)], axis=-1)
            return jnp.maximum(feats, EPS)
        q = _heads(x @ Wq)
        k = _heads(x @ Wk)
        v = _heads(x @ Wv)
        qf = _feature_map(q, Kq)
        kf = _feature_map(k, Kk)
        kv = jnp.cumsum(kf[:, :, :, None, :] * v[..., None], axis=2)
        o = jnp.einsum('bhlf,bhldf->bhld', qf, kv)
        z = jnp.einsum('bhlf,bhlf->bhl', qf, jnp.cumsum(kf, axis=2)) + EPS
        o = o / z[..., None]
        y = o.transpose(0, 2, 1, 3).reshape(x.shape[0], x.shape[1], H * HD)
        return y @ Wo

    def _L0_ffn_ref(x, slot_init, slot_scale, w1, b1, w2, b2, gru_wih, gru_whh, gru_bih, gru_bhh, wv, bv, wo, bo, tau):
        import jax, jax.numpy as jnp
        import numpy as np
        D_MODEL = 256
        NUM_SLOTS = 64
        TOP_K = 8
        B, T = (4, 1024)

        def _forward(x, slot_init, slot_scale, w1, b1, w2, b2, gru_wih, gru_whh, gru_bih, gru_bhh, wv, bv, wo, bo, tau):
            Bn, Tn, D = x.shape
            Sn = slot_init.shape[0]
            S = jnp.broadcast_to((slot_init * slot_scale)[None], (Bn, Sn, D)).astype(x.dtype)
            slot_mean = S.mean(axis=1, keepdims=True)
            ctx = jnp.concatenate([x, jnp.broadcast_to(slot_mean, x.shape)], axis=-1)
            h = jax.nn.gelu(ctx @ w1.T + b1, approximate=False)
            route_logits = (h @ w2.T + b2) / (jnp.abs(tau) + 0.1)
            topk_vals, topk_idx = jax.lax.top_k(route_logits, TOP_K)
            topk_w = jax.nn.softmax(topk_vals, axis=-1)
            alpha = jnp.sum(topk_w[..., None] * jax.nn.one_hot(topk_idx, Sn, dtype=x.dtype), axis=-2)
            slot_input = jnp.einsum('bts,btd->bsd', alpha, x)
            slot_wsum = alpha.sum(axis=1) + 1e-08
            gi = (slot_input / slot_wsum[..., None]).reshape(Bn * Sn, D)
            hs = S.reshape(Bn * Sn, D)
            gx = gi @ gru_wih.T + gru_bih
            gh = hs @ gru_whh.T + gru_bhh
            xr, xz, xn = jnp.split(gx, 3, axis=-1)
            hr, hz, hn = jnp.split(gh, 3, axis=-1)
            r = jax.nn.sigmoid(xr + hr)
            z = jax.nn.sigmoid(xz + hz)
            n = jnp.tanh(xn + r * hn)
            h_new = (1.0 - z) * n + z * hs
            S_new = h_new.reshape(Bn, Sn, D)
            slot_values = S_new @ wv.T + bv
            out = jnp.einsum('bts,bsd->btd', alpha, slot_values)
            return out @ wo.T + bo
        return _forward(x, slot_init, slot_scale, w1, b1, w2, b2, gru_wih, gru_whh, gru_bih, gru_bhh, wv, bv, wo, bo, tau)
    x = x + _L0_xattn_ref(_layernorm(x, axis=-1), ctx_1024, ctx_1024, L0_xattn_Wq, L0_xattn_bq, L0_xattn_Wk, L0_xattn_bk, L0_xattn_Wv, L0_xattn_bv, L0_xattn_Wo, L0_xattn_bo)
    x = x + _L0_attn_ref(_layernorm(x, axis=-1), L0_attn_Wq, L0_attn_Wk, L0_attn_Wv, L0_attn_Wo, L0_attn_Kq, L0_attn_Kk)
    x = x + _L0_ffn_ref(_layernorm(x, axis=-1), L0_ffn_slot_init, L0_ffn_slot_scale, L0_ffn_w1, L0_ffn_b1, L0_ffn_w2, L0_ffn_b2, L0_ffn_gru_wih, L0_ffn_gru_whh, L0_ffn_gru_bih, L0_ffn_gru_bhh, L0_ffn_wv, L0_ffn_bv, L0_ffn_wo, L0_ffn_bo, L0_ffn_tau)
    return x

_drawn_inputs = setup_inputs


def setup_inputs(seed=0):
    import zlib

    import numpy as np

    out = dict(_drawn_inputs(seed))
    spreads = {'L0_xattn_bq': (0.0, 0.299),
     'L0_xattn_bk': (0.0, 0.8),
     'L0_xattn_bv': (0.0, 0.1),
     'L0_xattn_bo': (0.0, 0.1),
     'L0_ffn_slot_scale': (1.0, 0.6),
     'L0_ffn_b1': (0.0, 0.58),
     'L0_ffn_b2': (0.0, 0.491),
     'L0_ffn_gru_bih': (0.0, 0.287),
     'L0_ffn_gru_bhh': (0.0, 0.595),
     'L0_ffn_bv': (0.0, 0.1),
     'L0_ffn_bo': (0.0, 0.1)}
    factors = {'L0_ffn_slot_init': 3.95, 'L0_ffn_gru_whh': 8.0}
    for name, (base, spread) in spreads.items():
        noise = np.random.default_rng([zlib.crc32(name.encode()), seed]).standard_normal(out[name].shape)
        drawn = base * np.exp(spread * noise) if base else spread * noise
        out[name] = jnp.asarray(drawn.astype(out[name].dtype))
    for name, factor in factors.items():
        out[name] = (out[name] * factor).astype(out[name].dtype)
    return out
```

```python
from contextlib import ExitStack

import concourse.bass as bass
from concourse import mybir

F32 = mybir.dt.float32
F16 = mybir.dt.float16
BF16 = mybir.dt.bfloat16
ALU = mybir.AluOpType
ACT = mybir.ActivationFunctionType
AX = mybir.AxisListType

P = 128
D = 256
KD = D // P
BT = 4
SQ = 32
SK = 256
H = 16
DK = D // H
HD = 64
E2 = H * HD
NQ = 4
SLOTS = 64
NEG = -3.0e38
LN_EPS = 1e-5
FEAT_EPS = 1e-12
WSUM_EPS = 1e-8

PE_STEPS = {
    "P1": ["xT"], "P2": ["q"],
    "KV": ["kT", "v"], "A": ["A"], "ST": ["ST"], "PV": ["PV"], "C1": ["X"], "C2": ["aT"], "C3": ["o"],
    "L2b": ["xT"], "F": ["f"], "V": ["v"], "T": ["T"], "AT": ["AT"], "AV": ["AV"], "Y": ["Y"], "W": ["W"],
    "3b": ["xT"], "3c": ["h"], "3d": ["lg"], "3e": ["si"], "3f": ["aT"], "3g": ["rz"], "3h": ["n"],
    "3i": ["as"], "3j": ["y"],
}
ACT_STEPS = {
    "P1": ["xhi"], "P2": ["qf0", "qf1", "qhi"],
    "KV": ["kh0", "kh1", "vh"], "ST": ["pf", "ph"], "C1": ["ae"], "C2": ["ahi"],
    "L2b": ["xhi"], "F": ["exp"], "V": ["v"], "T": ["feat"], "Y": ["yT"],
    "3b": ["xhi"], "3c": ["gelu"], "3d": ["e"], "3e": ["si"], "3f": ["aT"], "3g": ["tanh"], "3h": ["n"],
    "3i": ["as"],
}
DVE_STEPS = {
    "P0": ["stats", "aggr", "eps", "xn"], "P1": ["xlo"], "P2": ["qnat", "qlo"], "P3": ["bdhi", "bdlo", "slast"],
    "KV": ["kl0", "kl1", "vl"], "A": ["max"], "PV": ["om", "zx", "mx"],
    "C1": ["d", "ta", "te", "za", "zt", "rz", "ea", "at0", "at"], "C2": ["alo"], "C3": ["x1"],
    "L2a": ["stats", "aggr", "eps", "xn"], "L2b": ["xlo"],
    "F": ["max", "min", "subp", "subm", "sum", "rs", "clamp"], "AT": ["mask"],
    "AV": ["z", "rz", "y"], "W": ["x2"],
    "3a": ["stats", "aggr", "eps", "xn"], "3b": ["xlo"],
    "3d": ["lb", "lg", "top", "repl", "sel", "nmax", "ea", "rs", "al", "abd"],
    "3f": ["ws", "rw"], "3g": ["rz"], "3h": ["u", "v", "q", "S"], "3j": ["out"],
}
POOL_STEPS = {
    "P0": ["rstd"], "P3": ["xres", "prod"],
    "KV": ["chi", "clo"], "ST": ["plo"], "C1": ["wv"],
    "L2a": ["rstd"], "F": ["norm"],
    "3a": ["x2b", "rstd"], "3h": ["w", "d"],
}
STAGE_PLANS = {
    "P": [("P0",), ("P1",), ("P2",), ("P3",)],
    "S1": [("KV", 0), ("A", 0), ("KV", 1), ("ST", 0), ("A", 1), ("KV", 2), ("ST", 1), ("PV", 0), ("A", 2),
           ("KV", 3), ("ST", 2), ("PV", 1), ("A", 3), ("ST", 3), ("PV", 2), ("PV", 3), ("C1",), ("C2",), ("C3",)],
    "S2": [("L2a",), ("L2b",), ("F", 0), ("F", 1), ("V", 0), ("F", 2), ("T", 0, 0), ("T", 1, 0), ("F", 3),
           ("AT", 0), ("T", 0, 1), ("T", 1, 1), ("V", 1), ("AV", 0), ("AT", 1), ("T", 2, 0), ("T", 3, 0),
           ("AV", 1), ("AT", 2), ("T", 2, 1), ("T", 3, 1), ("AV", 2), ("AT", 3), ("Y", 0), ("AV", 3), ("Y", 1),
           ("W",)],
    "S3": [("3a",), ("3b",), ("3c",), ("3d",), ("3e",), ("3f",), ("3g", 0), ("3h", 0), ("3g", 1), ("3h", 1),
           ("3i",), ("3j",)],
}


def interleave(main, side, at):
    out = []
    for n, item in enumerate(main):
        out.append(item)
        out += [s for s, a in zip(side, at) if a == n]
    return out


S1_S3 = interleave([("S1", *i) for i in STAGE_PLANS["S1"]], [("S3", *i) for i in STAGE_PLANS["S3"]],
                   [0, 1, 2, 3, 4, 6, 7, 9, 10, 12, 14, 15])
S2_P = interleave([("S2", *i) for i in STAGE_PLANS["S2"]], [("P", *i) for i in STAGE_PLANS["P"]],
                  [2, 5, 8, 12])


class Tile:

    def __init__(self, reg, off):
        self.reg, self.off = reg, off

    def times(self, n, plus=0):
        c = self.off * n + plus
        return c if self.reg is None else self.reg * n + c

    def shifted(self, by):
        return Tile(self.reg, self.off + by)

    @property
    def first(self):
        return self.reg is None and self.off == 0


class Progress:

    def __init__(self, sem, plan, steps):
        self.sem = sem
        self.names = [(name, *item[1:]) for item in plan for name in steps.get(item[0], [])]
        self.index = {name: n + 1 for n, name in enumerate(self.names)}
        assert len(self.index) == len(self.names), self.names
        self.at = 0

    def step(self, *name):
        assert self.names[self.at % len(self.names)] == name, (self.names[self.at % len(self.names)], name)
        self.at += 1
        return self.sem, 1

    def after(self, tile, *name):
        return self.sem, tile.times(len(self.names), self.index[name])


def bass_perceiver_layer(nc, a, tiles):
    ctx = ExitStack()
    with ctx:
        def sb(name, shape, dt=F32):
            return ctx.enter_context(nc.sbuf_tensor(name, shape, dt))

        def pb(name, cols):
            return ctx.enter_context(nc.psum_tensor(name, [P, cols], F32))

        def sem(name):
            return ctx.enter_context(nc.semaphore(name))

        def split(name, shape):
            return sb(name + "_hi", shape, F16), sb(name + "_lo", shape, F16)

        WQ, WK, WV, WO = (split(n, [P, KD, D]) for n in ("WQ", "WK", "WV", "WO"))
        FQ, FK, WV2 = (split(n, [P, KD, E2]) for n in ("FQ", "FK", "WV2"))
        W1 = split("W1", [P, KD, P])
        wo2 = sb("wo2", [P, E2 // P, D])
        w2 = sb("w2", [P, SLOTS])
        wih = sb("wih", [P, KD, 3 * D])
        gvo = sb("gvo", [P, KD, D])
        ident = sb("ident", [P, P])
        identb = sb("identb", [P, P], BF16)
        same_q = sb("same_q", [P, SQ])
        collapse = sb("collapse", [P, BT, P])
        mask8 = sb("mask8", [P, 8, SQ], F16)
        mask_o = sb("mask_o", [P, 4, DK])
        mask_c = sb("mask_c", [P, P])
        half = sb("half", [P, 1])
        bq4c = sb("bq4c", [P, KD])
        bkc = sb("bkc", [P, KD])
        bq4 = sb("bq4", [P, D])
        bk_row = sb("bk_row", [P, D])
        b_o1 = sb("b_o1", [P, D])
        b_o3 = sb("b_o3", [P, D])
        b2r = sb("b2r", [P, SLOTS])
        c_h = sb("c_h", [P, 1])
        tinv = sb("tinv", [P, 1])
        hs = sb("hs", [P, D])
        c_rz = sb("c_rz", [P, 2 * D])
        hn_half = sb("hn_half", [P, D])
        bihn = sb("bihn", [P, D])

        x_in = sb("x_in", [P, D])
        kv_last = sb("kv_last", [P, 2 * D])
        ctx_in = sb("ctx_in", [P, BT, KD, SK])
        st6 = sb("st6", [P, 3, 6])
        mv = sb("mv", [P, 3, 2])
        vareps = sb("vareps", [P, 3])
        rstd = sb("rstd", [P, 3])
        xn1 = sb("xn1", [P, D])
        x1T = split("x1T", [P, KD, P])
        qf = sb("qf", [P, 2, P])
        qs = split("qs", [P, 2, P])
        qnat = sb("qnat", [P, D])
        prod = sb("prod", [P, D])
        s_last = sb("s_last", [P, H])
        xres = sb("xres", [P, D])
        BD = split("BD", [P, 2, BT, 8, SQ])
        cs = split("cs", [P, 2, KD, SK])
        ks = split("ks", [P, 2, 2, SK])
        vs = split("vs", [P, BT, 2, NQ, DK * 4 + 1])
        nmax = sb("nmax", [P, BT, NQ], BF16)
        pf = sb("pf", [P, 2, 2, 512])
        ps = split("ps", [P, 2, 2, 512])
        om = sb("om", [P, BT, D + 2 * H])
        lk = sb("lk", [P, 8, H])
        lk2 = sb("lk2", [P, H])
        attn = sb("attn", [P, D])
        wv_l = sb("wv_l", [P, D])
        attT = split("attT", [P, KD, P])
        x1 = sb("x1", [P, D])
        xn2 = sb("xn2", [P, D])
        x2T = split("x2T", [P, KD, P])
        arg = sb("arg", [P, 4, 8, 2, HD])
        fmx = sb("fmx", [P, 4, 2, 8])
        fsum = sb("fsum", [P, 4, 2, 8, 2])
        featT = sb("featT", [P, 4, 2, 4, P])
        v1 = sb("v1", [P, H * (HD + 1) + 31])
        at_m = sb("at_m", [P, 2, 4, P])
        zr = sb("zr", [P, 4, 2, 4])
        y = sb("y", [P, E2])
        yT = sb("yT", [P, 8, P])
        x2 = sb("x2", [P, D])
        x2b = sb("x2b", [P, D])
        xn3 = sb("xn3", [P, D])
        x3T = split("x3T", [P, KD, P])
        hT = sb("hT", [P, P])
        lg = sb("lg", [P, 6, SLOTS])
        sc3 = sb("sc3", [P, 16])
        abd = sb("abd", [P, BT, SLOTS])
        siT = sb("siT", [P, KD, BT * SLOTS])
        aT = sb("aT", [P, 2, P])
        rw = sb("rw", [P, 2, 2])
        rz = sb("rz", [P, 2, 2 * D])
        gu = sb("gu", [P, 6, D])
        s_new = sb("s_new", [P, 2, D])
        asT = sb("asT", [P, KD, P])
        y_out = sb("y_out", [P, D])

        b_k = pb("b_k", 512)
        b_v = pb("b_v", 512)
        b_a = pb("b_a", 1024)
        b_s = pb("b_s", 1024)
        b_o = pb("b_o", 512)
        b_x = pb("b_x", 512)

        scratch = nc.dram_tensor("kv_last_scratch", (P, 2 * D), F32, kind="Internal").ap()

        w_kv32 = pf[:].rearrange("p a b c -> p (a b c)")
        w2q32 = arg[:].rearrange("p a b c d -> p (a b c d)")
        w2k32 = featT[:].rearrange("p a b c d -> p (a b c d)")
        kq32 = om[:].rearrange("p a b -> p (a b)")[:, 0:1024]
        kk32 = y[:]
        wv232 = ctx_in[:].rearrange("p a b c -> p (a b c)")
        w132 = yT[:].rearrange("p a b -> p (a b)")[:, 0:4 * P]
        whh32 = gu[:].rearrange("p a b -> p (a b)").rearrange("p (k n) -> p k n", k=KD)
        wv3 = rz[:, 0].rearrange("p (k n) -> p k n", k=KD)
        wo3 = rz[:, 1].rearrange("p (k n) -> p k n", k=KD)
        ctl = siT[:].rearrange("p a b -> p (a b)")[:, 0:KD * P]
        hsT = at_m[:].rearrange("p a b c -> p (a b c)")[:, 0:KD * P]
        small = sb("small", [P, 16])
        rows = [prod, wv_l, attn, xn2]
        bih_r = at_m[:].rearrange("p a b c -> p (a b c)")[:, 512:1024]
        bhh_r = yT[:].rearrange("p a b -> p (a b)")[:, 512:1024]
        kvl_sb = s_new[:].rearrange("p a b -> p (a b)")

        w_in = sem("weights_in")
        x_ld = sem("x_loaded")
        kv_ld = sem("kv_last_loaded")
        ctx_ld = [sem(f"ctx_loaded_{b}") for b in range(BT)]
        out_st = sem("out_stored")
        scr_st = sem("scratch_stored")
        prep = {e: sem(f"prep_{e}") for e in ("pe", "act", "dve", "pool")}

        passed = {e: sem(f"passed_waits_{e}") for e in ("pool", "dve")}

        def progress(engine, steps):
            return {s: Progress(sem(f"{engine}_{s}"), plan, steps) for s, plan in STAGE_PLANS.items()}

        pe_at, act_at = progress("pe", PE_STEPS), progress("act", ACT_STEPS)
        dve_at, pool_at = progress("dve", DVE_STEPS), progress("pool", POOL_STEPS)

        loads = [
            (w_kv32[:, 0:512].rearrange("p (k n) -> p k n", k=KD), a["xWk"]),
            (w_kv32[:, 512:1024].rearrange("p (k n) -> p k n", k=KD), a["xWv"]),
            (w_kv32[:, 1024:1536].rearrange("p (k n) -> p k n", k=KD), a["xWq"]),
            (w_kv32[:, 1536:2048].rearrange("p (k n) -> p k n", k=KD), a["xWo"]),
            (ctl.rearrange("p (k n) -> p k n", k=KD), a["ctx_last"]),
            (bk_row[:], a["xbk"].partition_broadcast(P)),
            (w2q32[0:HD].rearrange("p (h n) -> p h n", h=H), a["aWq"]),
            (w2k32[0:HD].rearrange("p (h n) -> p h n", h=H), a["aWk"]),
            (kq32[0:HD].rearrange("p (h n) -> p h n", h=H), a["aKq"]),
            (kk32[0:HD].rearrange("p (h n) -> p h n", h=H), a["aKk"]),
            (wv232.rearrange("p (k n) -> p k n", k=KD), a["aWv"]),
            (wo2[:], a["aWo"]),
            (w132.rearrange("p (k n) -> p k n", k=4), a["fw1"]),
            (w2[:], a["fw2"]),
            (wih[:], a["fwih"]),
            (whh32, a["fwhh"]),
            (wv3, a["fWv"]),
            (wo3, a["fWo"]),
            (hs[0:SLOTS], a["slot_init"]),
            (hs[SLOTS:P], a["slot_init"]),
            (small[:, 0:2], a["xbv"]),
            (small[:, 2:4], a["fbv"]),
            (small[:, 6:7], a["tau"].partition_broadcast(P)),
            (small[0:SLOTS, 7:8], a["slot_scale"]),
            (small[SLOTS:P, 7:8], a["slot_scale"]),
            (small[:, 8:10], a["xbq_col"]),
            (bkc[:], a["xbk_col"]),
            (small[:, 10:11], a["fb1"]),
            (rows[0][:], a["xbq"].partition_broadcast(P)),
            (rows[1][:], a["xbo"].partition_broadcast(P)),
            (rows[2][:], a["fbo"].partition_broadcast(P)),
            (rows[3][:], a["fbhh"][2 * D:3 * D].partition_broadcast(P)),
            (bih_r, a["fbih"][0:2 * D].partition_broadcast(P)),
            (bhh_r, a["fbhh"][0:2 * D].partition_broadcast(P)),
            (bihn[:], a["fbih"][2 * D:3 * D].partition_broadcast(P)),
            (b2r[:], a["fb2"].partition_broadcast(P)),
        ]
        ALL_LOADED = 16 * len(loads)
        POOL_PREP = 15
        PE_PREP = 5
        ACT_PREP = 11

        block = ctx.enter_context(nc.Block())

        def turns(run, eng, before, behind):
            before()
            for item in STAGE_PLANS["P"]:
                run(("P", *item), Tile(None, -1))
            for n in range(2):
                for item in (S1_S3 if n else [i for i in S1_S3 if i[0] == "S1"]) + S2_P:
                    run(item, Tile(None, n))
            with eng.Fori(2, tiles - 1) as reg:
                for item in S1_S3 + S2_P:
                    run(item, Tile(reg, 0))
            last = Tile(None, tiles - 1)
            for item in S1_S3 + [i for i in S2_P if i[0] == "S2"]:
                run(item, last)
            for item in STAGE_PLANS["S3"]:
                run(("S3", *item), Tile(None, tiles))
            behind()

        def tile_of(stage, turn):
            return turn.shifted({"P": 1, "S3": -1}.get(stage, 0))

        @block.sync
        def _(sp):
            for dst, src in loads:
                sp.dma_start(dst, src).then_inc(w_in, 16)
            sp.wait_ge(prep["dve"], KVL_DONE)
            sp.dma_start(scratch, kvl_sb).then_inc(scr_st, 16)
            sp.wait_ge(scr_st, 16)

            def load_x(t):
                if not t.first:
                    sp.wait_ge(*dve_at["P"].after(t.shifted(-1), "xn"))
                    sp.wait_ge(*pool_at["P"].after(t.shifted(-1), "xres"))
                sp.dma_start(x_in[:], a["x"][t.times(1)]).then_inc(x_ld, 16)

            def load_kv(t):
                if not t.first:
                    sp.wait_ge(*pool_at["S1"].after(t.shifted(-1), "wv"))
                for b in range(BT):
                    sp.dma_start(kv_last[SQ * b:SQ * (b + 1), :],
                                 scratch[t.times(BT, b)].partition_broadcast(SQ)).then_inc(kv_ld, 16)

            def load_ctx(t, b):
                if t.first:
                    if b == 0:
                        sp.wait_ge(prep["act"], ACT_PREP)
                        sp.wait_ge(prep["dve"], DVE_PREP)
                else:
                    sp.wait_ge(*pool_at["S1"].after(t.shifted(-1), "clo", b))
                sp.dma_start(ctx_in[:, b, :, :], a["ctx"][t.times(BT, b)]).then_inc(ctx_ld[b], 16)

            first = Tile(None, 0)
            load_x(first)
            load_kv(first)
            for b in range(BT):
                load_ctx(first, b)

            def turn(t):
                nxt = t.shifted(1)
                load_x(nxt)
                for b in range(BT):
                    load_ctx(nxt, b)
                load_kv(nxt)
                if not t.first:
                    store(t.shifted(-1))

            def store(t):
                sp.wait_ge(*dve_at["S3"].after(t, "out"))
                sp.dma_start(a["out"][t.times(1)], y_out[:]).then_inc(out_st, 16)

            turn(first)
            turn(Tile(None, 1))
            with sp.Fori(2, tiles - 1) as reg:
                turn(Tile(reg, 0))
            store(Tile(None, tiles - 2))
            store(Tile(None, tiles - 1))
            sp.wait_ge(out_st, 16 * tiles)

        @block.gpsimd
        def _(pool):
            g = nc.gpsimd

            def before():
                n = [0]

                def link(ins):
                    n[0] += 1
                    ins.then_inc(prep["pool"], 1)
                    pool.wait_ge(prep["pool"], n[0])

                link(g.memset(ident[:], 0.0))
                link(g.affine_select(out=ident[:], in_=ident[:], compare_op=ALU.not_equal, fill=1.0, base=0,
                                     pattern=[[-1, P]], channel_multiplier=1))
                link(g.tensor_copy(identb[:], ident[:]))
                link(g.memset(mask8[:], 1.0))
                link(g.affine_select(out=mask8[:], in_=mask8[:], compare_op=ALU.is_ge, fill=0.0, base=0,
                                     pattern=[[-DK, 8], [0, SQ]], channel_multiplier=1))
                link(g.affine_select(out=mask8[:], in_=mask8[:], compare_op=ALU.is_ge, fill=0.0, base=DK - 1,
                                     pattern=[[DK, 8], [0, SQ]], channel_multiplier=-1))
                link(g.memset(mask_o[:], 1.0))
                link(g.affine_select(out=mask_o[:], in_=mask_o[:], compare_op=ALU.is_ge, fill=0.0, base=0,
                                     pattern=[[-SQ, 4], [0, DK]], channel_multiplier=1))
                link(g.affine_select(out=mask_o[:], in_=mask_o[:], compare_op=ALU.is_ge, fill=0.0, base=SQ - 1,
                                     pattern=[[SQ, 4], [0, DK]], channel_multiplier=-1))
                mc = mask_c[:].rearrange("p (c r) -> p c r", c=4)
                link(g.memset(mask_c[:], 1.0))
                link(g.affine_select(out=mc, in_=mc, compare_op=ALU.is_ge, fill=0.0, base=0,
                                     pattern=[[-SQ, 4], [0, SQ]], channel_multiplier=1))
                link(g.affine_select(out=mc, in_=mc, compare_op=ALU.is_ge, fill=0.0, base=0,
                                     pattern=[[SQ, 4], [1, SQ]], channel_multiplier=-1))
                link(g.memset(collapse[:], 0.0))
                link(g.memset(half[:], -0.5))
                link(g.memset(v1[:], 1.0))
                assert n[0] == POOL_PREP

            def apart(*waits):
                for sm, val in waits:
                    pool.wait_ge(sm, val)
                pool.sem_inc(passed["pool"], 1)

            def power(stage, t, name, n):
                pool.wait_ge(*dve_at[stage].after(t, "eps"))
                g.tensor_tensor(rstd[:, n:n + 1], vareps[:, n:n + 1], half[:], ALU.pow)\
                 .then_inc(*pool_at[stage].step(name))

            def run(item, turn):
                stage, kind, *arg_ = item
                t = tile_of(stage, turn)
                prev = t.shifted(-1)
                if kind == "P0":
                    power("P", t, "rstd", 0)
                elif kind == "L2a":
                    power("S2", t, "rstd", 1)
                elif kind == "P3":
                    pool.wait_ge(x_ld, t.times(16, 16))
                    if not t.first:
                        pool.wait_ge(*dve_at["S1"].after(prev, "x1"))
                    g.tensor_tensor(xres[:], x_in[:], b_o1[:], ALU.add).then_inc(*pool_at["P"].step("xres"))
                    pool.wait_ge(kv_ld, t.times(64, 64))
                    pool.wait_ge(*dve_at["P"].after(t, "qnat"))
                    g.tensor_tensor(prod[:], qnat[:], kv_last[:, 0:D], ALU.mult)\
                     .then_inc(*pool_at["P"].step("prod"))
                elif kind == "KV":
                    b, = arg_
                    waits = [(ctx_ld[b], t.times(16, 16))]
                    if b >= 2:
                        waits.append(pe_at["S1"].after(t, "v", b - 2))
                    elif not t.first:
                        waits.append(pe_at["S1"].after(prev, "v", b + 2))
                    apart(*waits)
                    g.tensor_copy(cs[0][:, b % 2], ctx_in[:, b]).then_inc(*pool_at["S1"].step("chi", b))
                    pool.wait_ge(*pool_at["S1"].after(t, "chi", b))
                    g.tensor_tensor(cs[1][:, b % 2], ctx_in[:, b], cs[0][:, b % 2], ALU.subtract)\
                     .then_inc(*pool_at["S1"].step("clo", b))
                elif kind == "ST":
                    b, = arg_
                    pool.wait_ge(*act_at["S1"].after(t, "ph", b))
                    if b >= 2:
                        pool.wait_ge(*pe_at["S1"].after(t, "PV", b - 2))
                    elif not t.first:
                        pool.wait_ge(*pe_at["S1"].after(prev, "PV", b + 2))
                    g.tensor_tensor(ps[1][:, b % 2], pf[:, b % 2], ps[0][:, b % 2], ALU.subtract)\
                     .then_inc(*pool_at["S1"].step("plo", b))
                elif kind == "C1":
                    pool.wait_ge(*dve_at["S1"].after(t, "ea"))
                    g.tensor_tensor(wv_l[:].rearrange("p (h d) -> p h d", h=H),
                                    kv_last[:, D:2 * D].rearrange("p (h d) -> p h d", h=H),
                                    lk2[:].unsqueeze(2).to_broadcast([P, H, DK]), ALU.mult)\
                     .then_inc(*pool_at["S1"].step("wv"))
                elif kind == "F":
                    c, = arg_
                    pool.wait_ge(*act_at["S2"].after(t, "exp", c))
                    pool.wait_ge(*dve_at["S2"].after(t, "rs", c))
                    f = arg[:, c].rearrange("p h s f -> p (h s) f")
                    g.tensor_tensor(f, f, fsum[:, c, 1].rearrange("p h s -> p (h s)").unsqueeze(2)
                                    .to_broadcast([P, 16, HD]), ALU.mult).then_inc(*pool_at["S2"].step("norm", c))
                elif kind == "3a":
                    pool.wait_ge(*dve_at["S2"].after(t, "x2"))
                    if not t.first:
                        pool.wait_ge(*dve_at["S3"].after(prev, "out"))
                    g.tensor_tensor(x2b[:], x2[:], b_o3[:], ALU.add).then_inc(*pool_at["S3"].step("x2b"))
                    power("S3", t, "rstd", 2)
                elif kind == "3h":
                    s, = arg_
                    pool.wait_ge(*dve_at["S3"].after(t, "v", s))
                    g.tensor_tensor(gu[:, 2], gu[:, 0], gu[:, 1], ALU.add).then_inc(*pool_at["S3"].step("w", s))
                    pool.wait_ge(*act_at["S3"].after(t, "n", s))
                    g.tensor_tensor(gu[:, 4], hs[:], gu[:, 3], ALU.subtract).then_inc(*pool_at["S3"].step("d", s))

            pool.wait_ge(w_in, ALL_LOADED) if False else None
            turns(run, pool, before, lambda: None)

        @block.scalar
        def _(act):
            s = nc.scalar

            def before():
                n = [0]

                def done(ins):
                    n[0] += 1
                    ins.then_inc(prep["act"], 1)

                act.wait_ge(w_in, ALL_LOADED)
                kv4 = w_kv32.rearrange("p (w k n) -> p w k n", w=4, k=KD)
                for i, w in enumerate((WK, WV, WQ, WO)):
                    done(s.copy(w[0][:], kv4[:, i]))
                done(s.copy(WV2[0][:], wv232.rearrange("p (k n) -> p k n", k=KD)))
                done(s.copy(W1[0][:], w132.rearrange("p (k n) -> p k n", k=4)[:, 0:KD]))
                done(s.mul(bq4c[:], small[:, 8:10], 0.25))
                done(s.mul(bq4[:], rows[0][:], 0.25))
                act.wait_ge(prep["pe"], 1)
                for w, b0, b1 in ((FQ, b_k, b_v),):
                    done(s.copy(w[0][:, 0, 0:512], b0[:]))
                    done(s.copy(w[0][:, 0, 512:1024], b1[:]))
                done(s.copy(FQ[0][:, 1, :], b_a[:]))
                assert n[0] == ACT_PREP, n[0]

            def run(item, turn):
                stage, kind, *arg_ = item
                t = tile_of(stage, turn)
                prev = t.shifted(-1)
                if kind in ("P1", "L2b", "3b"):
                    xT, bank = {"P1": (x1T, b_x), "L2b": (x2T, b_a), "3b": (x3T, b_x)}[kind]
                    act.wait_ge(*pe_at[stage].after(t, "xT"))
                    s.copy(xT[0][:].rearrange("p k n -> p (k n)"), bank[:, 0:D])\
                     .then_inc(*act_at[stage].step("xhi"))
                elif kind == "P2":
                    act.wait_ge(*pe_at["P"].after(t, "q"))
                    if not t.first:
                        act.wait_ge(*dve_at["P"].after(prev, "qlo"))
                    for n in range(2):
                        s.activation(qf[:, n], b_x[:, n * P:(n + 1) * P], ACT.Identity, bias=bq4c[:, n:n + 1],
                                     scale=0.25).then_inc(*act_at["P"].step(f"qf{n}"))
                    act.wait_ge(*act_at["P"].after(t, "qf1"))
                    if not t.first:
                        act.wait_ge(*dve_at["P"].after(prev, "bdhi"))
                    s.copy(qs[0][:], qf[:]).then_inc(*act_at["P"].step("qhi"))
                elif kind == "KV":
                    b, = arg_
                    act.wait_ge(*pe_at["S1"].after(t, "kT", b))
                    if b >= 2:
                        act.wait_ge(*pe_at["S1"].after(t, "ST", b - 2))
                    elif not t.first:
                        act.wait_ge(*pe_at["S1"].after(prev, "ST", b + 2))
                    for n in range(2):
                        s.activation(ks[0][:, b % 2, n], b_k[:, n * SK:(n + 1) * SK], ACT.Identity,
                                     bias=bkc[:, n:n + 1]).then_inc(*act_at["S1"].step(f"kh{n}", b))
                    act.wait_ge(*pe_at["S1"].after(t, "v", b))
                    if not t.first:
                        act.wait_ge(*pe_at["S1"].after(prev, "PV", b))
                    s.copy(vs[0][:, b, :, :, 0:4 * DK].rearrange("p k j d -> p (k j) d"),
                           b_v[:].rearrange("p (k d) -> p k d", d=4 * DK))\
                     .then_inc(*act_at["S1"].step("vh", b))
                elif kind == "ST":
                    b, = arg_
                    act.wait_ge(*pe_at["S1"].after(t, "ST", b))
                    if b >= 2:
                        act.wait_ge(*pool_at["S1"].after(t, "plo", b - 2))
                        act.wait_ge(*pe_at["S1"].after(t, "PV", b - 2))
                    elif not t.first:
                        act.wait_ge(*pool_at["S1"].after(prev, "plo", b + 2))
                        act.wait_ge(*pe_at["S1"].after(prev, "PV", b + 2))
                    s.activation(ps[0][:, b % 2].rearrange("p k n -> p (k n)"), b_s[:], ACT.Exp)\
                     .then_inc(*act_at["S1"].step("pf", b))
                    s.activation(pf[:, b % 2].rearrange("p k n -> p (k n)"), b_s[:], ACT.Exp)\
                     .then_inc(*act_at["S1"].step("ph", b))
                elif kind == "C1":
                    act.wait_ge(*dve_at["S1"].after(t, "te"))
                    s.activation(lk[:, 3:5, :].rearrange("p a b -> p (a b)"),
                                 lk[:, 1:3, :].rearrange("p a b -> p (a b)"), ACT.Exp)\
                     .then_inc(*act_at["S1"].step("ae"))
                elif kind == "C2":
                    act.wait_ge(*pe_at["S1"].after(t, "aT"))
                    s.copy(attT[0][:].rearrange("p k n -> p (k n)"), b_k[:, 0:D])\
                     .then_inc(*act_at["S1"].step("ahi"))
                elif kind == "F":
                    c, = arg_
                    act.wait_ge(*dve_at["S2"].after(t, "subm", c))
                    f = arg[:, c].rearrange("p h s f -> p (h s f)")
                    s.activation(f, f, ACT.Exp).then_inc(*act_at["S2"].step("exp", c))
                elif kind == "V":
                    n, = arg_
                    act.wait_ge(*pe_at["S2"].after(t, "v", n))
                    if not t.first:
                        act.wait_ge(*pe_at["S2"].after(prev, "AV", 2 * n + 1))
                        if n == 0:
                            act.wait_ge(*pe_at["S2"].after(prev, "AV", 2))
                    w = (HD + 1) * 8
                    s.copy(v1[:, n * w:(n + 1) * w].rearrange("p (h d) -> p h d", h=8)[:, :, 0:HD],
                           (b_k, b_v)[n][:].rearrange("p (h d) -> p h d", h=8))\
                     .then_inc(*act_at["S2"].step("v", n))
                elif kind == "T":
                    c, i = arg_
                    act.wait_ge(*pe_at["S2"].after(t, "T", c, i))
                    if not t.first:
                        act.wait_ge(*pe_at["S2"].after(prev, "AT", c // 2 * 2 + i))
                    s.copy(featT[:, c, i].rearrange("p h n -> p (h n)"), b_a[:, (c % 2) * 512:(c % 2) * 512 + 512])\
                     .then_inc(*act_at["S2"].step("feat", c, i))
                elif kind == "Y":
                    n, = arg_
                    act.wait_ge(*pe_at["S2"].after(t, "Y", n))
                    if not t.first and n == 0:
                        act.wait_ge(*pe_at["S2"].after(prev, "W"))
                    s.copy(yT[:, 4 * n:4 * n + 4].rearrange("p h n -> p (h n)"), b_a[:, n * 512:(n + 1) * 512])\
                     .then_inc(*act_at["S2"].step("yT", n))
                elif kind == "3c":
                    act.wait_ge(*pe_at["S3"].after(t, "h"))
                    s.activation(hT[:], b_x[:, 0:P], ACT.Gelu, bias=c_h[:, 0:1])\
                     .then_inc(*act_at["S3"].step("gelu"))
                elif kind == "3d":
                    act.wait_ge(*dve_at["S3"].after(t, "nmax"))
                    s.activation(lg[:, 4], lg[:, 1], ACT.Exp, bias=sc3[:, 8:9]).then_inc(*act_at["S3"].step("e"))
                elif kind == "3e":
                    act.wait_ge(*pe_at["S3"].after(t, "si"))
                    s.copy(siT[:].rearrange("p k n -> p (k n)"), b_x[:]).then_inc(*act_at["S3"].step("si"))
                elif kind == "3f":
                    act.wait_ge(*pe_at["S3"].after(t, "aT"))
                    s.copy(aT[:].rearrange("p k n -> p (k n)"), b_x[:, 0:2 * P]).then_inc(*act_at["S3"].step("aT"))
                elif kind == "3g":
                    n, = arg_
                    act.wait_ge(*dve_at["S3"].after(t, "rz", n))
                    s.activation(rz[:, n], rz[:, n], ACT.Tanh, scale=0.5).then_inc(*act_at["S3"].step("tanh", n))
                elif kind == "3h":
                    n, = arg_
                    act.wait_ge(*pool_at["S3"].after(t, "w", n))
                    s.activation(gu[:, 3], gu[:, 2], ACT.Tanh).then_inc(*act_at["S3"].step("n", n))
                elif kind == "3i":
                    act.wait_ge(*pe_at["S3"].after(t, "as"))
                    s.copy(asT[:].rearrange("p k n -> p (k n)"), b_x[:, 0:D]).then_inc(*act_at["S3"].step("as"))

            turns(run, act, before, lambda: None)

        @block.vector
        def _(dve):
            v = nc.vector

            def before():
                n = [0]

                def link(ins):
                    n[0] += 1
                    ins.then_inc(prep["dve"], 1)
                    dve.wait_ge(prep["dve"], n[0])

                dve.wait_ge(w_in, ALL_LOADED)
                dve.wait_ge(prep["pool"], POOL_PREP)
                link(v.tensor_scalar(hs[:], hs[:], small[:, 7:8], None, ALU.mult))
                assert n[0] == 1
                dve.wait_ge(prep["pe"], 2)
                link(v.tensor_tensor(kvl_sb[:, 0:D], b_s[:, 0:D], bk_row[:], ALU.add))
                link(v.tensor_copy(kvl_sb[:, D:2 * D], b_s[:, D:2 * D]))
                assert n[0] == KVL_DONE
                link(v.tensor_copy(hsT, b_s[:, 512:512 + D]))
                link(v.tensor_tensor(b_o1[:], b_o[:, 0:D], rows[1][:], ALU.add))
                link(v.tensor_tensor(b_o3[:], b_o[:, D:2 * D], rows[2][:], ALU.add))
                link(v.tensor_reduce(small[:, 4:6], hsT.rearrange("p (k n) -> p k n", k=KD)[:, :, 0:SLOTS], AX.X,
                                     ALU.add))
                link(v.tensor_scalar(small[:, 4:6], small[:, 4:6], 1.0 / SLOTS, None, ALU.mult))
                assert n[0] == MEAN_DONE
                dve.wait_ge(prep["act"], ACT_PREP)
                kv4 = w_kv32.rearrange("p (w k n) -> p w k n", w=4, k=KD)
                for i, w in enumerate((WK, WV, WQ, WO)):
                    link(v.tensor_tensor(w[1][:], kv4[:, i], w[0][:], ALU.subtract))
                link(v.tensor_tensor(WV2[1][:], wv232.rearrange("p (k n) -> p k n", k=KD), WV2[0][:], ALU.subtract))
                link(v.tensor_tensor(W1[1][:], w132.rearrange("p (k n) -> p k n", k=4)[:, 0:KD], W1[0][:],
                                     ALU.subtract))
                link(v.tensor_tensor(FQ[1][:, 0, 0:512], b_k[:], FQ[0][:, 0, 0:512], ALU.subtract))
                link(v.tensor_tensor(FQ[1][:, 0, 512:1024], b_v[:], FQ[0][:, 0, 512:1024], ALU.subtract))
                link(v.tensor_tensor(FQ[1][:, 1], b_a[:], FQ[0][:, 1], ALU.subtract))
                link(v.memset(vs[0][:, :, :, :, 4 * DK:4 * DK + 1], 1.0))
                link(v.memset(vs[1][:, :, :, :, 4 * DK:4 * DK + 1], 0.0))
                assert n[0] == FQ_DONE
                dve.wait_ge(prep["pe"], 3)
                link(v.tensor_copy(FK[0][:, 0, 0:512], b_k[:]))
                link(v.tensor_copy(FK[0][:, 0, 512:1024], b_v[:]))
                link(v.tensor_copy(FK[0][:, 1], b_a[:]))
                link(v.tensor_tensor(FK[1][:, 0, 0:512], b_k[:], FK[0][:, 0, 0:512], ALU.subtract))
                link(v.tensor_tensor(FK[1][:, 0, 512:1024], b_v[:], FK[0][:, 0, 512:1024], ALU.subtract))
                link(v.tensor_tensor(FK[1][:, 1], b_a[:], FK[0][:, 1], ALU.subtract))
                dve.wait_ge(prep["pe"], 4)
                link(v.tensor_tensor(c_h[:], b_x[:, 0:1], small[:, 10:11], ALU.add))
                link(v.tensor_tensor(c_rz[:], b_s[:, 0:512], bih_r, ALU.add))
                link(v.tensor_tensor(c_rz[:], c_rz[:], bhh_r, ALU.add))
                link(v.tensor_tensor(hn_half[:], b_s[:, 512:768], rows[3][:], ALU.add))
                link(v.tensor_scalar(hn_half[:], hn_half[:], 0.5, None, ALU.mult))
                link(v.tensor_copy(gvo[:].rearrange("p k n -> p (k n)"), b_o[:]))
                link(v.tensor_scalar(small[:, 11:12], small[:, 6:7], -1.0, None, ALU.mult))
                link(v.tensor_tensor(small[:, 12:13], small[:, 6:7], small[:, 11:12], ALU.max))
                link(v.tensor_scalar(small[:, 13:14], small[:, 12:13], 0.1, None, ALU.add))
                link(v.reciprocal(tinv[:], small[:, 13:14]))
                link(v.tensor_reduce(same_q[:], ident[:].rearrange("p (h r) -> p r h", h=4), AX.X, ALU.add))
                for b in range(BT):
                    link(v.tensor_copy(collapse[:, b, SQ * b:SQ * (b + 1)], same_q[:]))
                assert n[0] == DVE_PREP, n[0]

            def apart(*waits):
                for sm, val in waits:
                    dve.wait_ge(sm, val)
                dve.sem_inc(passed["dve"], 1)

            def norm_stats(stage, t, src, dst, n):
                v.bn_stats(st6[:, n, :], src).then_inc(*dve_at[stage].step("stats"))
                apart(dve_at[stage].after(t, "stats"))
                v.bn_aggr(mv[:, n, :], st6[:, n, :]).then_inc(*dve_at[stage].step("aggr"))
                dve.wait_ge(*dve_at[stage].after(t, "aggr"))
                v.tensor_scalar(vareps[:, n:n + 1], mv[:, n, 1:2], LN_EPS, None, ALU.add)\
                 .then_inc(*dve_at[stage].step("eps"))
                dve.wait_ge(*pool_at[stage].after(t, "rstd"))
                v.tensor_scalar(dst, src, mv[:, n, 0:1], rstd[:, n:n + 1], ALU.subtract, ALU.mult)\
                 .then_inc(*dve_at[stage].step("xn"))

            def run(item, turn):
                stage, kind, *arg_ = item
                t = tile_of(stage, turn)
                prev = t.shifted(-1)
                if kind == "P0":
                    dve.wait_ge(x_ld, t.times(16, 16))
                    if not t.first:
                        dve.wait_ge(*pe_at["P"].after(prev, "xT"))
                    norm_stats("P", t, x_in[:], xn1[:], 0)
                elif kind == "L2a":
                    dve.wait_ge(*dve_at["S1"].after(t, "x1"))
                    norm_stats("S2", t, x1[:], xn2[:], 1)
                elif kind == "3a":
                    dve.wait_ge(*dve_at["S2"].after(t, "x2"))
                    if not t.first:
                        dve.wait_ge(*pe_at["S3"].after(prev, "si"))
                    norm_stats("S3", t, x2[:], xn3[:], 2)
                elif kind in ("P1", "L2b", "3b"):
                    xT, bank = {"P1": (x1T, b_x), "L2b": (x2T, b_a), "3b": (x3T, b_x)}[kind]
                    dve.wait_ge(*act_at[stage].after(t, "xhi"))
                    v.tensor_tensor(xT[1][:].rearrange("p k n -> p (k n)"), bank[:, 0:D],
                                    xT[0][:].rearrange("p k n -> p (k n)"), ALU.subtract)\
                     .then_inc(*dve_at[stage].step("xlo"))
                elif kind == "P2":
                    dve.wait_ge(*act_at["P"].after(t, "qhi"))
                    if not t.first:
                        dve.wait_ge(*pool_at["P"].after(prev, "prod"))
                    v.scalar_tensor_tensor(qnat[:], b_x[:, 256:512], 0.25, bq4[:], ALU.mult, ALU.add)\
                     .then_inc(*dve_at["P"].step("qnat"))
                    v.tensor_tensor(qs[1][:], qf[:], qs[0][:], ALU.subtract).then_inc(*dve_at["P"].step("qlo"))
                elif kind == "P3":
                    dve.wait_ge(*dve_at["P"].after(t, "qlo"))
                    if not t.first:
                        dve.wait_ge(*pe_at["S1"].after(prev, "ST", BT - 1))
                    for n, name in ((0, "bdhi"), (1, "bdlo")):
                        q4 = qs[n][:].rearrange("p g (b q) -> p (g b) q", b=BT)
                        v.tensor_tensor(BD[n][:].rearrange("p g b h q -> p (g b) h q"),
                                        q4.unsqueeze(2).to_broadcast([P, 2 * BT, 8, SQ]),
                                        mask8[:].unsqueeze(1).to_broadcast([P, 2 * BT, 8, SQ]), ALU.mult)\
                         .then_inc(*dve_at["P"].step(name))
                    dve.wait_ge(*pool_at["P"].after(t, "prod"))
                    v.tensor_reduce(s_last[:], prod[:].rearrange("p (h d) -> p h d", h=H), AX.X, ALU.add)\
                     .then_inc(*dve_at["P"].step("slast"))
                elif kind == "KV":
                    b, = arg_
                    dve.wait_ge(*act_at["S1"].after(t, "kh1", b))
                    for n in range(2):
                        v.scalar_tensor_tensor(ks[1][:, b % 2, n], b_k[:, n * SK:(n + 1) * SK], bkc[:, n:n + 1],
                                               ks[0][:, b % 2, n], ALU.add, ALU.subtract)\
                         .then_inc(*dve_at["S1"].step(f"kl{n}", b))
                    dve.wait_ge(*act_at["S1"].after(t, "vh", b))
                    v.tensor_tensor(vs[1][:, b, :, :, 0:4 * DK].rearrange("p k j d -> p (k j) d"),
                                    b_v[:].rearrange("p (k d) -> p k d", d=4 * DK),
                                    vs[0][:, b, :, :, 0:4 * DK].rearrange("p k j d -> p (k j) d"), ALU.subtract)\
                     .then_inc(*dve_at["S1"].step("vl", b))
                elif kind == "A":
                    b, = arg_
                    dve.wait_ge(*pe_at["S1"].after(t, "A", b))
                    if not t.first:
                        dve.wait_ge(*pe_at["S1"].after(prev, "ST", b))
                    v.tensor_reduce(nmax[:, b, :], b_a[:].rearrange("p (j n) -> p j n", j=NQ), AX.X, ALU.max,
                                    negate=True).then_inc(*dve_at["S1"].step("max", b))
                elif kind == "PV":
                    b, = arg_
                    dve.wait_ge(*pe_at["S1"].after(t, "PV", b))
                    if not t.first:
                        dve.wait_ge(*pe_at["S1"].after(prev, "X"))
                    o4 = b_o[:, 0:NQ * 65].rearrange("p (j d) -> p j d", j=NQ)
                    mo = mask_o[:].rearrange("p a b -> p (a b)")
                    v.tensor_tensor(om[:, b, 0:D].rearrange("p (j d) -> p j d", j=NQ), o4[:, :, 0:64],
                                    mo.unsqueeze(1).to_broadcast([P, NQ, 64]), ALU.mult)\
                     .then_inc(*dve_at["S1"].step("om", b))
                    m4 = mask_o[:, :, 0].unsqueeze(1).to_broadcast([P, NQ, 4])
                    v.tensor_tensor(om[:, b, D:D + H].rearrange("p (j h) -> p j h", j=NQ),
                                    o4[:, :, 64:65].to_broadcast([P, NQ, 4]), m4, ALU.mult)\
                     .then_inc(*dve_at["S1"].step("zx", b))
                    v.tensor_tensor(om[:, b, D + H:D + 2 * H].rearrange("p (j h) -> p j h", j=NQ),
                                    nmax[:, b, :].unsqueeze(2).to_broadcast([P, NQ, 4]), m4, ALU.mult)\
                     .then_inc(*dve_at["S1"].step("mx", b))
                elif kind == "C1":
                    dve.wait_ge(*pe_at["S1"].after(t, "X"))
                    at = dve_at["S1"]
                    v.tensor_tensor(lk[:, 0], b_o[:, D + H:D + 2 * H], s_last[:], ALU.add).then_inc(*at.step("d"))
                    dve.wait_ge(*at.after(t, "d"))
                    v.tensor_scalar(lk[:, 1], lk[:, 0], -1.0, 0.0, ALU.mult, ALU.min).then_inc(*at.step("ta"))
                    v.tensor_scalar(lk[:, 2], lk[:, 0], 0.0, None, ALU.min).then_inc(*at.step("te"))
                    dve.wait_ge(*act_at["S1"].after(t, "ae"))
                    v.tensor_tensor(lk[:, 5], b_o[:, D:D + H], lk[:, 3], ALU.mult).then_inc(*at.step("za"))
                    dve.wait_ge(*at.after(t, "za"))
                    v.tensor_tensor(lk[:, 6], lk[:, 5], lk[:, 4], ALU.add).then_inc(*at.step("zt"))
                    dve.wait_ge(*at.after(t, "zt"))
                    v.reciprocal(lk[:, 7], lk[:, 6]).then_inc(*at.step("rz"))
                    dve.wait_ge(*at.after(t, "rz"))
                    v.tensor_tensor(lk2[:], lk[:, 4], lk[:, 7], ALU.mult).then_inc(*at.step("ea"))
                    v.scalar_tensor_tensor(lk[:, 5], lk[:, 3], 1.0, lk[:, 7], ALU.mult, ALU.mult)\
                     .then_inc(*at.step("at0"))
                    dve.wait_ge(*at.after(t, "at0"))
                    v.tensor_tensor(attn[:].rearrange("p (h d) -> p h d", h=H),
                                    b_o[:, 0:D].rearrange("p (h d) -> p h d", h=H),
                                    lk[:, 5].unsqueeze(2).to_broadcast([P, H, DK]), ALU.mult)\
                     .then_inc(*at.step("at"))
                elif kind == "C2":
                    dve.wait_ge(*act_at["S1"].after(t, "ahi"))
                    v.tensor_tensor(attT[1][:].rearrange("p k n -> p (k n)"), b_k[:, 0:D],
                                    attT[0][:].rearrange("p k n -> p (k n)"), ALU.subtract)\
                     .then_inc(*dve_at["S1"].step("alo"))
                elif kind == "C3":
                    dve.wait_ge(*pe_at["S1"].after(t, "o"))
                    v.tensor_tensor(x1[:], b_v[:, 0:D], xres[:], ALU.add).then_inc(*dve_at["S1"].step("x1"))
                elif kind == "F":
                    c, = arg_
                    at = dve_at["S2"]
                    dve.wait_ge(*pe_at["S2"].after(t, "f", c))
                    if not t.first:
                        dve.wait_ge(*pe_at["S2"].after(prev, "T", c, 1))
                    f = (b_k, b_v)[c % 2][:].rearrange("p (h f) -> p h f", h=8)
                    v.tensor_reduce(fmx[:, c, 0], f, AX.X, ALU.max).then_inc(*at.step("max", c))
                    v.tensor_reduce(fmx[:, c, 1], f, AX.X, ALU.min).then_inc(*at.step("min", c))
                    dve.wait_ge(*at.after(t, "max", c))
                    v.tensor_tensor(arg[:, c, :, 0, :], f, fmx[:, c, 0].unsqueeze(2).to_broadcast([P, 8, HD]),
                                    ALU.subtract).then_inc(*at.step("subp", c))
                    dve.wait_ge(*at.after(t, "min", c))
                    v.scalar_tensor_tensor(arg[:, c, :, 1, :], f, -1.0,
                                           fmx[:, c, 1].unsqueeze(2).to_broadcast([P, 8, HD]),
                                           ALU.mult, ALU.add).then_inc(*at.step("subm", c))
                    dve.wait_ge(*act_at["S2"].after(t, "exp", c))
                    v.tensor_reduce(fsum[:, c, 0].rearrange("p h s -> p (h s)"),
                                    arg[:, c].rearrange("p h s f -> p (h s) f"), AX.X, ALU.add)\
                     .then_inc(*at.step("sum", c))
                    dve.wait_ge(*at.after(t, "sum", c))
                    v.reciprocal(fsum[:, c, 1], fsum[:, c, 0]).then_inc(*at.step("rs", c))
                    dve.wait_ge(*pool_at["S2"].after(t, "norm", c))
                    fl = arg[:, c].rearrange("p h s f -> p (h s f)")
                    v.tensor_scalar(fl, fl, FEAT_EPS, None, ALU.max).then_inc(*at.step("clamp", c))
                elif kind == "AT":
                    g4, = arg_
                    dve.wait_ge(*pe_at["S2"].after(t, "AT", g4))
                    if g4 >= 2:
                        dve.wait_ge(*pe_at["S2"].after(t, "AV", g4 - 2))
                    elif not t.first:
                        dve.wait_ge(*pe_at["S2"].after(prev, "AV", g4 + 2))
                    v.tensor_tensor(at_m[:, g4 % 2],
                                    b_s[:, g4 % 2 * 512:g4 % 2 * 512 + 512].rearrange("p (h n) -> p h n", h=4),
                                    mask_c[:].unsqueeze(1).to_broadcast([P, 4, P]), ALU.mult)\
                     .then_inc(*dve_at["S2"].step("mask", g4))
                elif kind == "AV":
                    g4, = arg_
                    at = dve_at["S2"]
                    dve.wait_ge(*pe_at["S2"].after(t, "AV", g4))
                    if not t.first:
                        dve.wait_ge(*pe_at["S2"].after(prev, "Y", g4 // 2))
                    o = b_o[:, 0:384].rearrange("p (h d) -> p h d", h=4)
                    v.tensor_scalar(zr[:, g4, 0], o[:, :, HD], FEAT_EPS, None, ALU.add).then_inc(*at.step("z", g4))
                    dve.wait_ge(*at.after(t, "z", g4))
                    v.reciprocal(zr[:, g4, 1], zr[:, g4, 0]).then_inc(*at.step("rz", g4))
                    dve.wait_ge(*at.after(t, "rz", g4))
                    v.tensor_tensor(y[:, g4 * 256:(g4 + 1) * 256].rearrange("p (h d) -> p h d", h=4), o[:, :, 0:HD],
                                    zr[:, g4, 1].unsqueeze(2).to_broadcast([P, 4, HD]), ALU.mult)\
                     .then_inc(*at.step("y", g4))
                elif kind == "W":
                    dve.wait_ge(*pe_at["S2"].after(t, "W"))
                    v.tensor_tensor(x2[:], b_k[:, 0:D], x1[:], ALU.add).then_inc(*dve_at["S2"].step("x2"))
                elif kind == "3d":
                    at = dve_at["S3"]
                    dve.wait_ge(*pe_at["S3"].after(t, "lg"))
                    v.tensor_tensor(lg[:, 0], b_x[:, 0:SLOTS], b2r[:], ALU.add).then_inc(*at.step("lb"))
                    dve.wait_ge(*at.after(t, "lb"))
                    v.tensor_scalar(lg[:, 1], lg[:, 0], tinv[:, 0:1], None, ALU.mult).then_inc(*at.step("lg"))
                    apart(at.after(t, "lg"))
                    v.max(sc3[:, 0:8], lg[:, 1]).then_inc(*at.step("top"))
                    apart(at.after(t, "top"))
                    v.match_replace(lg[:, 2], sc3[:, 0:8], lg[:, 1], NEG).then_inc(*at.step("repl"))
                    dve.wait_ge(*at.after(t, "repl"))
                    v.tensor_tensor(lg[:, 3], lg[:, 2], lg[:, 1], ALU.not_equal).then_inc(*at.step("sel"))
                    v.tensor_scalar(sc3[:, 8:9], sc3[:, 0:1], -1.0, None, ALU.mult).then_inc(*at.step("nmax"))
                    dve.wait_ge(*act_at["S3"].after(t, "e"))
                    dve.wait_ge(*at.after(t, "sel"))
                    v.scalar_tensor_tensor(lg[:, 5], lg[:, 4], 1.0, lg[:, 3], ALU.mult, ALU.mult,
                                           accum_out=sc3[:, 9:10]).then_inc(*at.step("ea"))
                    dve.wait_ge(*at.after(t, "ea"))
                    v.reciprocal(sc3[:, 10:11], sc3[:, 9:10]).then_inc(*at.step("rs"))
                    dve.wait_ge(*at.after(t, "rs"))
                    v.tensor_scalar(lg[:, 0], lg[:, 5], sc3[:, 10:11], None, ALU.mult).then_inc(*at.step("al"))
                    dve.wait_ge(*at.after(t, "al"))
                    if not t.first:
                        dve.wait_ge(*pe_at["S3"].after(prev, "aT"))
                    v.tensor_tensor(abd[:], lg[:, 0].unsqueeze(1).to_broadcast([P, BT, SLOTS]),
                                    mask_o[:, :, 0].unsqueeze(2).to_broadcast([P, BT, SLOTS]), ALU.mult)\
                     .then_inc(*at.step("abd"))
                elif kind == "3f":
                    at = dve_at["S3"]
                    dve.wait_ge(*act_at["S3"].after(t, "aT"))
                    v.tensor_scalar(rw[:, 0], b_x[:, 2 * P:2 * P + 2], WSUM_EPS, None, ALU.add)\
                     .then_inc(*at.step("ws"))
                    dve.wait_ge(*at.after(t, "ws"))
                    v.reciprocal(rw[:, 1], rw[:, 0]).then_inc(*at.step("rw"))
                elif kind == "3g":
                    n, = arg_
                    dve.wait_ge(*pe_at["S3"].after(t, "rz", n))
                    if n == 0:
                        dve.wait_ge(*dve_at["S3"].after(t, "rw"))
                    v.scalar_tensor_tensor(rz[:, n], b_x[:], rw[:, 1, n:n + 1], c_rz[:], ALU.mult, ALU.add)\
                     .then_inc(*dve_at["S3"].step("rz", n))
                elif kind == "3h":
                    n, = arg_
                    at = dve_at["S3"]
                    dve.wait_ge(*pe_at["S3"].after(t, "n", n))
                    if n == 1:
                        dve.wait_ge(*pool_at["S3"].after(t, "w", 0))
                    v.scalar_tensor_tensor(gu[:, 0], b_x[:, 0:D], rw[:, 1, n:n + 1], bihn[:], ALU.mult, ALU.add)\
                     .then_inc(*at.step("u", n))
                    dve.wait_ge(*act_at["S3"].after(t, "tanh", n))
                    v.scalar_tensor_tensor(gu[:, 1], rz[:, n, 0:D], 1.0, hn_half[:], ALU.add, ALU.mult)\
                     .then_inc(*at.step("v", n))
                    dve.wait_ge(*pool_at["S3"].after(t, "d", n))
                    v.scalar_tensor_tensor(gu[:, 5], rz[:, n, D:2 * D], 1.0, gu[:, 4], ALU.add, ALU.mult)\
                     .then_inc(*at.step("q", n))
                    dve.wait_ge(*at.after(t, "q", n))
                    v.scalar_tensor_tensor(s_new[:, n], gu[:, 5], 0.5, gu[:, 3], ALU.mult, ALU.add)\
                     .then_inc(*at.step("S", n))
                elif kind == "3j":
                    dve.wait_ge(*pe_at["S3"].after(t, "y"))
                    if not t.first:
                        dve.wait_ge(out_st, t.times(16, 0))
                    v.tensor_tensor(y_out[:], b_x[:, 0:D], x2b[:], ALU.add).then_inc(*dve_at["S3"].step("out"))

            turns(run, dve, before, lambda: None)

        @block.tensor
        def _(pe):
            def mm(out, lhsT, rhs, start, stop):
                return pe.matmul(out, lhsT, rhs, start=start, stop=stop, skip_group_check=True)

            def split_product(out, terms, start=True, stop=True):
                last = None
                for n, (lh, ll, rh, rl) in enumerate(terms):
                    end = stop and n == len(terms) - 1
                    mm(out, lh, rh, start and n == 0, False)
                    mm(out, lh, rl, False, False)
                    last = mm(out, ll, rh, False, end)
                return last

            def before():
                pe.wait_ge(w_in, ALL_LOADED)
                pe.wait_ge(prep["pool"], POOL_PREP)

                def features(w32, k32):
                    wv = w32[0:HD].rearrange("p (h n) -> p h n", h=H)
                    kv = k32[0:HD].rearrange("p (h n) -> p h n", h=H)
                    for h in range(H):
                        for k in range(KD):
                            bank = [(b_k, b_v)[h // 8][:], b_a[:, h // 8 * 512:h // 8 * 512 + 512]][k]
                            last = mm(bank[:, h % 8 * HD:(h % 8 + 1) * HD], wv[:, h, k * P:(k + 1) * P], kv[:, h, :],
                                      True, True)
                    return last

                features(w2q32, kq32).then_inc(prep["pe"], 1)
                kv4 = w_kv32.rearrange("p (w k n) -> p w k n", w=4, k=KD)
                cl = ctl.rearrange("p (k n) -> p k n", k=KD)
                for w in range(2):
                    for k in range(KD):
                        mm(b_s[:, w * D:(w + 1) * D], cl[:, k, :], kv4[:, w, k, :], k == 0, k == KD - 1)
                for w, wo in ((0, kv4[:, 3]), (1, wo3)):
                    for k in range(KD):
                        mm(b_o[:, w * D:(w + 1) * D], small[:, 2 * w + k:2 * w + k + 1].to_broadcast([P, P]),
                           wo[:, k, :], k == 0, k == KD - 1)
                pe.wait_ge(prep["dve"], 1)
                for k in range(KD):
                    last = pe.transpose(b_s[:, 512 + k * P:512 + (k + 1) * P], hs[:, k * P:(k + 1) * P], ident[:])
                last.then_inc(prep["pe"], 1)
                pe.wait_ge(prep["dve"], FQ_DONE)
                features(w2k32, kk32).then_inc(prep["pe"], 1)
                hT_ = hsT.rearrange("p (k n) -> p k n", k=KD)
                w1_ = w132.rearrange("p (k n) -> p k n", k=4)
                for k in range(KD):
                    mm(b_x[:, 0:1], w1_[:, KD + k, :], small[:, 4 + k:5 + k], k == 0, k == KD - 1)
                for lo, n in ((0, 512), (512, 256)):
                    for k in range(KD):
                        mm(b_s[:, lo:lo + n], hT_[:, k, :], whh32[:, k, lo:lo + n], k == 0, k == KD - 1)
                for m in range(KD):
                    for k in range(KD):
                        last = mm(b_o[:, m * D:(m + 1) * D], wv3[:, k, m * P:(m + 1) * P], wo3[:, k, :], k == 0,
                                  k == KD - 1)
                last.then_inc(prep["pe"], 1)
                pe.wait_ge(prep["dve"], DVE_PREP)

            def transposed(stage, t, src, bank):
                for k in range(KD):
                    last = pe.transpose(bank[:, k * P:(k + 1) * P], src[:, k * P:(k + 1) * P], ident[:])
                last.then_inc(*pe_at[stage].step("xT"))

            def run(item, turn):
                stage, kind, *arg_ = item
                t = tile_of(stage, turn)
                prev = t.shifted(-1)
                if kind == "P1":
                    pe.wait_ge(*dve_at["P"].after(t, "xn"))
                    if t.off >= 2 or t.reg is not None:
                        pe.wait_ge(*dve_at["S3"].after(t.shifted(-2), "out"))
                    transposed("P", t, xn1, b_x)
                elif kind == "L2b":
                    pe.wait_ge(*dve_at["S2"].after(t, "xn"))
                    transposed("S2", t, xn2, b_a)
                elif kind == "3b":
                    pe.wait_ge(*dve_at["S3"].after(t, "xn"))
                    transposed("S3", t, xn3, b_x)
                elif kind == "P2":
                    pe.wait_ge(*dve_at["P"].after(t, "xlo"))
                    for g in range(2):
                        split_product(b_x[:, g * P:(g + 1) * P],
                                      [(WQ[0][:, k, g * P:(g + 1) * P], WQ[1][:, k, g * P:(g + 1) * P],
                                        x1T[0][:, k], x1T[1][:, k]) for k in range(KD)])
                    split_product(b_x[:, D:2 * D],
                                  [(x1T[0][:, k], x1T[1][:, k], WQ[0][:, k], WQ[1][:, k]) for k in range(KD)])\
                        .then_inc(*pe_at["P"].step("q"))
                elif kind == "KV":
                    b, = arg_
                    pe.wait_ge(*pool_at["S1"].after(t, "clo", b))
                    if b:
                        pe.wait_ge(*dve_at["S1"].after(t, "vl", b - 1))
                    elif not t.first:
                        pe.wait_ge(*act_at["S2"].after(prev, "v", 1))
                        pe.wait_ge(*dve_at["S2"].after(prev, "x2"))
                    c = [cs[n][:, b % 2] for n in range(2)]
                    for g in range(2):
                        last = split_product(b_k[:, g * SK:(g + 1) * SK],
                                             [(WK[0][:, k, g * P:(g + 1) * P], WK[1][:, k, g * P:(g + 1) * P],
                                               c[0][:, k], c[1][:, k]) for k in range(KD)])
                    last.then_inc(*pe_at["S1"].step("kT", b))
                    for m in range(2):
                        last = split_product(b_v[:, m * D:(m + 1) * D],
                                             [(c[0][:, k, m * P:(m + 1) * P], c[1][:, k, m * P:(m + 1) * P],
                                               WV[0][:, k], WV[1][:, k]) for k in range(KD)])
                    last.then_inc(*pe_at["S1"].step("v", b))
                elif kind == "A":
                    b, = arg_
                    pe.wait_ge(*act_at["S1"].after(t, "kh1", b))
                    if b:
                        pe.wait_ge(*dve_at["S1"].after(t, "max", b - 1))
                    else:
                        pe.wait_ge(*dve_at["P"].after(t, "bdlo"))
                        if not t.first:
                            pe.wait_ge(*act_at["S2"].after(prev, "yT", 1))
                    for j in range(NQ):
                        q = BD[0][:, j // 2, b].rearrange("p h q -> p (h q)")[:, j % 2 * P:(j % 2 + 1) * P]
                        last = mm(b_a[:, j * SK:(j + 1) * SK], q, ks[0][:, b % 2, j // 2], True, True)
                    last.then_inc(*pe_at["S1"].step("A", b))
                elif kind == "ST":
                    b, = arg_
                    pe.wait_ge(*dve_at["S1"].after(t, "kl1", b))
                    if b:
                        pe.wait_ge(*act_at["S1"].after(t, "ph", b - 1))
                    elif not t.first:
                        pe.wait_ge(*dve_at["S2"].after(prev, "mask", 3))
                    for m in range(2):
                        for g in range(2):
                            k = [ks[n][:, b % 2, g, m * P:(m + 1) * P] for n in range(2)]
                            q = [BD[n][:, g, b].rearrange("p h q -> p (h q)") for n in range(2)]
                            split_product(b_s[:, m * 512 + g * 256:m * 512 + (g + 1) * 256],
                                          [(k[0], k[1], q[0], q[1])], start=(g == 0), stop=False)
                    pe.wait_ge(*dve_at["S1"].after(t, "max", b))
                    for m in range(2):
                        for j in range(NQ):
                            last = mm(b_s[:, m * 512 + j * P:m * 512 + (j + 1) * P],
                                      nmax[:, b, j:j + 1].to_broadcast([P, P]), identb[:], False, True)
                    last.then_inc(*pe_at["S1"].step("ST", b))
                elif kind == "PV":
                    b, = arg_
                    pe.wait_ge(*pool_at["S1"].after(t, "plo", b))
                    pe.wait_ge(*dve_at["S1"].after(t, "vl", b))
                    if b:
                        pe.wait_ge(*dve_at["S1"].after(t, "zx", b - 1))
                    elif not t.first:
                        pe.wait_ge(*dve_at["S2"].after(prev, "y", 3))
                    for j in range(NQ):
                        p = [[ps[n][:, b % 2, m, j * P:(j + 1) * P] for n in range(2)] for m in range(2)]
                        w = [[vs[n][:, b, m, j, :] for n in range(2)] for m in range(2)]
                        last = split_product(b_o[:, j * 65:(j + 1) * 65],
                                             [(p[m][0], p[m][1], w[m][0], w[m][1]) for m in range(2)])
                    last.then_inc(*pe_at["S1"].step("PV", b))
                elif kind == "C1":
                    pe.wait_ge(*dve_at["S1"].after(t, "mx", BT - 1))
                    for b in range(BT):
                        last = mm(b_o[:, 0:D + 2 * H], collapse[:, b], om[:, b], b == 0, b == BT - 1)
                    last.then_inc(*pe_at["S1"].step("X"))
                elif kind == "C2":
                    pe.wait_ge(*dve_at["S1"].after(t, "at"))
                    pe.wait_ge(*pool_at["S1"].after(t, "wv"))
                    for k in range(KD):
                        mm(b_k[:, k * P:(k + 1) * P], attn[:, k * P:(k + 1) * P], ident[:], True, False)
                        last = mm(b_k[:, k * P:(k + 1) * P], wv_l[:, k * P:(k + 1) * P], ident[:], False, True)
                    last.then_inc(*pe_at["S1"].step("aT"))
                elif kind == "C3":
                    pe.wait_ge(*dve_at["S1"].after(t, "alo"))
                    split_product(b_v[:, 0:D],
                                  [(attT[0][:, k], attT[1][:, k], WO[0][:, k], WO[1][:, k]) for k in range(KD)])\
                        .then_inc(*pe_at["S1"].step("o"))
                elif kind == "F":
                    c, = arg_
                    if c == 0:
                        pe.wait_ge(*dve_at["S2"].after(t, "xlo"))
                    elif c == 1:
                        pe.wait_ge(*dve_at["S1"].after(t, "x1"))
                    elif c == 2:
                        pe.wait_ge(*act_at["S2"].after(t, "v", 0))
                    else:
                        pe.wait_ge(*dve_at["S2"].after(t, "subm", 1))
                    w, lo = (FQ, FK)[c % 2], c // 2 * 512
                    split_product((b_k, b_v)[c % 2][:],
                                  [(x2T[0][:, k], x2T[1][:, k], w[0][:, k, lo:lo + 512], w[1][:, k, lo:lo + 512])
                                   for k in range(KD)]).then_inc(*pe_at["S2"].step("f", c))
                elif kind == "V":
                    n, = arg_
                    pe.wait_ge(*dve_at["S2"].after(t, "subm", (0, 3)[n]))
                    split_product((b_k, b_v)[n][:],
                                  [(x2T[0][:, k], x2T[1][:, k], WV2[0][:, k, n * 512:(n + 1) * 512],
                                    WV2[1][:, k, n * 512:(n + 1) * 512]) for k in range(KD)])\
                        .then_inc(*pe_at["S2"].step("v", n))
                elif kind == "T":
                    c, i = arg_
                    pe.wait_ge(*dve_at["S2"].after(t, "clamp", c))
                    if i:
                        pe.wait_ge(*act_at["S2"].after(t, "feat", c, 0))
                    elif c >= 2:
                        pe.wait_ge(*act_at["S2"].after(t, "feat", c - 2, 1))
                    for h in range(4):
                        bank = b_a[:, (c % 2) * 512 + h * P:(c % 2) * 512 + (h + 1) * P]
                        last = pe.transpose(bank, arg[:, c, 4 * i + h].rearrange("p s f -> p (s f)"), ident[:])
                    last.then_inc(*pe_at["S2"].step("T", c, i))
                elif kind == "AT":
                    g4, = arg_
                    c, i = g4 // 2 * 2, g4 % 2
                    pe.wait_ge(*act_at["S2"].after(t, "feat", c + 1, i))
                    if g4 >= 2:
                        pe.wait_ge(*dve_at["S2"].after(t, "mask", g4 - 2))
                    for h in range(4):
                        last = mm(b_s[:, g4 % 2 * 512 + h * P:g4 % 2 * 512 + (h + 1) * P], featT[:, c + 1, i, h],
                                  featT[:, c, i, h], True, True)
                    last.then_inc(*pe_at["S2"].step("AT", g4))
                elif kind == "AV":
                    g4, = arg_
                    pe.wait_ge(*dve_at["S2"].after(t, "mask", g4))
                    pe.wait_ge(*act_at["S2"].after(t, "v", min(1, (g4 + 1) // 2)))
                    if g4:
                        pe.wait_ge(*dve_at["S2"].after(t, "y", g4 - 1))
                    for h in range(4):
                        lo = (4 * g4 + h) * (HD + 1)
                        last = mm(b_o[:, h * 96:(h + 1) * 96], at_m[:, g4 % 2, h], v1[:, lo:lo + 96], True, True)
                    last.then_inc(*pe_at["S2"].step("AV", g4))
                elif kind == "Y":
                    n, = arg_
                    pe.wait_ge(*dve_at["S2"].after(t, "y", 2 * n + 1))
                    pe.wait_ge(*act_at["S2"].after(t, "feat", 2 + n, 1))
                    for h in range(4):
                        last = pe.transpose(b_a[:, n * 512 + h * P:n * 512 + (h + 1) * P],
                                            y[:, (4 * n + h) * P:(4 * n + h + 1) * P], ident[:])
                    last.then_inc(*pe_at["S2"].step("Y", n))
                elif kind == "W":
                    pe.wait_ge(*act_at["S2"].after(t, "yT", 1))
                    for k in range(8):
                        last = mm(b_k[:, 0:D], yT[:, k], wo2[:, k], k == 0, k == 7)
                    last.then_inc(*pe_at["S2"].step("W"))
                elif kind == "3c":
                    pe.wait_ge(*dve_at["S3"].after(t, "xlo"))
                    split_product(b_x[:, 0:P],
                                  [(W1[0][:, k], W1[1][:, k], x3T[0][:, k], x3T[1][:, k]) for k in range(KD)])\
                        .then_inc(*pe_at["S3"].step("h"))
                elif kind == "3d":
                    pe.wait_ge(*act_at["S3"].after(t, "gelu"))
                    mm(b_x[:, 0:SLOTS], hT[:], w2[:], True, True).then_inc(*pe_at["S3"].step("lg"))
                elif kind == "3e":
                    pe.wait_ge(*dve_at["S3"].after(t, "abd"))
                    for k in range(KD):
                        last = mm(b_x[:, k * D:(k + 1) * D], xn3[:, k * P:(k + 1) * P],
                                  abd[:].rearrange("p b s -> p (b s)"), True, True)
                    last.then_inc(*pe_at["S3"].step("si"))
                elif kind == "3f":
                    pe.wait_ge(*act_at["S3"].after(t, "si"))
                    ab = abd[:].rearrange("p b s -> p (b s)")
                    for n in range(2):
                        pe.transpose(b_x[:, n * P:(n + 1) * P], ab[:, n * P:(n + 1) * P], ident[:])
                    for n in range(2):
                        last = mm(b_x[:, 2 * P + n:2 * P + n + 1], ab[:, n * P:(n + 1) * P], v1[:, HD:HD + 1], True,
                                  True)
                    last.then_inc(*pe_at["S3"].step("aT"))
                elif kind == "3g":
                    n, = arg_
                    if n:
                        pe.wait_ge(*dve_at["S3"].after(t, "u", n - 1))
                    else:
                        pe.wait_ge(*dve_at["S3"].after(t, "ws"))
                    for k in range(KD):
                        last = mm(b_x[:], siT[:, k, n * P:(n + 1) * P], wih[:, k, 0:2 * D], k == 0, k == KD - 1)
                    last.then_inc(*pe_at["S3"].step("rz", n))
                elif kind == "3h":
                    n, = arg_
                    pe.wait_ge(*dve_at["S3"].after(t, "rz", n))
                    for k in range(KD):
                        last = mm(b_x[:, 0:D], siT[:, k, n * P:(n + 1) * P], wih[:, k, 2 * D:3 * D], k == 0,
                                  k == KD - 1)
                    last.then_inc(*pe_at["S3"].step("n", n))
                elif kind == "3i":
                    pe.wait_ge(*dve_at["S3"].after(t, "S", 1))
                    for k in range(KD):
                        for n in range(2):
                            last = mm(b_x[:, k * P:(k + 1) * P], s_new[:, n, k * P:(k + 1) * P], aT[:, n], n == 0,
                                      n == 1)
                    last.then_inc(*pe_at["S3"].step("as"))
                elif kind == "3j":
                    pe.wait_ge(*act_at["S3"].after(t, "as"))
                    for k in range(KD):
                        last = mm(b_x[:, 0:D], asT[:, k], gvo[:, k], k == 0, k == KD - 1)
                    last.then_inc(*pe_at["S3"].step("y"))

            turns(run, pe, before, lambda: None)


KVL_DONE = 3
MEAN_DONE = 8
FQ_DONE = 19
DVE_PREP = 40


def kernel(_tiles=None, **inputs):
    import numpy as _np
    import concourse.bacc as _bacc
    from concourse import mybir as _mybir
    from concourse.bass_utils import run_bass_kernel_spmd as _run

    i = {k: _np.asarray(v) for k, v in inputs.items()}
    n_b = i["x"].shape[0]
    all_tiles = n_b // BT
    tiles = _tiles or all_tiles

    def chunks(w):
        return _np.ascontiguousarray(w.reshape(-1, P, w.shape[1]).transpose(1, 0, 2))

    def column(b):
        return _np.ascontiguousarray(b.reshape(-1, P).T)

    def heads(w):
        return _np.ascontiguousarray(w.reshape(D, H, HD).transpose(2, 1, 0))

    c = i["ctx_1024"]
    arrays = {
        "x": i["x"].reshape(all_tiles, P, D),
        "ctx": _np.ascontiguousarray(c[:, :SK].reshape(n_b, SK, KD, P).transpose(0, 3, 2, 1)),
        "ctx_last": _np.ascontiguousarray(c[:, SK].reshape(n_b, KD, P).transpose(2, 1, 0)),
        "xWq": chunks(i["L0_xattn_Wq"].T), "xWk": chunks(i["L0_xattn_Wk"].T), "xWv": chunks(i["L0_xattn_Wv"].T),
        "xWo": chunks(i["L0_xattn_Wo"].T),
        "xbq": i["L0_xattn_bq"], "xbk": i["L0_xattn_bk"], "xbo": i["L0_xattn_bo"],
        "xbv": column(i["L0_xattn_bv"]), "xbq_col": column(i["L0_xattn_bq"]), "xbk_col": column(i["L0_xattn_bk"]),
        "aWq": heads(i["L0_attn_Wq"]), "aWk": heads(i["L0_attn_Wk"]), "aWv": chunks(i["L0_attn_Wv"]),
        "aWo": chunks(i["L0_attn_Wo"]),
        "aKq": _np.ascontiguousarray(i["L0_attn_Kq"].transpose(1, 0, 2)),
        "aKk": _np.ascontiguousarray(i["L0_attn_Kk"].transpose(1, 0, 2)),
        "slot_init": i["L0_ffn_slot_init"], "slot_scale": i["L0_ffn_slot_scale"],
        "fw1": chunks(i["L0_ffn_w1"].T), "fb1": column(i["L0_ffn_b1"]),
        "fw2": _np.ascontiguousarray(i["L0_ffn_w2"].T), "fb2": i["L0_ffn_b2"],
        "fwih": chunks(i["L0_ffn_gru_wih"].T), "fwhh": chunks(i["L0_ffn_gru_whh"].T),
        "fbih": i["L0_ffn_gru_bih"], "fbhh": i["L0_ffn_gru_bhh"],
        "fWv": chunks(i["L0_ffn_wv"]), "fbv": column(i["L0_ffn_bv"]),
        "fWo": chunks(i["L0_ffn_wo"].T), "fbo": i["L0_ffn_bo"], "tau": i["L0_ffn_tau"],
    }
    nc = _bacc.Bacc("TRN2", target_bir_lowering=False, num_devices=1)
    sent, aps = {}, {}
    for name, v in arrays.items():
        v = _np.ascontiguousarray(v)
        sent[f"in_{name}"] = v
        aps[name] = nc.dram_tensor(f"in_{name}", v.shape, _mybir.dt.from_np(v.dtype), kind="ExternalInput").ap()
    aps["out"] = nc.dram_tensor("out_0", (all_tiles, P, D), F32, kind="ExternalOutput").ap()
    bass_perceiver_layer(nc, aps, tiles)
    r = _run(nc, [sent], core_ids=[0])
    return r.results[0]["out_0"].reshape(n_b, SQ, D)
```

```python
from contextlib import ExitStack

import concourse.bass as bass
from concourse import mybir

F32 = mybir.dt.float32
F16 = mybir.dt.float16
BF16 = mybir.dt.bfloat16
ALU = mybir.AluOpType
ACT = mybir.ActivationFunctionType
AX = mybir.AxisListType

P = 128
D = 256
KD = D // P
BT = 4
SQ = 32
SK = 256
H = 16
DK = D // H
HD = 64
E2 = H * HD
NQ = 4
SLOTS = 64
BANK_F32 = 512
NEG = -3.0e38
LN_EPS = 1e-5
FEAT_EPS = 1e-12
WSUM_EPS = 1e-8

STEPS = {
    "pe": {
        "P1": ["xT"], "P2": ["q"],
        "K": ["kT"], "VB": ["v"], "A": ["A"], "ST": ["ST"], "PV": ["PV"], "C1": ["X"], "C2": ["aT"], "C3": ["o"],
        "L2b": ["xT"], "F": ["f"], "V": ["v"], "T": ["T"], "AT": ["AT"], "AV": ["AV"], "Y": ["Y"], "W": ["W"],
        "3b": ["xT"], "3c": ["h"], "3d": ["lg"], "3e": ["si"], "3f": ["aT"], "3g": ["rz"], "3h": ["n"],
        "3i": ["as"], "3j": ["y"],
    },
    "act": {
        "P1": ["xhi"], "P2": ["qf0", "qf1", "qhi"],
        "CS": ["chi"], "K": ["kh0", "kh1"], "VB": ["vh"], "ST": ["ph", "pf"], "C1": ["ae"], "C2": ["ahi"],
        "L2b": ["xhi"], "F": ["exp"], "V": ["v"], "T": ["feat"], "Y": ["yT"],
        "3b": ["xhi"], "3c": ["gelu"], "3d": ["e"], "3e": ["si"], "3f": ["aT"], "3g": ["tanh"], "3h": ["n"],
        "3i": ["as"],
    },
    "dve": {
        "P0": ["stats", "aggr", "eps"], "P0x": ["xn"], "P1": ["xlo"], "P2": ["qnat", "qlo"],
        "P3": ["bdhi", "bdlo"], "P4": ["slast"],
        "K": ["kl0", "kl1"], "VB": ["vl"], "A": ["max"], "PV": ["om", "zx", "mx"],
        "C1": ["d", "ta", "te"], "C1e": ["za", "zt", "rz", "ea", "at0", "at"], "C2": ["alo"], "C3": ["x1"],
        "L2a": ["stats", "aggr", "eps"], "L2x": ["xn"], "L2b": ["xlo"],
        "F": ["max", "min", "subp", "subm"], "G": ["sum", "rs"], "N": ["clamp"], "AT": ["mask"],
        "AV": ["z", "rz", "y"], "W": ["x2"],
        "3a": ["stats", "aggr", "eps"], "3x": ["xn"], "3b": ["xlo"],
        "3d": ["lb", "lg", "top", "repl", "sel", "nmax"], "3w": ["ea", "rs", "al", "abd"],
        "3f": ["ws", "rw"], "3g": ["rz"], "3h": ["u"], "3v": ["v"], "3S": ["q", "S"], "3j": ["out"],
    },
    "pool": {
        "P0": ["rstd"], "P4": ["xres", "prod"],
        "CS": ["clo"], "ST": ["plo"], "C1": ["wv"],
        "L2a": ["rstd"], "N": ["norm"],
        "3a": ["x2b"], "3x": ["rstd"], "3h": ["w"], "3S": ["d"],
    },
}
ORDERS = {
    "pe": """
        W@-2 C2@-1 P1 3j@-3 C3@-1 P2 3b@-2 K.0 VB.0 L2b@-1 3c@-2 K.1 VB.1 3d@-2 A.0 F.0@-1 F.1@-1 A.1
        ST.0 3e@-2 ST.1 3f@-2 K.2 VB.2 3g.0@-2 A.2 V.0@-1 3h.0@-2 K.3 F.2@-1 PV.0 T.0.0@-1 ST.2 VB.3
        F.3@-1 T.1.0@-1 T.0.1@-1 V.1@-1 A.3 PV.1 T.1.1@-1 3g.1@-2 AT.0@-1 AT.1@-1 ST.3 AV.0@-1 PV.2
        T.2.0@-1 AV.1@-1 T.3.0@-1 T.2.1@-1 T.3.1@-1 3h.1@-2 AT.2@-1 AT.3@-1 PV.3 Y.0@-1 AV.2@-1 AV.3@-1
        C1 Y.1@-1 3i@-2
    """,
    "act": """
        3i@-3 C1@-1 C2@-1 P1 CS.0 CS.1 P2 3b@-2 K.0 L2b@-1 VB.0 3c@-2 K.1 CS.2 3d@-2 VB.1 CS.3 ST.0
        3e@-2 F.0@-1 3f@-2 K.2 ST.1 F.1@-1 K.3 VB.2 3g.0@-2 V.0@-1 T.0.0@-1 ST.2 3h.0@-2 T.1.0@-1
        T.0.1@-1 F.2@-1 V.1@-1 F.3@-1 T.1.1@-1 VB.3 ST.3 T.2.0@-1 T.3.0@-1 T.2.1@-1 T.3.1@-1 3g.1@-2
        Y.0@-1 3h.1@-2 Y.1@-1
    """,
    "dve": """
        P0 C1@-1 P0x C1e@-1 W@-2 C2@-1 P1 3j@-3 3a@-2 C3@-1 L2a@-1 3x@-2 L2x@-1 P2 3b@-2 P3 L2b@-1 K.0
        VB.0 3d@-2 A.0 3w@-2 K.1 A.1 F.0@-1 F.1@-1 3f@-2 G.0@-1 VB.1 3g.0@-2 A.2 K.2 3h.0@-2 N.0@-1
        G.1@-1 F.2@-1 PV.0 VB.2 3v.0@-2 N.1@-1 K.3 F.3@-1 A.3 G.2@-1 G.3@-1 AT.0@-1 PV.1 AT.1@-1 N.2@-1
        3S.0@-2 N.3@-1 AV.0@-1 3g.1@-2 PV.2 AV.1@-1 VB.3 3h.1@-2 3v.1@-2 AT.2@-1 AT.3@-1 PV.3 P4 AV.2@-1
        AV.3@-1 3S.1@-2
    """,
    "pool": """
        P0 C1@-1 3a@-2 3x@-2 CS.0 L2a@-1 CS.1 CS.2 CS.3 ST.0 N.0@-1 N.1@-1 P4 3h.0@-2 ST.1 ST.2 3S.0@-2
        N.2@-1 N.3@-1 ST.3 3h.1@-2 3S.1@-2
    """,
}
AHEAD = 0
BEHIND = 3

def stage_of(kind):
    if kind[0] == "3":
        return "S3"
    if kind[0] == "P" and kind != "PV":
        return "P"
    return "S2" if kind in ("L2a", "L2x", "L2b", "F", "G", "N", "V", "T", "AT", "AV", "Y", "W") else "S1"


def parsed(order):
    out = []
    for word in order.split():
        body, _, off = word.partition("@")
        kind, *args = body.split(".")
        out.append((kind, tuple(int(x) for x in args), int(off or 0)))
    return out


ORDERS = {engine: parsed(order) for engine, order in ORDERS.items()}

LAST_READER = {
    "K": ("dve", "kl1"), "VB": ("dve", "vl"), "A": ("dve", "max"), "ST": ("act", "pf"), "PV": ("dve", "zx"),
    "C1": ("dve", "at"), "C2": ("dve", "alo"), "C3": ("dve", "x1"),
    "P1": ("dve", "xlo"), "P2": ("dve", "qnat"),
    "L2b": ("dve", "xlo"), "F": ("dve", "subm"), "V": ("act", "v"), "T": ("act", "feat"), "AT": ("dve", "mask"),
    "AV": ("dve", "y"), "Y": ("act", "yT"), "W": ("dve", "x2"),
    "3b": ("dve", "xlo"), "3c": ("act", "gelu"), "3d": ("dve", "lb"), "3e": ("act", "si"), "3f": ("dve", "ws"),
    "3g": ("dve", "rz"), "3h": ("dve", "u"), "3i": ("act", "as"), "3j": ("dve", "out"),
}


BANKS = """
    W:1 C2:3 P1:6 3j:2 C3:0 P2:6 3b:4 K.0:1 VB.0:3 L2b:6 3c:7 K.1:5 VB.1:4 3d:2 A.0:0 F.0:7 F.1:6 A.1:2
    ST.0:0 3e:5 ST.1:2 3f:1 K.2:0 VB.2:5 3g.0:1 A.2:6 V.0:2 3h.0:3 K.3:1 F.2:0 PV.0:4 T.0.0:3 ST.2:6 VB.3:3
    F.3:2 T.1.0:6 T.0.1:5 V.1:7 A.3:4 PV.1:0 T.1.1:1 3g.1:2 AT.0:7 AT.1:1 ST.3:4 AV.0:6 PV.2:7 T.2.0:1
    AV.1:0 T.3.0:4 T.2.1:5 T.3.1:6 3h.1:2 AT.2:1 AT.3:6 PV.3:0 Y.0:4 AV.2:2 AV.3:5 C1:3 Y.1:1 3i:6
"""
BANKS = {(word.split(":")[0]): int(word.split(":")[1]) for word in BANKS.split()}


def banks_of(kind, args):
    first = BANKS[".".join([kind, *(str(x) for x in args)])]
    return range(first, first + (2 if kind in ("A", "ST") else 1))


class Tile:

    def __init__(self, reg, off):
        self.reg, self.off = reg, off

    def times(self, n, plus=0):
        c = self.off * n + plus
        return c if self.reg is None else self.reg * n + c

    def shifted(self, by):
        return Tile(self.reg, self.off + by)

    def exists(self, tiles):
        return self.reg is not None or 0 <= self.off < tiles

    @property
    def first(self):
        return self.reg is None and self.off == 0


class Count(tuple):

    def __new__(cls, sem, value, rank):
        count = super().__new__(cls, (sem, value))
        count.rank = rank
        return count


class Progress:

    def __init__(self, sem, engine, stage):
        self.sem = sem
        items = sorted((i for i in ORDERS[engine] if stage_of(i[0]) == stage), key=lambda i: -i[2])
        self.names = [(name, *args) for kind, args, _ in items for name in STEPS[engine][kind]]
        self.index = {name: n + 1 for n, name in enumerate(self.names)}
        assert len(self.index) == len(self.names), self.names
        self.at = 0

    def step(self, *name):
        assert self.names[self.at % len(self.names)] == name, (self.names[self.at % len(self.names)], name)
        self.at += 1
        return self.sem, 1

    def after(self, tile, *name):
        return Count(self.sem, tile.times(len(self.names), self.index[name]),
                     tile.off * len(self.names) + self.index[name])


def bass_perceiver_layer(nc, a, tiles):
    ctx = ExitStack()
    with ctx:
        def sb(name, shape, dt=F32):
            return ctx.enter_context(nc.sbuf_tensor(name, shape, dt))

        def pb(name, cols):
            return ctx.enter_context(nc.psum_tensor(name, [P, cols], F32))

        def sem(name):
            return ctx.enter_context(nc.semaphore(name))

        def split(name, shape):
            return sb(name + "_hi", shape, F16), sb(name + "_lo", shape, F16)

        WQ, WK, WV, WO = (split(n, [P, KD, D]) for n in ("WQ", "WK", "WV", "WO"))
        FQ, FK, WV2 = (split(n, [P, KD, E2]) for n in ("FQ", "FK", "WV2"))
        W1 = split("W1", [P, KD, P])
        wo2 = sb("wo2", [P, E2 // P, D])
        w2 = sb("w2", [P, SLOTS])
        wih = sb("wih", [P, KD, 3 * D])
        gvo = sb("gvo", [P, KD, D])
        ident = sb("ident", [P, P])
        identb = sb("identb", [P, P], BF16)
        same_q = sb("same_q", [P, SQ])
        collapse = sb("collapse", [P, BT, P])
        mask8 = sb("mask8", [P, 8, SQ], F16)
        mask_o = sb("mask_o", [P, 4, DK])
        mask_c = sb("mask_c", [P, P])
        half = sb("half", [P, 1])
        bq4c = sb("bq4c", [P, KD])
        bkc = sb("bkc", [P, KD])
        bq4 = sb("bq4", [P, D])
        bk_row = sb("bk_row", [P, D])
        b_o1 = sb("b_o1", [P, D])
        b_o3 = sb("b_o3", [P, D])
        b2r = sb("b2r", [P, SLOTS])
        c_h = sb("c_h", [P, 1])
        tinv = sb("tinv", [P, 1])
        hs = sb("hs", [P, D])
        c_rz = sb("c_rz", [P, 2 * D])
        hn_half = sb("hn_half", [P, D])
        bihn = sb("bihn", [P, D])

        x_in = sb("x_in", [P, D])
        kv_last = sb("kv_last", [P, 2 * D])
        ctx_in = sb("ctx_in", [P, BT, KD, SK])
        st6 = sb("st6", [P, 3, 6])
        mv = sb("mv", [P, 3, 2])
        vareps = sb("vareps", [P, 3])
        rstd = sb("rstd", [P, 3])
        xn1 = sb("xn1", [P, D])
        x1T = split("x1T", [P, KD, P])
        qf = sb("qf", [P, 2, P])
        qs = split("qs", [P, 2, P])
        qnat = sb("qnat", [P, D])
        prod = sb("prod", [P, D])
        s_last = sb("s_last", [P, H])
        xres = sb("xres", [P, D])
        BD = split("BD", [P, 2, BT, 8, SQ])
        cs = split("cs", [P, 2, KD, SK])
        ks = split("ks", [P, 2, 2, SK])
        vs = split("vs", [P, BT, 2, NQ, DK * 4 + 1])
        nmax = sb("nmax", [P, BT, NQ], BF16)
        pf = sb("pf", [P, 2, 2, 512])
        ps = split("ps", [P, 2, 2, 512])
        om = sb("om", [P, BT, D + 2 * H])
        lk = sb("lk", [P, 8, H])
        lk2 = sb("lk2", [P, H])
        attn = sb("attn", [P, D])
        wv_l = sb("wv_l", [P, D])
        attT = split("attT", [P, KD, P])
        x1 = sb("x1", [P, D])
        xn2 = sb("xn2", [P, D])
        x2T = split("x2T", [P, KD, P])
        arg = sb("arg", [P, 4, 8, 2, HD])
        fmx = sb("fmx", [P, 4, 2, 8])
        fsum = sb("fsum", [P, 4, 2, 8, 2])
        featT = sb("featT", [P, 4, 2, 4, P])
        v1 = sb("v1", [P, H * (HD + 1) + 31])
        at_m = sb("at_m", [P, 2, 4, P])
        zr = sb("zr", [P, 4, 2, 4])
        y = sb("y", [P, E2])
        yT = sb("yT", [P, 8, P])
        x2 = sb("x2", [P, D])
        x2b = sb("x2b", [P, D])
        xn3 = sb("xn3", [P, D])
        x3T = split("x3T", [P, KD, P])
        hT = sb("hT", [P, P])
        lg = sb("lg", [P, 6, SLOTS])
        sc3 = sb("sc3", [P, 16])
        abd = sb("abd", [P, BT, SLOTS])
        siT = sb("siT", [P, KD, BT * SLOTS])
        aT = sb("aT", [P, 2, P])
        rw = sb("rw", [P, 2, 2])
        rz = sb("rz", [P, 2, 2 * D])
        gu = sb("gu", [P, 6, D])
        s_new = sb("s_new", [P, 2, D])
        asT = sb("asT", [P, KD, P])
        y_out = sb("y_out", [P, D])

        psum = pb("psum", 8 * BANK_F32)

        def bank(kind, *args):
            nums = banks_of(kind, args)
            return psum[:, nums[0] * BANK_F32:(nums[-1] + 1) * BANK_F32]

        b_k, b_v, b_a, b_s, b_o, b_x = (psum[:, lo * BANK_F32:hi * BANK_F32]
                                        for lo, hi in ((0, 1), (1, 2), (2, 4), (4, 6), (6, 7), (7, 8)))

        scratch = nc.dram_tensor("kv_last_scratch", (P, 2 * D), F32, kind="Internal").ap()

        STORED_BEHIND = -next(off for kind, _, off in ORDERS["dve"] if kind == "3j")

        w_kv32 = pf[:].rearrange("p a b c -> p (a b c)")
        w2q32 = arg[:].rearrange("p a b c d -> p (a b c d)")
        w2k32 = featT[:].rearrange("p a b c d -> p (a b c d)")
        kq32 = om[:].rearrange("p a b -> p (a b)")[:, 0:1024]
        kk32 = y[:]
        wv232 = ctx_in[:].rearrange("p a b c -> p (a b c)")
        w132 = yT[:].rearrange("p a b -> p (a b)")[:, 0:4 * P]
        whh32 = gu[:].rearrange("p a b -> p (a b)").rearrange("p (k n) -> p k n", k=KD)
        wv3 = rz[:, 0].rearrange("p (k n) -> p k n", k=KD)
        wo3 = rz[:, 1].rearrange("p (k n) -> p k n", k=KD)
        ctl = siT[:].rearrange("p a b -> p (a b)")[:, 0:KD * P]
        hsT = at_m[:].rearrange("p a b c -> p (a b c)")[:, 0:KD * P]
        small = sb("small", [P, 16])
        rows = [prod, wv_l, attn, xn2]
        bih_r = at_m[:].rearrange("p a b c -> p (a b c)")[:, 512:1024]
        bhh_r = yT[:].rearrange("p a b -> p (a b)")[:, 512:1024]
        kvl_sb = s_new[:].rearrange("p a b -> p (a b)")

        w_in = sem("weights_in")
        x_ld = sem("x_loaded")
        kv_ld = sem("kv_last_loaded")
        ctx_ld = [sem(f"ctx_loaded_{b}") for b in range(BT)]
        out_st = sem("out_stored")
        scr_st = sem("scratch_stored")
        prep = {e: sem(f"prep_{e}") for e in ("pe", "act", "dve", "pool")}

        passed = {e: sem(f"passed_waits_{e}") for e in ("pool", "dve")}

        at_of = {e: {s: Progress(sem(f"{e}_{s}"), e, s) for s in ("P", "S1", "S2", "S3")} for e in STEPS}
        pe_at, act_at, dve_at, pool_at = (at_of[e] for e in ("pe", "act", "dve", "pool"))

        def bank_read(item, turn):
            order = ORDERS["pe"]
            here = order.index(item)
            waits = {}
            for bank_no in banks_of(*item[:2]):
                for back in range(1, 2 * len(order)):
                    pos, turns_back = (here - back) % len(order), -((here - back) // len(order))
                    kind, args, off = order[pos]
                    t = turn.shifted(off - turns_back)
                    if bank_no in banks_of(kind, args) and t.exists(tiles):
                        waits[kind, args] = t
                        break
            return [at_of[LAST_READER[kind][0]][stage_of(kind)].after(t, LAST_READER[kind][1], *args)
                    for (kind, args), t in waits.items()]

        loads = [
            (w_kv32[:, 0:512].rearrange("p (k n) -> p k n", k=KD), a["xWk"]),
            (w_kv32[:, 512:1024].rearrange("p (k n) -> p k n", k=KD), a["xWv"]),
            (w_kv32[:, 1024:1536].rearrange("p (k n) -> p k n", k=KD), a["xWq"]),
            (w_kv32[:, 1536:2048].rearrange("p (k n) -> p k n", k=KD), a["xWo"]),
            (ctl.rearrange("p (k n) -> p k n", k=KD), a["ctx_last"]),
            (bk_row[:], a["xbk"].partition_broadcast(P)),
            (w2q32[0:HD].rearrange("p (h n) -> p h n", h=H), a["aWq"]),
            (w2k32[0:HD].rearrange("p (h n) -> p h n", h=H), a["aWk"]),
            (kq32[0:HD].rearrange("p (h n) -> p h n", h=H), a["aKq"]),
            (kk32[0:HD].rearrange("p (h n) -> p h n", h=H), a["aKk"]),
            (wv232.rearrange("p (k n) -> p k n", k=KD), a["aWv"]),
            (wo2[:], a["aWo"]),
            (w132.rearrange("p (k n) -> p k n", k=4), a["fw1"]),
            (w2[:], a["fw2"]),
            (wih[:], a["fwih"]),
            (whh32, a["fwhh"]),
            (wv3, a["fWv"]),
            (wo3, a["fWo"]),
            (hs[0:SLOTS], a["slot_init"]),
            (hs[SLOTS:P], a["slot_init"]),
            (small[:, 0:2], a["xbv"]),
            (small[:, 2:4], a["fbv"]),
            (small[:, 6:7], a["tau"].partition_broadcast(P)),
            (small[0:SLOTS, 7:8], a["slot_scale"]),
            (small[SLOTS:P, 7:8], a["slot_scale"]),
            (small[:, 8:10], a["xbq_col"]),
            (bkc[:], a["xbk_col"]),
            (small[:, 10:11], a["fb1"]),
            (rows[0][:], a["xbq"].partition_broadcast(P)),
            (rows[1][:], a["xbo"].partition_broadcast(P)),
            (rows[2][:], a["fbo"].partition_broadcast(P)),
            (rows[3][:], a["fbhh"][2 * D:3 * D].partition_broadcast(P)),
            (bih_r, a["fbih"][0:2 * D].partition_broadcast(P)),
            (bhh_r, a["fbhh"][0:2 * D].partition_broadcast(P)),
            (bihn[:], a["fbih"][2 * D:3 * D].partition_broadcast(P)),
            (b2r[:], a["fb2"].partition_broadcast(P)),
        ]
        ALL_LOADED = 16 * len(loads)
        POOL_PREP = 15
        PE_PREP = 5
        ACT_PREP = 11

        block = ctx.enter_context(nc.Block())

        def turns(engine, eng, run):
            def turn(n, reg=None):
                for item in ORDERS[engine]:
                    kind, args, off = item
                    t = Tile(reg, n + off)
                    if t.exists(tiles):
                        run(item, t)

            for n in range(-AHEAD, BEHIND + 1):
                turn(n)
            with eng.Fori(BEHIND + 1, tiles - AHEAD) as reg:
                turn(0, reg)
            for n in range(tiles - AHEAD, tiles + BEHIND):
                turn(n)

        @block.sync
        def _(sp):
            for dst, src in loads:
                sp.dma_start(dst, src).then_inc(w_in, 16)
            sp.wait_ge(prep["dve"], KVL_DONE)
            sp.dma_start(scratch, kvl_sb).then_inc(scr_st, 16)
            sp.wait_ge(scr_st, 16)

            def load_x(t):
                if not t.first:
                    sp.wait_ge(*dve_at["P"].after(t.shifted(-1), "xn"))
                    sp.wait_ge(*pool_at["P"].after(t.shifted(-1), "xres"))
                sp.dma_start(x_in[:], a["x"][t.times(1)]).then_inc(x_ld, 16)

            def load_kv(t):
                if not t.first:
                    sp.wait_ge(*pool_at["S1"].after(t.shifted(-1), "wv"))
                for b in range(BT):
                    sp.dma_start(kv_last[SQ * b:SQ * (b + 1), :],
                                 scratch[t.times(BT, b)].partition_broadcast(SQ)).then_inc(kv_ld, 16)

            def load_ctx(t, b):
                if not t.first:
                    sp.wait_ge(*pool_at["S1"].after(t.shifted(-1), "clo", b))
                sp.dma_start(ctx_in[:, b, :, :], a["ctx"][t.times(BT, b)]).then_inc(ctx_ld[b], 16)

            def store(t):
                sp.wait_ge(*dve_at["S3"].after(t, "out"))
                sp.dma_start(a["out"][t.times(1)], y_out[:]).then_inc(out_st, 16)

            first = Tile(None, 0)
            sp.wait_ge(prep["act"], ACT_PREP)
            sp.wait_ge(prep["dve"], DVE_PREP)
            load_x(first)
            for b in range(BT):
                load_ctx(first, b)
            load_kv(first)
            load_x(Tile(None, 1))

            def turn(t):
                if t.shifted(-STORED_BEHIND).exists(tiles):
                    store(t.shifted(-STORED_BEHIND))
                if t.shifted(1).exists(tiles):
                    for b in range(BT):
                        load_ctx(t.shifted(1), b)
                    load_kv(t.shifted(1))
                if t.shifted(2).exists(tiles):
                    load_x(t.shifted(2))

            peeled = STORED_BEHIND + 1
            for n in range(peeled):
                turn(Tile(None, n))
            with sp.Fori(peeled, tiles - 2) as reg:
                turn(Tile(reg, 0))
            for n in range(tiles - 2, tiles + STORED_BEHIND):
                turn(Tile(None, n))
            sp.wait_ge(out_st, 16 * tiles)

        @block.gpsimd
        def _(pool):
            g = nc.gpsimd

            def before():
                n = [0]

                def link(ins):
                    n[0] += 1
                    ins.then_inc(prep["pool"], 1)
                    pool.wait_ge(prep["pool"], n[0])

                link(g.memset(ident[:], 0.0))
                link(g.affine_select(out=ident[:], in_=ident[:], compare_op=ALU.not_equal, fill=1.0, base=0,
                                     pattern=[[-1, P]], channel_multiplier=1))
                link(g.tensor_copy(identb[:], ident[:]))
                link(g.memset(mask8[:], 1.0))
                link(g.affine_select(out=mask8[:], in_=mask8[:], compare_op=ALU.is_ge, fill=0.0, base=0,
                                     pattern=[[-DK, 8], [0, SQ]], channel_multiplier=1))
                link(g.affine_select(out=mask8[:], in_=mask8[:], compare_op=ALU.is_ge, fill=0.0, base=DK - 1,
                                     pattern=[[DK, 8], [0, SQ]], channel_multiplier=-1))
                link(g.memset(mask_o[:], 1.0))
                link(g.affine_select(out=mask_o[:], in_=mask_o[:], compare_op=ALU.is_ge, fill=0.0, base=0,
                                     pattern=[[-SQ, 4], [0, DK]], channel_multiplier=1))
                link(g.affine_select(out=mask_o[:], in_=mask_o[:], compare_op=ALU.is_ge, fill=0.0, base=SQ - 1,
                                     pattern=[[SQ, 4], [0, DK]], channel_multiplier=-1))
                mc = mask_c[:].rearrange("p (c r) -> p c r", c=4)
                link(g.memset(mask_c[:], 1.0))
                link(g.affine_select(out=mc, in_=mc, compare_op=ALU.is_ge, fill=0.0, base=0,
                                     pattern=[[-SQ, 4], [0, SQ]], channel_multiplier=1))
                link(g.affine_select(out=mc, in_=mc, compare_op=ALU.is_ge, fill=0.0, base=0,
                                     pattern=[[SQ, 4], [1, SQ]], channel_multiplier=-1))
                link(g.memset(collapse[:], 0.0))
                link(g.memset(half[:], -0.5))
                link(g.memset(v1[:], 1.0))
                assert n[0] == POOL_PREP

            def apart(*waits):
                for sm, val in waits:
                    pool.wait_ge(sm, val)
                pool.sem_inc(passed["pool"], 1)

            def power(stage, t, name, n):
                pool.wait_ge(*dve_at[stage].after(t, "eps"))
                g.tensor_tensor(rstd[:, n:n + 1], vareps[:, n:n + 1], half[:], ALU.pow)\
                 .then_inc(*pool_at[stage].step(name))

            def run(item, t):
                kind, arg_, off = item
                stage = stage_of(kind)
                prev = t.shifted(-1)
                if kind == "P0":
                    power("P", t, "rstd", 0)
                elif kind == "L2a":
                    power("S2", t, "rstd", 1)
                elif kind == "P4":
                    pool.wait_ge(x_ld, t.times(16, 16))
                    if not t.first:
                        pool.wait_ge(*dve_at["S1"].after(prev, "x1"))
                    g.tensor_tensor(xres[:], x_in[:], b_o1[:], ALU.add).then_inc(*pool_at["P"].step("xres"))
                    pool.wait_ge(kv_ld, t.times(64, 64))
                    pool.wait_ge(*dve_at["P"].after(t, "qnat"))
                    g.tensor_tensor(prod[:], qnat[:], kv_last[:, 0:D], ALU.mult)\
                     .then_inc(*pool_at["P"].step("prod"))
                elif kind == "CS":
                    b, = arg_
                    pool.wait_ge(*act_at["S1"].after(t, "chi", b))
                    g.tensor_tensor(cs[1][:, b % 2], ctx_in[:, b], cs[0][:, b % 2], ALU.subtract)\
                     .then_inc(*pool_at["S1"].step("clo", b))
                elif kind == "ST":
                    b, = arg_
                    pool.wait_ge(*act_at["S1"].after(t, "pf", b))
                    if b >= 2:
                        pool.wait_ge(*pe_at["S1"].after(t, "PV", b - 2))
                    elif not t.first:
                        pool.wait_ge(*pe_at["S1"].after(prev, "PV", b + 2))
                    g.tensor_tensor(ps[1][:, b % 2], pf[:, b % 2], ps[0][:, b % 2], ALU.subtract)\
                     .then_inc(*pool_at["S1"].step("plo", b))
                elif kind == "C1":
                    pool.wait_ge(*dve_at["S1"].after(t, "ea"))
                    g.tensor_tensor(wv_l[:].rearrange("p (h d) -> p h d", h=H),
                                    kv_last[:, D:2 * D].rearrange("p (h d) -> p h d", h=H),
                                    lk2[:].unsqueeze(2).to_broadcast([P, H, DK]), ALU.mult)\
                     .then_inc(*pool_at["S1"].step("wv"))
                elif kind == "N":
                    c, = arg_
                    pool.wait_ge(*dve_at["S2"].after(t, "rs", c))
                    f = arg[:, c].rearrange("p h s f -> p (h s) f")
                    g.tensor_tensor(f, f, fsum[:, c, 1].rearrange("p h s -> p (h s)").unsqueeze(2)
                                    .to_broadcast([P, 16, HD]), ALU.mult).then_inc(*pool_at["S2"].step("norm", c))
                elif kind == "3a":
                    pool.wait_ge(*dve_at["S2"].after(t, "x2"))
                    if not t.first:
                        pool.wait_ge(*dve_at["S3"].after(prev, "out"))
                    g.tensor_tensor(x2b[:], x2[:], b_o3[:], ALU.add).then_inc(*pool_at["S3"].step("x2b"))
                elif kind == "3x":
                    power("S3", t, "rstd", 2)
                elif kind == "3h":
                    n, = arg_
                    pool.wait_ge(*dve_at["S3"].after(t, "v", n))
                    g.tensor_tensor(gu[:, 2], gu[:, 0], gu[:, 1], ALU.add).then_inc(*pool_at["S3"].step("w", n))
                elif kind == "3S":
                    n, = arg_
                    pool.wait_ge(*act_at["S3"].after(t, "n", n))
                    g.tensor_tensor(gu[:, 4], hs[:], gu[:, 3], ALU.subtract).then_inc(*pool_at["S3"].step("d", n))

            before()
            turns("pool", pool, run)

        @block.scalar
        def _(act):
            s = nc.scalar

            def before():
                n = [0]

                def done(ins):
                    n[0] += 1
                    ins.then_inc(prep["act"], 1)

                act.wait_ge(w_in, ALL_LOADED)
                kv4 = w_kv32.rearrange("p (w k n) -> p w k n", w=4, k=KD)
                for i, w in enumerate((WK, WV, WQ, WO)):
                    done(s.copy(w[0][:], kv4[:, i]))
                done(s.copy(WV2[0][:], wv232.rearrange("p (k n) -> p k n", k=KD)))
                done(s.copy(W1[0][:], w132.rearrange("p (k n) -> p k n", k=4)[:, 0:KD]))
                done(s.mul(bq4c[:], small[:, 8:10], 0.25))
                done(s.mul(bq4[:], rows[0][:], 0.25))
                act.wait_ge(prep["pe"], 1)
                for w, b0, b1 in ((FQ, b_k, b_v),):
                    done(s.copy(w[0][:, 0, 0:512], b0[:]))
                    done(s.copy(w[0][:, 0, 512:1024], b1[:]))
                done(s.copy(FQ[0][:, 1, :], b_a[:]))
                assert n[0] == ACT_PREP, n[0]

            def run(item, t):
                kind, arg_, off = item
                stage = stage_of(kind)
                prev = t.shifted(-1)
                if kind in ("P1", "L2b", "3b"):
                    xT = {"P1": x1T, "L2b": x2T, "3b": x3T}[kind]
                    act.wait_ge(*pe_at[stage].after(t, "xT"))
                    s.copy(xT[0][:].rearrange("p k n -> p (k n)"), bank(kind, *arg_)[:, 0:D])\
                     .then_inc(*act_at[stage].step("xhi"))
                elif kind == "P2":
                    act.wait_ge(*pe_at["P"].after(t, "q"))
                    if not t.first:
                        act.wait_ge(*dve_at["P"].after(prev, "qlo"))
                    for n in range(2):
                        s.activation(qf[:, n], bank("P2")[:, n * P:(n + 1) * P], ACT.Identity, bias=bq4c[:, n:n + 1],
                                     scale=0.25).then_inc(*act_at["P"].step(f"qf{n}"))
                    act.wait_ge(*act_at["P"].after(t, "qf1"))
                    if not t.first:
                        act.wait_ge(*dve_at["P"].after(prev, "bdhi"))
                    s.copy(qs[0][:], qf[:]).then_inc(*act_at["P"].step("qhi"))
                elif kind == "CS":
                    b, = arg_
                    act.wait_ge(ctx_ld[b], t.times(16, 16))
                    if b >= 2:
                        act.wait_ge(*pe_at["S1"].after(t, "v", b - 2))
                    elif not t.first:
                        act.wait_ge(*pe_at["S1"].after(prev, "v", b + 2))
                    s.copy(cs[0][:, b % 2], ctx_in[:, b]).then_inc(*act_at["S1"].step("chi", b))
                elif kind == "K":
                    b, = arg_
                    act.wait_ge(*pe_at["S1"].after(t, "kT", b))
                    if b >= 2:
                        act.wait_ge(*pe_at["S1"].after(t, "ST", b - 2))
                    elif not t.first:
                        act.wait_ge(*pe_at["S1"].after(prev, "ST", b + 2))
                    for n in range(2):
                        s.activation(ks[0][:, b % 2, n], bank("K", b)[:, n * SK:(n + 1) * SK], ACT.Identity,
                                     bias=bkc[:, n:n + 1]).then_inc(*act_at["S1"].step(f"kh{n}", b))
                elif kind == "VB":
                    b, = arg_
                    act.wait_ge(*pe_at["S1"].after(t, "v", b))
                    if not t.first:
                        act.wait_ge(*pe_at["S1"].after(prev, "PV", b))
                    s.copy(vs[0][:, b, :, :, 0:4 * DK].rearrange("p k j d -> p (k j) d"),
                           bank("VB", b).rearrange("p (k d) -> p k d", d=4 * DK))\
                     .then_inc(*act_at["S1"].step("vh", b))
                elif kind == "ST":
                    b, = arg_
                    act.wait_ge(*pe_at["S1"].after(t, "ST", b))
                    if b >= 2:
                        act.wait_ge(*pool_at["S1"].after(t, "plo", b - 2))
                        act.wait_ge(*pe_at["S1"].after(t, "PV", b - 2))
                    elif not t.first:
                        act.wait_ge(*pool_at["S1"].after(prev, "plo", b + 2))
                        act.wait_ge(*pe_at["S1"].after(prev, "PV", b + 2))
                    s.activation(ps[0][:, b % 2].rearrange("p k n -> p (k n)"), bank("ST", b), ACT.Exp)\
                     .then_inc(*act_at["S1"].step("ph", b))
                    s.activation(pf[:, b % 2].rearrange("p k n -> p (k n)"), bank("ST", b), ACT.Exp)\
                     .then_inc(*act_at["S1"].step("pf", b))
                elif kind == "C1":
                    act.wait_ge(*dve_at["S1"].after(t, "te"))
                    s.activation(lk[:, 3:5, :].rearrange("p a b -> p (a b)"),
                                 lk[:, 1:3, :].rearrange("p a b -> p (a b)"), ACT.Exp)\
                     .then_inc(*act_at["S1"].step("ae"))
                elif kind == "C2":
                    act.wait_ge(*pe_at["S1"].after(t, "aT"))
                    s.copy(attT[0][:].rearrange("p k n -> p (k n)"), bank("C2")[:, 0:D])\
                     .then_inc(*act_at["S1"].step("ahi"))
                elif kind == "F":
                    c, = arg_
                    act.wait_ge(*dve_at["S2"].after(t, "subm", c))
                    f = arg[:, c].rearrange("p h s f -> p (h s f)")
                    s.activation(f, f, ACT.Exp).then_inc(*act_at["S2"].step("exp", c))
                elif kind == "V":
                    n, = arg_
                    act.wait_ge(*pe_at["S2"].after(t, "v", n))
                    if not t.first:
                        act.wait_ge(*pe_at["S2"].after(prev, "AV", 2 * n + 1))
                    w = (HD + 1) * 8
                    s.copy(v1[:, n * w:(n + 1) * w].rearrange("p (h d) -> p h d", h=8)[:, :, 0:HD],
                           bank("V", n).rearrange("p (h d) -> p h d", h=8))\
                     .then_inc(*act_at["S2"].step("v", n))
                elif kind == "T":
                    c, i = arg_
                    act.wait_ge(*pe_at["S2"].after(t, "T", c, i))
                    if not t.first:
                        act.wait_ge(*pe_at["S2"].after(prev, "AT", c // 2 * 2 + i))
                    s.copy(featT[:, c, i].rearrange("p h n -> p (h n)"), bank("T", c, i))\
                     .then_inc(*act_at["S2"].step("feat", c, i))
                elif kind == "Y":
                    n, = arg_
                    act.wait_ge(*pe_at["S2"].after(t, "Y", n))
                    if not t.first and n == 0:
                        act.wait_ge(*pe_at["S2"].after(prev, "W"))
                    s.copy(yT[:, 4 * n:4 * n + 4].rearrange("p h n -> p (h n)"), bank("Y", n))\
                     .then_inc(*act_at["S2"].step("yT", n))
                elif kind == "3c":
                    act.wait_ge(*pe_at["S3"].after(t, "h"))
                    s.activation(hT[:], bank(kind, *arg_)[:, 0:P], ACT.Gelu, bias=c_h[:, 0:1])\
                     .then_inc(*act_at["S3"].step("gelu"))
                elif kind == "3d":
                    act.wait_ge(*dve_at["S3"].after(t, "nmax"))
                    s.activation(lg[:, 4], lg[:, 1], ACT.Exp, bias=sc3[:, 8:9]).then_inc(*act_at["S3"].step("e"))
                elif kind == "3e":
                    act.wait_ge(*pe_at["S3"].after(t, "si"))
                    s.copy(siT[:].rearrange("p k n -> p (k n)"), bank(kind, *arg_)).then_inc(*act_at["S3"].step("si"))
                elif kind == "3f":
                    act.wait_ge(*pe_at["S3"].after(t, "aT"))
                    s.copy(aT[:].rearrange("p k n -> p (k n)"), bank(kind, *arg_)[:, 0:2 * P]).then_inc(*act_at["S3"].step("aT"))
                elif kind == "3g":
                    n, = arg_
                    act.wait_ge(*dve_at["S3"].after(t, "rz", n))
                    s.activation(rz[:, n], rz[:, n], ACT.Tanh, scale=0.5).then_inc(*act_at["S3"].step("tanh", n))
                elif kind == "3h":
                    n, = arg_
                    act.wait_ge(*pool_at["S3"].after(t, "w", n))
                    s.activation(gu[:, 3], gu[:, 2], ACT.Tanh).then_inc(*act_at["S3"].step("n", n))
                elif kind == "3i":
                    act.wait_ge(*pe_at["S3"].after(t, "as"))
                    s.copy(asT[:].rearrange("p k n -> p (k n)"), bank(kind, *arg_)[:, 0:D]).then_inc(*act_at["S3"].step("as"))

            before()
            turns("act", act, run)

        @block.vector
        def _(dve):
            v = nc.vector

            def before():
                n = [0]

                def link(ins):
                    n[0] += 1
                    ins.then_inc(prep["dve"], 1)
                    dve.wait_ge(prep["dve"], n[0])

                dve.wait_ge(w_in, ALL_LOADED)
                dve.wait_ge(prep["pool"], POOL_PREP)
                link(v.tensor_scalar(hs[:], hs[:], small[:, 7:8], None, ALU.mult))
                assert n[0] == 1
                dve.wait_ge(prep["pe"], 2)
                link(v.tensor_tensor(kvl_sb[:, 0:D], b_s[:, 0:D], bk_row[:], ALU.add))
                link(v.tensor_copy(kvl_sb[:, D:2 * D], b_s[:, D:2 * D]))
                assert n[0] == KVL_DONE
                link(v.tensor_copy(hsT, b_s[:, 512:512 + D]))
                link(v.tensor_tensor(b_o1[:], b_o[:, 0:D], rows[1][:], ALU.add))
                link(v.tensor_tensor(b_o3[:], b_o[:, D:2 * D], rows[2][:], ALU.add))
                link(v.tensor_reduce(small[:, 4:6], hsT.rearrange("p (k n) -> p k n", k=KD)[:, :, 0:SLOTS], AX.X,
                                     ALU.add))
                link(v.tensor_scalar(small[:, 4:6], small[:, 4:6], 1.0 / SLOTS, None, ALU.mult))
                assert n[0] == MEAN_DONE
                dve.wait_ge(prep["act"], ACT_PREP)
                kv4 = w_kv32.rearrange("p (w k n) -> p w k n", w=4, k=KD)
                for i, w in enumerate((WK, WV, WQ, WO)):
                    link(v.tensor_tensor(w[1][:], kv4[:, i], w[0][:], ALU.subtract))
                link(v.tensor_tensor(WV2[1][:], wv232.rearrange("p (k n) -> p k n", k=KD), WV2[0][:], ALU.subtract))
                link(v.tensor_tensor(W1[1][:], w132.rearrange("p (k n) -> p k n", k=4)[:, 0:KD], W1[0][:],
                                     ALU.subtract))
                link(v.tensor_tensor(FQ[1][:, 0, 0:512], b_k[:], FQ[0][:, 0, 0:512], ALU.subtract))
                link(v.tensor_tensor(FQ[1][:, 0, 512:1024], b_v[:], FQ[0][:, 0, 512:1024], ALU.subtract))
                link(v.tensor_tensor(FQ[1][:, 1], b_a[:], FQ[0][:, 1], ALU.subtract))
                link(v.memset(vs[0][:, :, :, :, 4 * DK:4 * DK + 1], 1.0))
                link(v.memset(vs[1][:, :, :, :, 4 * DK:4 * DK + 1], 0.0))
                assert n[0] == FQ_DONE
                dve.wait_ge(prep["pe"], 3)
                link(v.tensor_copy(FK[0][:, 0, 0:512], b_k[:]))
                link(v.tensor_copy(FK[0][:, 0, 512:1024], b_v[:]))
                link(v.tensor_copy(FK[0][:, 1], b_a[:]))
                link(v.tensor_tensor(FK[1][:, 0, 0:512], b_k[:], FK[0][:, 0, 0:512], ALU.subtract))
                link(v.tensor_tensor(FK[1][:, 0, 512:1024], b_v[:], FK[0][:, 0, 512:1024], ALU.subtract))
                link(v.tensor_tensor(FK[1][:, 1], b_a[:], FK[0][:, 1], ALU.subtract))
                dve.wait_ge(prep["pe"], 4)
                link(v.tensor_tensor(c_h[:], b_x[:, 0:1], small[:, 10:11], ALU.add))
                link(v.tensor_tensor(c_rz[:], b_s[:, 0:512], bih_r, ALU.add))
                link(v.tensor_tensor(c_rz[:], c_rz[:], bhh_r, ALU.add))
                link(v.tensor_tensor(hn_half[:], b_s[:, 512:768], rows[3][:], ALU.add))
                link(v.tensor_scalar(hn_half[:], hn_half[:], 0.5, None, ALU.mult))
                link(v.tensor_copy(gvo[:].rearrange("p k n -> p (k n)"), b_o[:]))
                link(v.tensor_scalar(small[:, 11:12], small[:, 6:7], -1.0, None, ALU.mult))
                link(v.tensor_tensor(small[:, 12:13], small[:, 6:7], small[:, 11:12], ALU.max))
                link(v.tensor_scalar(small[:, 13:14], small[:, 12:13], 0.1, None, ALU.add))
                link(v.reciprocal(tinv[:], small[:, 13:14]))
                link(v.tensor_reduce(same_q[:], ident[:].rearrange("p (h r) -> p r h", h=4), AX.X, ALU.add))
                for b in range(BT):
                    link(v.tensor_copy(collapse[:, b, SQ * b:SQ * (b + 1)], same_q[:]))
                assert n[0] == DVE_PREP, n[0]

            def apart(*waits):
                for sm, val in waits:
                    dve.wait_ge(sm, val)
                dve.sem_inc(passed["dve"], 1)

            def norm_stats(stage, t, src, n):
                v.bn_stats(st6[:, n, :], src).then_inc(*dve_at[stage].step("stats"))
                apart(dve_at[stage].after(t, "stats"))
                v.bn_aggr(mv[:, n, :], st6[:, n, :]).then_inc(*dve_at[stage].step("aggr"))
                dve.wait_ge(*dve_at[stage].after(t, "aggr"))
                v.tensor_scalar(vareps[:, n:n + 1], mv[:, n, 1:2], LN_EPS, None, ALU.add)\
                 .then_inc(*dve_at[stage].step("eps"))

            def normed(stage, t, src, dst, n):
                dve.wait_ge(*pool_at[stage].after(t, "rstd"))
                v.tensor_scalar(dst, src, mv[:, n, 0:1], rstd[:, n:n + 1], ALU.subtract, ALU.mult)\
                 .then_inc(*dve_at[stage].step("xn"))

            def run(item, t):
                kind, arg_, off = item
                stage = stage_of(kind)
                prev = t.shifted(-1)
                if kind == "P0":
                    dve.wait_ge(x_ld, t.times(16, 16))
                    norm_stats("P", t, x_in[:], 0)
                elif kind == "P0x":
                    if not t.first:
                        dve.wait_ge(*pe_at["P"].after(prev, "xT"))
                    normed("P", t, x_in[:], xn1[:], 0)
                elif kind == "L2a":
                    dve.wait_ge(*dve_at["S1"].after(t, "x1"))
                    norm_stats("S2", t, x1[:], 1)
                elif kind == "L2x":
                    normed("S2", t, x1[:], xn2[:], 1)
                elif kind == "3a":
                    dve.wait_ge(*dve_at["S2"].after(t, "x2"))
                    norm_stats("S3", t, x2[:], 2)
                elif kind == "3x":
                    if not t.first:
                        dve.wait_ge(*pe_at["S3"].after(prev, "si"))
                    normed("S3", t, x2[:], xn3[:], 2)
                elif kind in ("P1", "L2b", "3b"):
                    xT = {"P1": x1T, "L2b": x2T, "3b": x3T}[kind]
                    dve.wait_ge(*act_at[stage].after(t, "xhi"))
                    v.tensor_tensor(xT[1][:].rearrange("p k n -> p (k n)"), bank(kind, *arg_)[:, 0:D],
                                    xT[0][:].rearrange("p k n -> p (k n)"), ALU.subtract)\
                     .then_inc(*dve_at[stage].step("xlo"))
                elif kind == "P2":
                    dve.wait_ge(*act_at["P"].after(t, "qhi"))
                    if not t.first:
                        dve.wait_ge(*pool_at["P"].after(prev, "prod"))
                    v.scalar_tensor_tensor(qnat[:], bank("P2")[:, 256:512], 0.25, bq4[:], ALU.mult, ALU.add)\
                     .then_inc(*dve_at["P"].step("qnat"))
                    v.tensor_tensor(qs[1][:], qf[:], qs[0][:], ALU.subtract).then_inc(*dve_at["P"].step("qlo"))
                elif kind == "P3":
                    dve.wait_ge(*dve_at["P"].after(t, "qlo"))
                    if not t.first:
                        dve.wait_ge(*pe_at["S1"].after(prev, "ST", BT - 1))
                    for n, name in ((0, "bdhi"), (1, "bdlo")):
                        q4 = qs[n][:].rearrange("p g (b q) -> p (g b) q", b=BT)
                        v.tensor_tensor(BD[n][:].rearrange("p g b h q -> p (g b) h q"),
                                        q4.unsqueeze(2).to_broadcast([P, 2 * BT, 8, SQ]),
                                        mask8[:].unsqueeze(1).to_broadcast([P, 2 * BT, 8, SQ]), ALU.mult)\
                         .then_inc(*dve_at["P"].step(name))
                elif kind == "P4":
                    dve.wait_ge(*pool_at["P"].after(t, "prod"))
                    v.tensor_reduce(s_last[:], prod[:].rearrange("p (h d) -> p h d", h=H), AX.X, ALU.add)\
                     .then_inc(*dve_at["P"].step("slast"))
                elif kind == "K":
                    b, = arg_
                    dve.wait_ge(*act_at["S1"].after(t, "kh1", b))
                    for n in range(2):
                        v.scalar_tensor_tensor(ks[1][:, b % 2, n], bank("K", b)[:, n * SK:(n + 1) * SK], bkc[:, n:n + 1],
                                               ks[0][:, b % 2, n], ALU.add, ALU.subtract)\
                         .then_inc(*dve_at["S1"].step(f"kl{n}", b))
                elif kind == "VB":
                    b, = arg_
                    dve.wait_ge(*act_at["S1"].after(t, "vh", b))
                    v.tensor_tensor(vs[1][:, b, :, :, 0:4 * DK].rearrange("p k j d -> p (k j) d"),
                                    bank("VB", b).rearrange("p (k d) -> p k d", d=4 * DK),
                                    vs[0][:, b, :, :, 0:4 * DK].rearrange("p k j d -> p (k j) d"), ALU.subtract)\
                     .then_inc(*dve_at["S1"].step("vl", b))
                elif kind == "A":
                    b, = arg_
                    dve.wait_ge(*pe_at["S1"].after(t, "A", b))
                    if not t.first:
                        dve.wait_ge(*pe_at["S1"].after(prev, "ST", b))
                    v.tensor_reduce(nmax[:, b, :], bank("A", b).rearrange("p (j n) -> p j n", j=NQ), AX.X, ALU.max,
                                    negate=True).then_inc(*dve_at["S1"].step("max", b))
                elif kind == "PV":
                    b, = arg_
                    dve.wait_ge(*pe_at["S1"].after(t, "PV", b))
                    if not t.first:
                        dve.wait_ge(*pe_at["S1"].after(prev, "X"))
                    o4 = bank("PV", b)[:, 0:NQ * 65].rearrange("p (j d) -> p j d", j=NQ)
                    mo = mask_o[:].rearrange("p a b -> p (a b)")
                    v.tensor_tensor(om[:, b, 0:D].rearrange("p (j d) -> p j d", j=NQ), o4[:, :, 0:64],
                                    mo.unsqueeze(1).to_broadcast([P, NQ, 64]), ALU.mult)\
                     .then_inc(*dve_at["S1"].step("om", b))
                    m4 = mask_o[:, :, 0].unsqueeze(1).to_broadcast([P, NQ, 4])
                    v.tensor_tensor(om[:, b, D:D + H].rearrange("p (j h) -> p j h", j=NQ),
                                    o4[:, :, 64:65].to_broadcast([P, NQ, 4]), m4, ALU.mult)\
                     .then_inc(*dve_at["S1"].step("zx", b))
                    v.tensor_tensor(om[:, b, D + H:D + 2 * H].rearrange("p (j h) -> p j h", j=NQ),
                                    nmax[:, b, :].unsqueeze(2).to_broadcast([P, NQ, 4]), m4, ALU.mult)\
                     .then_inc(*dve_at["S1"].step("mx", b))
                elif kind == "C1":
                    dve.wait_ge(*pe_at["S1"].after(t, "X"))
                    dve.wait_ge(*dve_at["P"].after(t, "slast"))
                    at = dve_at["S1"]
                    v.tensor_tensor(lk[:, 0], bank("C1")[:, D + H:D + 2 * H], s_last[:], ALU.add).then_inc(*at.step("d"))
                    dve.wait_ge(*at.after(t, "d"))
                    v.tensor_scalar(lk[:, 1], lk[:, 0], -1.0, 0.0, ALU.mult, ALU.min).then_inc(*at.step("ta"))
                    v.tensor_scalar(lk[:, 2], lk[:, 0], 0.0, None, ALU.min).then_inc(*at.step("te"))
                elif kind == "C1e":
                    at = dve_at["S1"]
                    dve.wait_ge(*act_at["S1"].after(t, "ae"))
                    v.tensor_tensor(lk[:, 5], bank("C1")[:, D:D + H], lk[:, 3], ALU.mult).then_inc(*at.step("za"))
                    dve.wait_ge(*at.after(t, "za"))
                    v.tensor_tensor(lk[:, 6], lk[:, 5], lk[:, 4], ALU.add).then_inc(*at.step("zt"))
                    dve.wait_ge(*at.after(t, "zt"))
                    v.reciprocal(lk[:, 7], lk[:, 6]).then_inc(*at.step("rz"))
                    dve.wait_ge(*at.after(t, "rz"))
                    v.tensor_tensor(lk2[:], lk[:, 4], lk[:, 7], ALU.mult).then_inc(*at.step("ea"))
                    v.scalar_tensor_tensor(lk[:, 5], lk[:, 3], 1.0, lk[:, 7], ALU.mult, ALU.mult)\
                     .then_inc(*at.step("at0"))
                    dve.wait_ge(*at.after(t, "at0"))
                    v.tensor_tensor(attn[:].rearrange("p (h d) -> p h d", h=H),
                                    bank("C1")[:, 0:D].rearrange("p (h d) -> p h d", h=H),
                                    lk[:, 5].unsqueeze(2).to_broadcast([P, H, DK]), ALU.mult)\
                     .then_inc(*at.step("at"))
                elif kind == "C2":
                    dve.wait_ge(*act_at["S1"].after(t, "ahi"))
                    v.tensor_tensor(attT[1][:].rearrange("p k n -> p (k n)"), bank("C2")[:, 0:D],
                                    attT[0][:].rearrange("p k n -> p (k n)"), ALU.subtract)\
                     .then_inc(*dve_at["S1"].step("alo"))
                elif kind == "C3":
                    dve.wait_ge(*pe_at["S1"].after(t, "o"))
                    v.tensor_tensor(x1[:], bank("C3")[:, 0:D], xres[:], ALU.add).then_inc(*dve_at["S1"].step("x1"))
                elif kind == "F":
                    c, = arg_
                    at = dve_at["S2"]
                    dve.wait_ge(*pe_at["S2"].after(t, "f", c))
                    if not t.first:
                        dve.wait_ge(*pe_at["S2"].after(prev, "T", c, 1))
                    f = bank("F", c).rearrange("p (h f) -> p h f", h=8)
                    v.tensor_reduce(fmx[:, c, 0], f, AX.X, ALU.max).then_inc(*at.step("max", c))
                    v.tensor_reduce(fmx[:, c, 1], f, AX.X, ALU.min).then_inc(*at.step("min", c))
                    dve.wait_ge(*at.after(t, "max", c))
                    v.tensor_tensor(arg[:, c, :, 0, :], f, fmx[:, c, 0].unsqueeze(2).to_broadcast([P, 8, HD]),
                                    ALU.subtract).then_inc(*at.step("subp", c))
                    dve.wait_ge(*at.after(t, "min", c))
                    v.scalar_tensor_tensor(arg[:, c, :, 1, :], f, -1.0,
                                           fmx[:, c, 1].unsqueeze(2).to_broadcast([P, 8, HD]),
                                           ALU.mult, ALU.add).then_inc(*at.step("subm", c))
                elif kind == "G":
                    c, = arg_
                    at = dve_at["S2"]
                    dve.wait_ge(*act_at["S2"].after(t, "exp", c))
                    v.tensor_reduce(fsum[:, c, 0].rearrange("p h s -> p (h s)"),
                                    arg[:, c].rearrange("p h s f -> p (h s) f"), AX.X, ALU.add)\
                     .then_inc(*at.step("sum", c))
                    dve.wait_ge(*at.after(t, "sum", c))
                    v.reciprocal(fsum[:, c, 1], fsum[:, c, 0]).then_inc(*at.step("rs", c))
                elif kind == "N":
                    c, = arg_
                    at = dve_at["S2"]
                    dve.wait_ge(*pool_at["S2"].after(t, "norm", c))
                    fl = arg[:, c].rearrange("p h s f -> p (h s f)")
                    v.tensor_scalar(fl, fl, FEAT_EPS, None, ALU.max).then_inc(*at.step("clamp", c))
                elif kind == "AT":
                    g4, = arg_
                    dve.wait_ge(*pe_at["S2"].after(t, "AT", g4))
                    if g4 >= 2:
                        dve.wait_ge(*pe_at["S2"].after(t, "AV", g4 - 2))
                    elif not t.first:
                        dve.wait_ge(*pe_at["S2"].after(prev, "AV", g4 + 2))
                    v.tensor_tensor(at_m[:, g4 % 2],
                                    bank("AT", g4).rearrange("p (h n) -> p h n", h=4),
                                    mask_c[:].unsqueeze(1).to_broadcast([P, 4, P]), ALU.mult)\
                     .then_inc(*dve_at["S2"].step("mask", g4))
                elif kind == "AV":
                    g4, = arg_
                    at = dve_at["S2"]
                    dve.wait_ge(*pe_at["S2"].after(t, "AV", g4))
                    if not t.first:
                        dve.wait_ge(*pe_at["S2"].after(prev, "Y", g4 // 2))
                    o = bank("AV", g4)[:, 0:384].rearrange("p (h d) -> p h d", h=4)
                    v.tensor_scalar(zr[:, g4, 0], o[:, :, HD], FEAT_EPS, None, ALU.add).then_inc(*at.step("z", g4))
                    dve.wait_ge(*at.after(t, "z", g4))
                    v.reciprocal(zr[:, g4, 1], zr[:, g4, 0]).then_inc(*at.step("rz", g4))
                    dve.wait_ge(*at.after(t, "rz", g4))
                    v.tensor_tensor(y[:, g4 * 256:(g4 + 1) * 256].rearrange("p (h d) -> p h d", h=4), o[:, :, 0:HD],
                                    zr[:, g4, 1].unsqueeze(2).to_broadcast([P, 4, HD]), ALU.mult)\
                     .then_inc(*at.step("y", g4))
                elif kind == "W":
                    dve.wait_ge(*pe_at["S2"].after(t, "W"))
                    if not t.first:
                        dve.wait_ge(*pool_at["S3"].after(prev, "x2b"))
                    v.tensor_tensor(x2[:], bank("W")[:, 0:D], x1[:], ALU.add).then_inc(*dve_at["S2"].step("x2"))
                elif kind == "3d":
                    at = dve_at["S3"]
                    dve.wait_ge(*pe_at["S3"].after(t, "lg"))
                    v.tensor_tensor(lg[:, 0], bank(kind, *arg_)[:, 0:SLOTS], b2r[:], ALU.add).then_inc(*at.step("lb"))
                    dve.wait_ge(*at.after(t, "lb"))
                    v.tensor_scalar(lg[:, 1], lg[:, 0], tinv[:, 0:1], None, ALU.mult).then_inc(*at.step("lg"))
                    apart(at.after(t, "lg"))
                    v.max(sc3[:, 0:8], lg[:, 1]).then_inc(*at.step("top"))
                    apart(at.after(t, "top"))
                    v.match_replace(lg[:, 2], sc3[:, 0:8], lg[:, 1], NEG).then_inc(*at.step("repl"))
                    dve.wait_ge(*at.after(t, "repl"))
                    v.tensor_tensor(lg[:, 3], lg[:, 2], lg[:, 1], ALU.not_equal).then_inc(*at.step("sel"))
                    v.tensor_scalar(sc3[:, 8:9], sc3[:, 0:1], -1.0, None, ALU.mult).then_inc(*at.step("nmax"))
                elif kind == "3w":
                    at = dve_at["S3"]
                    dve.wait_ge(*act_at["S3"].after(t, "e"))
                    dve.wait_ge(*at.after(t, "sel"))
                    v.scalar_tensor_tensor(lg[:, 5], lg[:, 4], 1.0, lg[:, 3], ALU.mult, ALU.mult,
                                           accum_out=sc3[:, 9:10]).then_inc(*at.step("ea"))
                    dve.wait_ge(*at.after(t, "ea"))
                    v.reciprocal(sc3[:, 10:11], sc3[:, 9:10]).then_inc(*at.step("rs"))
                    dve.wait_ge(*at.after(t, "rs"))
                    v.tensor_scalar(lg[:, 0], lg[:, 5], sc3[:, 10:11], None, ALU.mult).then_inc(*at.step("al"))
                    dve.wait_ge(*at.after(t, "al"))
                    if not t.first:
                        dve.wait_ge(*pe_at["S3"].after(prev, "aT"))
                    v.tensor_tensor(abd[:], lg[:, 0].unsqueeze(1).to_broadcast([P, BT, SLOTS]),
                                    mask_o[:, :, 0].unsqueeze(2).to_broadcast([P, BT, SLOTS]), ALU.mult)\
                     .then_inc(*at.step("abd"))
                elif kind == "3f":
                    at = dve_at["S3"]
                    dve.wait_ge(*act_at["S3"].after(t, "aT"))
                    v.tensor_scalar(rw[:, 0], bank(kind, *arg_)[:, 2 * P:2 * P + 2], WSUM_EPS, None, ALU.add)\
                     .then_inc(*at.step("ws"))
                    dve.wait_ge(*at.after(t, "ws"))
                    v.reciprocal(rw[:, 1], rw[:, 0]).then_inc(*at.step("rw"))
                elif kind == "3g":
                    n, = arg_
                    dve.wait_ge(*pe_at["S3"].after(t, "rz", n))
                    if n == 0:
                        dve.wait_ge(*dve_at["S3"].after(t, "rw"))
                    v.scalar_tensor_tensor(rz[:, n], bank(kind, *arg_), rw[:, 1, n:n + 1], c_rz[:], ALU.mult, ALU.add)\
                     .then_inc(*dve_at["S3"].step("rz", n))
                elif kind == "3h":
                    n, = arg_
                    at = dve_at["S3"]
                    dve.wait_ge(*pe_at["S3"].after(t, "n", n))
                    if n == 1:
                        dve.wait_ge(*pool_at["S3"].after(t, "w", 0))
                    v.scalar_tensor_tensor(gu[:, 0], bank(kind, *arg_)[:, 0:D], rw[:, 1, n:n + 1], bihn[:], ALU.mult, ALU.add)\
                     .then_inc(*at.step("u", n))
                elif kind == "3v":
                    n, = arg_
                    at = dve_at["S3"]
                    dve.wait_ge(*act_at["S3"].after(t, "tanh", n))
                    v.scalar_tensor_tensor(gu[:, 1], rz[:, n, 0:D], 1.0, hn_half[:], ALU.add, ALU.mult)\
                     .then_inc(*at.step("v", n))
                elif kind == "3S":
                    n, = arg_
                    at = dve_at["S3"]
                    dve.wait_ge(*pool_at["S3"].after(t, "d", n))
                    v.scalar_tensor_tensor(gu[:, 5], rz[:, n, D:2 * D], 1.0, gu[:, 4], ALU.add, ALU.mult)\
                     .then_inc(*at.step("q", n))
                    dve.wait_ge(*at.after(t, "q", n))
                    v.scalar_tensor_tensor(s_new[:, n], gu[:, 5], 0.5, gu[:, 3], ALU.mult, ALU.add)\
                     .then_inc(*at.step("S", n))
                elif kind == "3j":
                    dve.wait_ge(*pe_at["S3"].after(t, "y"))
                    if not t.first:
                        dve.wait_ge(out_st, t.times(16, 0))
                    v.tensor_tensor(y_out[:], bank(kind, *arg_)[:, 0:D], x2b[:], ALU.add).then_inc(*dve_at["S3"].step("out"))

            before()
            turns("dve", dve, run)

        @block.tensor
        def _(pe):
            def mm(out, lhsT, rhs, start, stop):
                return pe.matmul(out, lhsT, rhs, start=start, stop=stop, skip_group_check=True)

            def split_product(out, terms, start=True, stop=True):
                last = None
                for n, (lh, ll, rh, rl) in enumerate(terms):
                    end = stop and n == len(terms) - 1
                    mm(out, lh, rh, start and n == 0, False)
                    mm(out, lh, rl, False, False)
                    last = mm(out, ll, rh, False, end)
                return last

            def before():
                pe.wait_ge(w_in, ALL_LOADED)
                pe.wait_ge(prep["pool"], POOL_PREP)

                def features(w32, k32):
                    wv = w32[0:HD].rearrange("p (h n) -> p h n", h=H)
                    kv = k32[0:HD].rearrange("p (h n) -> p h n", h=H)
                    for h in range(H):
                        for k in range(KD):
                            bank = [(b_k, b_v)[h // 8][:], b_a[:, h // 8 * 512:h // 8 * 512 + 512]][k]
                            last = mm(bank[:, h % 8 * HD:(h % 8 + 1) * HD], wv[:, h, k * P:(k + 1) * P], kv[:, h, :],
                                      True, True)
                    return last

                features(w2q32, kq32).then_inc(prep["pe"], 1)
                kv4 = w_kv32.rearrange("p (w k n) -> p w k n", w=4, k=KD)
                cl = ctl.rearrange("p (k n) -> p k n", k=KD)
                for w in range(2):
                    for k in range(KD):
                        mm(b_s[:, w * D:(w + 1) * D], cl[:, k, :], kv4[:, w, k, :], k == 0, k == KD - 1)
                for w, wo in ((0, kv4[:, 3]), (1, wo3)):
                    for k in range(KD):
                        mm(b_o[:, w * D:(w + 1) * D], small[:, 2 * w + k:2 * w + k + 1].to_broadcast([P, P]),
                           wo[:, k, :], k == 0, k == KD - 1)
                pe.wait_ge(prep["dve"], 1)
                for k in range(KD):
                    last = pe.transpose(b_s[:, 512 + k * P:512 + (k + 1) * P], hs[:, k * P:(k + 1) * P], ident[:])
                last.then_inc(prep["pe"], 1)
                pe.wait_ge(prep["dve"], FQ_DONE)
                features(w2k32, kk32).then_inc(prep["pe"], 1)
                hT_ = hsT.rearrange("p (k n) -> p k n", k=KD)
                w1_ = w132.rearrange("p (k n) -> p k n", k=4)
                for k in range(KD):
                    mm(b_x[:, 0:1], w1_[:, KD + k, :], small[:, 4 + k:5 + k], k == 0, k == KD - 1)
                for lo, n in ((0, 512), (512, 256)):
                    for k in range(KD):
                        mm(b_s[:, lo:lo + n], hT_[:, k, :], whh32[:, k, lo:lo + n], k == 0, k == KD - 1)
                for m in range(KD):
                    for k in range(KD):
                        last = mm(b_o[:, m * D:(m + 1) * D], wv3[:, k, m * P:(m + 1) * P], wo3[:, k, :], k == 0,
                                  k == KD - 1)
                last.then_inc(prep["pe"], 1)
                pe.wait_ge(prep["dve"], DVE_PREP)

            def wait_all(*needs):
                for n, need in enumerate(needs):
                    same = [(other.rank, m) for m, other in enumerate(needs) if other[0] is need[0]]
                    if max(same)[1] == n:
                        pe.wait_ge(*need)

            def transposed(stage, t, src, out):
                for k in range(KD):
                    last = pe.transpose(out[:, k * P:(k + 1) * P], src[:, k * P:(k + 1) * P], ident[:])
                last.then_inc(*pe_at[stage].step("xT"))

            def run(item, t):
                kind, arg_, off = item
                stage = stage_of(kind)
                out = bank(kind, *arg_)
                bank_free = bank_read(item, t.shifted(-off))
                if kind == "P1":
                    wait_all(*bank_free, dve_at["P"].after(t, "xn"))
                    transposed("P", t, xn1, out)
                elif kind == "L2b":
                    wait_all(*bank_free, dve_at["S2"].after(t, "xn"))
                    transposed("S2", t, xn2, out)
                elif kind == "3b":
                    wait_all(*bank_free, dve_at["S3"].after(t, "xn"))
                    transposed("S3", t, xn3, out)
                elif kind == "P2":
                    wait_all(*bank_free, dve_at["P"].after(t, "xlo"))
                    for g in range(2):
                        split_product(out[:, g * P:(g + 1) * P],
                                      [(WQ[0][:, k, g * P:(g + 1) * P], WQ[1][:, k, g * P:(g + 1) * P],
                                        x1T[0][:, k], x1T[1][:, k]) for k in range(KD)])
                    split_product(out[:, D:2 * D],
                                  [(x1T[0][:, k], x1T[1][:, k], WQ[0][:, k], WQ[1][:, k]) for k in range(KD)])\
                        .then_inc(*pe_at["P"].step("q"))
                elif kind == "K":
                    b, = arg_
                    wait_all(*bank_free, pool_at["S1"].after(t, "clo", b))
                    c = [cs[n][:, b % 2] for n in range(2)]
                    for g in range(2):
                        last = split_product(out[:, g * SK:(g + 1) * SK],
                                             [(WK[0][:, k, g * P:(g + 1) * P], WK[1][:, k, g * P:(g + 1) * P],
                                               c[0][:, k], c[1][:, k]) for k in range(KD)])
                    last.then_inc(*pe_at["S1"].step("kT", b))
                elif kind == "VB":
                    b, = arg_
                    wait_all(*bank_free, pool_at["S1"].after(t, "clo", b))
                    c = [cs[n][:, b % 2] for n in range(2)]
                    for m in range(2):
                        last = split_product(out[:, m * D:(m + 1) * D],
                                             [(c[0][:, k, m * P:(m + 1) * P], c[1][:, k, m * P:(m + 1) * P],
                                               WV[0][:, k], WV[1][:, k]) for k in range(KD)])
                    last.then_inc(*pe_at["S1"].step("v", b))
                elif kind == "A":
                    b, = arg_
                    queries = [dve_at["P"].after(t, "bdlo")] if b == 0 else []
                    wait_all(*bank_free, *queries, act_at["S1"].after(t, "kh1", b))
                    for j in range(NQ):
                        q = BD[0][:, j // 2, b].rearrange("p h q -> p (h q)")[:, j % 2 * P:(j % 2 + 1) * P]
                        last = mm(out[:, j * SK:(j + 1) * SK], q, ks[0][:, b % 2, j // 2], True, True)
                    last.then_inc(*pe_at["S1"].step("A", b))
                elif kind == "ST":
                    b, = arg_
                    wait_all(*bank_free, dve_at["S1"].after(t, "kl1", b))
                    for m in range(2):
                        for g in range(2):
                            k = [ks[n][:, b % 2, g, m * P:(m + 1) * P] for n in range(2)]
                            q = [BD[n][:, g, b].rearrange("p h q -> p (h q)") for n in range(2)]
                            split_product(out[:, m * 512 + g * 256:m * 512 + (g + 1) * 256],
                                          [(k[0], k[1], q[0], q[1])], start=(g == 0), stop=False)
                    pe.wait_ge(*dve_at["S1"].after(t, "max", b))
                    for m in range(2):
                        for j in range(NQ):
                            last = mm(out[:, m * 512 + j * P:m * 512 + (j + 1) * P],
                                      nmax[:, b, j:j + 1].to_broadcast([P, P]), identb[:], False, True)
                    last.then_inc(*pe_at["S1"].step("ST", b))
                elif kind == "PV":
                    b, = arg_
                    wait_all(*bank_free, pool_at["S1"].after(t, "plo", b), dve_at["S1"].after(t, "vl", b))
                    for j in range(NQ):
                        p = [[ps[n][:, b % 2, m, j * P:(j + 1) * P] for n in range(2)] for m in range(2)]
                        w = [[vs[n][:, b, m, j, :] for n in range(2)] for m in range(2)]
                        last = split_product(out[:, j * 65:(j + 1) * 65],
                                             [(p[m][0], p[m][1], w[m][0], w[m][1]) for m in range(2)])
                    last.then_inc(*pe_at["S1"].step("PV", b))
                elif kind == "C1":
                    wait_all(*bank_free, dve_at["S1"].after(t, "mx", BT - 1))
                    for b in range(BT):
                        last = mm(out[:, 0:D + 2 * H], collapse[:, b], om[:, b], b == 0, b == BT - 1)
                    last.then_inc(*pe_at["S1"].step("X"))
                elif kind == "C2":
                    wait_all(*bank_free, dve_at["S1"].after(t, "at"), pool_at["S1"].after(t, "wv"))
                    for k in range(KD):
                        mm(out[:, k * P:(k + 1) * P], attn[:, k * P:(k + 1) * P], ident[:], True, False)
                        last = mm(out[:, k * P:(k + 1) * P], wv_l[:, k * P:(k + 1) * P], ident[:], False, True)
                    last.then_inc(*pe_at["S1"].step("aT"))
                elif kind == "C3":
                    wait_all(*bank_free, dve_at["S1"].after(t, "alo"))
                    split_product(out[:, 0:D],
                                  [(attT[0][:, k], attT[1][:, k], WO[0][:, k], WO[1][:, k]) for k in range(KD)])\
                        .then_inc(*pe_at["S1"].step("o"))
                elif kind == "F":
                    c, = arg_
                    wait_all(*bank_free, dve_at["S2"].after(t, "xlo"))
                    w, lo = (FQ, FK)[c % 2], c // 2 * 512
                    split_product(out,
                                  [(x2T[0][:, k], x2T[1][:, k], w[0][:, k, lo:lo + 512], w[1][:, k, lo:lo + 512])
                                   for k in range(KD)]).then_inc(*pe_at["S2"].step("f", c))
                elif kind == "V":
                    n, = arg_
                    wait_all(*bank_free, dve_at["S2"].after(t, "xlo"))
                    split_product(out,
                                  [(x2T[0][:, k], x2T[1][:, k], WV2[0][:, k, n * 512:(n + 1) * 512],
                                    WV2[1][:, k, n * 512:(n + 1) * 512]) for k in range(KD)])\
                        .then_inc(*pe_at["S2"].step("v", n))
                elif kind == "T":
                    c, i = arg_
                    wait_all(*bank_free, dve_at["S2"].after(t, "clamp", c))
                    for h in range(4):
                        last = pe.transpose(out[:, h * P:(h + 1) * P], arg[:, c, 4 * i + h].rearrange("p s f -> p (s f)"), ident[:])
                    last.then_inc(*pe_at["S2"].step("T", c, i))
                elif kind == "AT":
                    g4, = arg_
                    c, i = g4 // 2 * 2, g4 % 2
                    wait_all(*bank_free, act_at["S2"].after(t, "feat", c, i), act_at["S2"].after(t, "feat", c + 1, i))
                    for h in range(4):
                        last = mm(out[:, h * P:(h + 1) * P], featT[:, c + 1, i, h],
                                  featT[:, c, i, h], True, True)
                    last.then_inc(*pe_at["S2"].step("AT", g4))
                elif kind == "AV":
                    g4, = arg_
                    wait_all(*bank_free, dve_at["S2"].after(t, "mask", g4),
                             act_at["S2"].after(t, "v", min(1, (g4 + 1) // 2)))
                    for h in range(4):
                        lo = (4 * g4 + h) * (HD + 1)
                        last = mm(out[:, h * 96:(h + 1) * 96], at_m[:, g4 % 2, h], v1[:, lo:lo + 96], True, True)
                    last.then_inc(*pe_at["S2"].step("AV", g4))
                elif kind == "Y":
                    n, = arg_
                    wait_all(*bank_free, dve_at["S2"].after(t, "y", 2 * n + 1))
                    for h in range(4):
                        last = pe.transpose(out[:, h * P:(h + 1) * P],
                                            y[:, (4 * n + h) * P:(4 * n + h + 1) * P], ident[:])
                    last.then_inc(*pe_at["S2"].step("Y", n))
                elif kind == "W":
                    wait_all(*bank_free, act_at["S2"].after(t, "yT", 1))
                    for k in range(8):
                        last = mm(out[:, 0:D], yT[:, k], wo2[:, k], k == 0, k == 7)
                    last.then_inc(*pe_at["S2"].step("W"))
                elif kind == "3c":
                    wait_all(*bank_free, dve_at["S3"].after(t, "xlo"))
                    split_product(out[:, 0:P],
                                  [(W1[0][:, k], W1[1][:, k], x3T[0][:, k], x3T[1][:, k]) for k in range(KD)])\
                        .then_inc(*pe_at["S3"].step("h"))
                elif kind == "3d":
                    wait_all(*bank_free, act_at["S3"].after(t, "gelu"))
                    mm(out[:, 0:SLOTS], hT[:], w2[:], True, True).then_inc(*pe_at["S3"].step("lg"))
                elif kind == "3e":
                    wait_all(*bank_free, dve_at["S3"].after(t, "abd"))
                    for k in range(KD):
                        last = mm(out[:, k * D:(k + 1) * D], xn3[:, k * P:(k + 1) * P],
                                  abd[:].rearrange("p b s -> p (b s)"), True, True)
                    last.then_inc(*pe_at["S3"].step("si"))
                elif kind == "3f":
                    wait_all(*bank_free, act_at["S3"].after(t, "si"))
                    ab = abd[:].rearrange("p b s -> p (b s)")
                    for n in range(2):
                        pe.transpose(out[:, n * P:(n + 1) * P], ab[:, n * P:(n + 1) * P], ident[:])
                    for n in range(2):
                        last = mm(out[:, 2 * P + n:2 * P + n + 1], ab[:, n * P:(n + 1) * P], v1[:, HD:HD + 1], True,
                                  True)
                    last.then_inc(*pe_at["S3"].step("aT"))
                elif kind == "3g":
                    n, = arg_
                    wait_all(*bank_free, act_at["S3"].after(t, "si"))
                    for k in range(KD):
                        last = mm(out, siT[:, k, n * P:(n + 1) * P], wih[:, k, 0:2 * D], k == 0, k == KD - 1)
                    last.then_inc(*pe_at["S3"].step("rz", n))
                elif kind == "3h":
                    n, = arg_
                    wait_all(*bank_free, dve_at["S3"].after(t, "rz", n))
                    for k in range(KD):
                        last = mm(out[:, 0:D], siT[:, k, n * P:(n + 1) * P], wih[:, k, 2 * D:3 * D], k == 0,
                                  k == KD - 1)
                    last.then_inc(*pe_at["S3"].step("n", n))
                elif kind == "3i":
                    wait_all(*bank_free, dve_at["S3"].after(t, "S", 1))
                    for k in range(KD):
                        for n in range(2):
                            last = mm(out[:, k * P:(k + 1) * P], s_new[:, n, k * P:(k + 1) * P], aT[:, n], n == 0,
                                      n == 1)
                    last.then_inc(*pe_at["S3"].step("as"))
                elif kind == "3j":
                    wait_all(*bank_free, act_at["S3"].after(t, "as"))
                    for k in range(KD):
                        last = mm(out[:, 0:D], asT[:, k], gvo[:, k], k == 0, k == KD - 1)
                    last.then_inc(*pe_at["S3"].step("y"))

            before()
            turns("pe", pe, run)


KVL_DONE = 3
MEAN_DONE = 8
FQ_DONE = 19
DVE_PREP = 40


def kernel(_tiles=None, **inputs):
    import numpy as _np
    import concourse.bacc as _bacc
    from concourse import mybir as _mybir
    from concourse.bass_utils import run_bass_kernel_spmd as _run

    i = {k: _np.asarray(v) for k, v in inputs.items()}
    n_b = i["x"].shape[0]
    all_tiles = n_b // BT
    tiles = _tiles or all_tiles

    def chunks(w):
        return _np.ascontiguousarray(w.reshape(-1, P, w.shape[1]).transpose(1, 0, 2))

    def column(b):
        return _np.ascontiguousarray(b.reshape(-1, P).T)

    def heads(w):
        return _np.ascontiguousarray(w.reshape(D, H, HD).transpose(2, 1, 0))

    c = i["ctx_1024"]
    arrays = {
        "x": i["x"].reshape(all_tiles, P, D),
        "ctx": _np.ascontiguousarray(c[:, :SK].reshape(n_b, SK, KD, P).transpose(0, 3, 2, 1)),
        "ctx_last": _np.ascontiguousarray(c[:, SK].reshape(n_b, KD, P).transpose(2, 1, 0)),
        "xWq": chunks(i["L0_xattn_Wq"].T), "xWk": chunks(i["L0_xattn_Wk"].T), "xWv": chunks(i["L0_xattn_Wv"].T),
        "xWo": chunks(i["L0_xattn_Wo"].T),
        "xbq": i["L0_xattn_bq"], "xbk": i["L0_xattn_bk"], "xbo": i["L0_xattn_bo"],
        "xbv": column(i["L0_xattn_bv"]), "xbq_col": column(i["L0_xattn_bq"]), "xbk_col": column(i["L0_xattn_bk"]),
        "aWq": heads(i["L0_attn_Wq"]), "aWk": heads(i["L0_attn_Wk"]), "aWv": chunks(i["L0_attn_Wv"]),
        "aWo": chunks(i["L0_attn_Wo"]),
        "aKq": _np.ascontiguousarray(i["L0_attn_Kq"].transpose(1, 0, 2)),
        "aKk": _np.ascontiguousarray(i["L0_attn_Kk"].transpose(1, 0, 2)),
        "slot_init": i["L0_ffn_slot_init"], "slot_scale": i["L0_ffn_slot_scale"],
        "fw1": chunks(i["L0_ffn_w1"].T), "fb1": column(i["L0_ffn_b1"]),
        "fw2": _np.ascontiguousarray(i["L0_ffn_w2"].T), "fb2": i["L0_ffn_b2"],
        "fwih": chunks(i["L0_ffn_gru_wih"].T), "fwhh": chunks(i["L0_ffn_gru_whh"].T),
        "fbih": i["L0_ffn_gru_bih"], "fbhh": i["L0_ffn_gru_bhh"],
        "fWv": chunks(i["L0_ffn_wv"]), "fbv": column(i["L0_ffn_bv"]),
        "fWo": chunks(i["L0_ffn_wo"].T), "fbo": i["L0_ffn_bo"], "tau": i["L0_ffn_tau"],
    }
    nc = _bacc.Bacc("TRN2", target_bir_lowering=False, num_devices=1)
    sent, aps = {}, {}
    for name, v in arrays.items():
        v = _np.ascontiguousarray(v)
        sent[f"in_{name}"] = v
        aps[name] = nc.dram_tensor(f"in_{name}", v.shape, _mybir.dt.from_np(v.dtype), kind="ExternalInput").ap()
    aps["out"] = nc.dram_tensor("out_0", (all_tiles, P, D), F32, kind="ExternalOutput").ap()
    bass_perceiver_layer(nc, aps, tiles)
    r = _run(nc, [sent], core_ids=[0])
    return r.results[0]["out_0"].reshape(n_b, SQ, D)
```

```python
from contextlib import ExitStack

import concourse.bass as bass
from concourse import mybir

F32 = mybir.dt.float32
F16 = mybir.dt.float16
BF16 = mybir.dt.bfloat16
ALU = mybir.AluOpType
ACT = mybir.ActivationFunctionType
AX = mybir.AxisListType

P = 128
D = 256
KD = D // P
BT = 4
SQ = 32
SK = 256
H = 16
DK = D // H
HD = 64
E2 = H * HD
NQ = 4
SLOTS = 64
BANK_F32 = 512
NEG = -3.0e38
LN_EPS = 1e-5
FEAT_EPS = 1e-12
WSUM_EPS = 1e-8

STEPS = {
    "pe": {
        "P1": ["xT"], "P2": ["q"], "P4": ["qn"],
        "K": ["kT"], "VB": ["v"], "A": ["A"], "ST": ["ST"], "PV": ["PV"], "C1": ["X"], "C2": ["aT"], "C3": ["o"],
        "L2b": ["xT"], "F": ["f"], "V": ["v"], "T": ["T"], "AT": ["AT"], "AV": ["AV"], "Y": ["Y"], "W": ["W"],
        "3b": ["xT"], "3c": ["h"], "3d": ["lg"], "3s": ["ws"], "3e": ["si"], "3f": ["aT"], "3g": ["rz"], "3h": ["n"],
        "3i": ["as"], "3j": ["y"],
    },
    "act": {
        "P1": ["xhi"], "P2": ["qf0", "qf1", "qhi"],
        "CS": ["chi"], "K": ["kh0", "kh1"], "VB": ["vh"], "ST": ["ph", "pf"], "PV": ["ohi"],
        "C1": ["ae"], "C2": ["ahi"],
        "L2b": ["xhi"], "F": ["expm", "expp"], "V": ["v"], "T": ["feat"], "Y": ["yhi"],
        "3b": ["xhi"], "3c": ["gelu"], "3d": ["e"], "3e": ["sihi"], "3f": ["aT"], "3g": ["tanh"], "3h": ["n"],
        "3i": ["as"],
    },
    "dve": {
        "P0": ["stats", "aggr", "eps"], "P0x": ["xn"], "P1": ["xlo"],
        "P3": ["bdhi"], "P4": ["prod", "slast"],
        "K": ["kl0", "kl1"], "VB": ["vl"], "A": ["max"], "PV": ["om", "zx", "mx"],
        "C1": ["d", "ta", "te"], "C1e": ["za", "zt", "rz", "ea", "at0", "at"], "C2": ["alo"], "C3": ["x1"],
        "L2a": ["stats", "aggr", "eps"], "L2x": ["xn"], "L2b": ["xlo"],
        "F": ["max", "min", "subp"], "G": ["sum", "rs"], "N": ["clamp"], "AT": ["mask"],
        "AV": ["z", "rz", "y"], "Y": ["ylo"], "W": ["x2"],
        "3a": ["stats", "aggr", "eps"], "3x": ["xn"], "3b": ["xlo"],
        "3d": ["lb", "lg", "top", "repl", "sel", "nmax"], "3w": ["ea", "rs", "al", "abd"],
        "3s": ["ws", "rw", "an", "abn"], "3e": ["silo"],
        "3g": ["rz"], "3h": ["u"], "3S": ["q", "S"], "3j": ["out"],
    },
    "pool": {
        "P0": ["rstd"], "P2": ["qlo"], "P3": ["bdlo"], "P4": ["xres"],
        "CS": ["clo"], "ST": ["plo"], "PV": ["olo"], "C1": ["wv"], "C1e": ["sum"],
        "L2a": ["rstd"], "N": ["norm"],
        "3a": ["x2b"], "3x": ["rstd"], "3h": ["v", "w"], "3S": ["d"],
    },
}
ORDERS = {
    "pe": """
        PV.1@-1 T.0.1@-2 T.1.1@-2 3d@-3 AT.0@-2 ST.3@-1 AT.1@-2 T.2.0@-2 AV.0@-2 PV.2@-1 T.3.0@-2
        T.2.1@-2 3s@-3 T.3.1@-2 AT.2@-2 AV.1@-2 AT.3@-2 PV.3@-1 P1 AV.2@-2 AV.3@-2 3e@-3 3f@-3 C1@-1 P2
        Y.0@-2 Y.1@-2 3g.0@-3 3h.0@-3 3g.1@-3 C2@-1 W@-2 C3@-1 K.0 VB.0 A.0 L2b@-1 K.1 F.0@-1 VB.1
        3h.1@-3 A.1 F.1@-1 V.0@-1 F.2@-1 ST.0 3i@-3 K.2 P4 3j@-3 ST.1 F.3@-1 K.3 A.2 VB.2 3b@-2 T.0.0@-1
        PV.0 ST.2 A.3 T.1.0@-1 VB.3 3c@-2 V.1@-1
    """,
    "act": """
        ST.2@-1 T.1.0@-2 3c@-3 V.1@-2 T.0.1@-2 VB.3@-1 T.1.1@-2 PV.0@-1 3d@-3 ST.3@-1 T.2.0@-2 T.3.0@-2
        T.2.1@-2 PV.1@-1 T.3.1@-2 PV.2@-1 P1 PV.3@-1 3e@-3 3f@-3 C1@-1 Y.0@-2 Y.1@-2 3g.0@-3 P2 C2@-1
        CS.0 3h.0@-3 CS.1 K.0 VB.0 L2b@-1 K.1 3g.1@-3 CS.2 VB.1 CS.3 F.0@-1 3h.1@-3 V.0@-1 F.1@-1 3i@-3
        ST.0 K.2 F.2@-1 ST.1 K.3 VB.2 3b@-2 T.0.0@-1 F.3@-1
    """,
    "dve": """
        A.3@-1 G.2@-2 G.3@-2 P0 PV.1@-1 N.2@-2 3d@-3 VB.3@-1 AT.0@-2 N.3@-2 AT.1@-2 3w@-3 P0x AV.0@-2
        3s@-3 AT.2@-2 PV.2@-1 AT.3@-2 PV.3@-1 P1 AV.1@-2 AV.2@-2 AV.3@-2 C1@-1 3e@-3 C1e@-1 Y.0@-2
        3g.0@-3 Y.1@-2 3h.0@-3 C2@-1 P3 W@-2 C3@-1 L2a@-1 3S.0@-3 L2x@-1 K.0 3g.1@-3 L2b@-1 VB.0 A.0
        F.0@-1 K.1 3h.1@-3 VB.1 F.1@-1 G.0@-1 3S.1@-3 F.2@-1 A.1 G.1@-1 3j@-3 3a@-2 N.0@-1 P4 3x@-2 K.2
        F.3@-1 A.2 VB.2 PV.0 N.1@-1 3b@-2 K.3
    """,
    "pool": """
        ST.1@-1 N.2@-2 N.3@-2 ST.2@-1 P0 PV.0@-1 ST.3@-1 PV.1@-1 PV.2@-1 PV.3@-1 C1@-1 C1e@-1 3h.0@-3
        CS.0 3S.0@-3 CS.1 L2a@-1 P2 P3 CS.2 3h.1@-3 3S.1@-3 P4 N.0@-1 CS.3 3a@-2 3x@-2 ST.0 N.1@-1
    """,
}
AHEAD = 0
BEHIND = 3

def stage_of(kind):
    if kind[0] == "3":
        return "S3"
    if kind[0] == "P" and kind != "PV":
        return "P"
    return "S2" if kind in ("L2a", "L2x", "L2b", "F", "G", "N", "V", "T", "AT", "AV", "Y", "W") else "S1"


def parsed(order):
    out = []
    for word in order.split():
        body, _, off = word.partition("@")
        kind, *args = body.split(".")
        out.append((kind, tuple(int(x) for x in args), int(off or 0)))
    return out


ORDERS = {engine: parsed(order) for engine, order in ORDERS.items()}

LAST_READER = {
    "K": ("dve", "kl1"), "VB": ("dve", "vl"), "A": ("dve", "max"), "ST": ("act", "pf"), "PV": ("dve", "zx"),
    "C1": ("dve", "at"), "C2": ("dve", "alo"), "C3": ("dve", "x1"),
    "P1": ("dve", "xlo"), "P2": ("act", "qf1"), "P4": ("dve", "prod"),
    "L2b": ("dve", "xlo"), "F": ("act", "expm"), "V": ("act", "v"), "T": ("act", "feat"), "AT": ("dve", "mask"),
    "AV": ("dve", "y"), "Y": ("dve", "ylo"), "W": ("dve", "x2"),
    "3b": ("dve", "xlo"), "3c": ("act", "gelu"), "3d": ("dve", "lb"), "3s": ("dve", "ws"), "3e": ("dve", "silo"),
    "3f": ("act", "aT"),
    "3g": ("dve", "rz"), "3h": ("dve", "u"), "3i": ("act", "as"), "3j": ("dve", "out"),
}


BANKS = """
    PV.1:7 T.0.1:3 T.1.1:6 3d:5 AT.0:1 ST.3:3 AT.1:2 T.2.0:0 AV.0:6 PV.2:7 T.3.0:2 T.2.1:1 3s:3 T.3.1:4
    AT.2:0 AV.1:3 AT.3:1 PV.3:6 P1:2 AV.2:7 AV.3:4 3e:6 3f:0 C1:1 P2:0 Y.0:5 Y.1:3 3g.0:7 3h.0:6 3g.1:2 C2:1
    W:3 C3:6 K.0:0 VB.0:7 A.0:5 L2b:1 K.1:3 F.0:2 VB.1:4 3h.1:1 A.1:5 F.1:7 V.0:3 F.2:4 ST.0:1 3i:3 K.2:7
    P4:3 3j:0 ST.1:5 F.3:0 K.3:2 A.2:3 VB.2:7 3b:1 T.0.0:6 PV.0:5 ST.2:3 A.3:6 T.1.0:1 VB.3:0 3c:5 V.1:2
"""
BANKS = {(word.split(":")[0]): int(word.split(":")[1]) for word in BANKS.split()}


def banks_of(kind, args):
    first = BANKS[".".join([kind, *(str(x) for x in args)])]
    return range(first, first + (2 if kind in ("A", "ST") else 1))


class Tile:

    def __init__(self, reg, off):
        self.reg, self.off = reg, off

    def times(self, n, plus=0):
        c = self.off * n + plus
        return c if self.reg is None else self.reg * n + c

    def shifted(self, by):
        return Tile(self.reg, self.off + by)

    def exists(self, tiles):
        return self.reg is not None or 0 <= self.off < tiles

    @property
    def first(self):
        return self.reg is None and self.off == 0


class Count(tuple):

    def __new__(cls, sem, value, rank):
        count = super().__new__(cls, (sem, value))
        count.rank = rank
        return count


class Progress:

    def __init__(self, sem, engine, stage):
        self.sem = sem
        items = sorted((i for i in ORDERS[engine] if stage_of(i[0]) == stage), key=lambda i: -i[2])
        self.names = [(name, *args) for kind, args, _ in items for name in STEPS[engine][kind]]
        self.index = {name: n + 1 for n, name in enumerate(self.names)}
        assert len(self.index) == len(self.names), self.names
        self.at = 0

    def step(self, *name):
        assert self.names[self.at % len(self.names)] == name, (self.names[self.at % len(self.names)], name)
        self.at += 1
        return self.sem, 1

    def after(self, tile, *name):
        return Count(self.sem, tile.times(len(self.names), self.index[name]),
                     tile.off * len(self.names) + self.index[name])


def bass_perceiver_layer(nc, a, tiles):
    ctx = ExitStack()
    with ctx:
        def sb(name, shape, dt=F32):
            return ctx.enter_context(nc.sbuf_tensor(name, shape, dt))

        def pb(name, cols):
            return ctx.enter_context(nc.psum_tensor(name, [P, cols], F32))

        def sem(name):
            return ctx.enter_context(nc.semaphore(name))

        def split(name, shape):
            return sb(name + "_hi", shape, F16), sb(name + "_lo", shape, F16)

        WQ, WK, WV, WO = (split(n, [P, KD, D]) for n in ("WQ", "WK", "WV", "WO"))
        FQ, FK, WV2 = (split(n, [P, KD, E2]) for n in ("FQ", "FK", "WV2"))
        W1 = split("W1", [P, KD, P])
        WO2 = split("WO2", [P, E2 // P, D])
        w2 = sb("w2", [P, SLOTS])
        WIH = split("WIH", [P, KD, 3 * D])
        gvo = sb("gvo", [P, KD, D])
        ident = sb("ident", [P, P])
        identb = sb("identb", [P, P], BF16)
        collapse = sb("collapse", [P, BT, P], F16)
        mask8 = sb("mask8", [P, 8, SQ], F16)
        mask_o = sb("mask_o", [P, 4, DK])
        same_b = sb("same_b", [P, P])
        mask_c = sb("mask_c", [P, P])
        half = sb("half", [P, 1])
        bq4c = sb("bq4c", [P, KD])
        bkc = sb("bkc", [P, KD])
        b_o1 = sb("b_o1", [P, D])
        b_o3 = sb("b_o3", [P, D])
        b2r = sb("b2r", [P, SLOTS])
        c_h = sb("c_h", [P, 1])
        tinv = sb("tinv", [P, 1])
        hs = sb("hs", [P, D])
        c_rz = sb("c_rz", [P, 2 * D])
        hn_half = sb("hn_half", [P, D])
        bihn = sb("bihn", [P, D])

        x_in = sb("x_in", [P, D])
        kv_last = sb("kv_last", [P, 2 * D])
        ctx_in = sb("ctx_in", [P, BT, KD, SK])
        st6 = sb("st6", [P, 3, 6])
        mv = sb("mv", [P, 3, 2])
        vareps = sb("vareps", [P, 3])
        rstd = sb("rstd", [P, 3])
        xn1 = sb("xn1", [P, D])
        x1T = split("x1T", [P, KD, P])
        qf = sb("qf", [P, 2, P])
        qs = split("qs", [P, 2, P])
        prod = sb("prod", [P, D])
        s_last = sb("s_last", [P, H])
        xres = sb("xres", [P, D])
        BD = split("BD", [P, 2, BT, 8, SQ])
        cs = split("cs", [P, 2, KD, SK])
        ks = split("ks", [P, 2, 2, SK])
        vs = split("vs", [P, BT, 2, NQ, DK * 4 + 1])
        nmax = sb("nmax", [P, BT, NQ], BF16)
        pf = sb("pf", [P, 2, 2, 512])
        ps = split("ps", [P, 2, 2, 512])
        om = sb("om", [P, 2, D + 2 * H])
        oms = split("oms", [P, BT, D + 2 * H])
        lk = sb("lk", [P, 8, H])
        lk2 = sb("lk2", [P, H])
        attn = sb("attn", [P, D])
        wv_l = sb("wv_l", [P, D])
        attT = split("attT", [P, KD, P])
        x1 = sb("x1", [P, D])
        xn2 = sb("xn2", [P, D])
        x2T = split("x2T", [P, KD, P])
        arg = sb("arg", [P, 4, 8, 2, HD])
        fmx = sb("fmx", [P, 4, 2, 8])
        fsum = sb("fsum", [P, 4, 2, 8, 2])
        featT = sb("featT", [P, 4, 2, 4, P])
        v1 = sb("v1", [P, H * (HD + 1) + 31])
        at_m = sb("at_m", [P, 2, 4, P])
        zr = sb("zr", [P, 4, 2, 4])
        y = sb("y", [P, E2])
        yT = split("yT", [P, 8, P])
        x2 = sb("x2", [P, D])
        x2b = sb("x2b", [P, D])
        xn3 = sb("xn3", [P, D])
        x3T = split("x3T", [P, KD, P])
        hT = sb("hT", [P, P])
        lg = sb("lg", [P, 6, SLOTS])
        sc3 = sb("sc3", [P, 16])
        abd = sb("abd", [P, BT, SLOTS])
        siT = split("siT", [P, KD, BT * SLOTS])
        abn = sb("abn", [P, BT, SLOTS])
        aT = sb("aT", [P, 2, P])
        rw = sb("rw", [P, 3, SLOTS])
        rz = sb("rz", [P, 2, 2 * D])
        gu = sb("gu", [P, 6, D])
        s_new = sb("s_new", [P, 2, D])
        asT = sb("asT", [P, KD, P])
        y_out = sb("y_out", [P, D])

        psum = pb("psum", 8 * BANK_F32)

        def bank(kind, *args):
            nums = banks_of(kind, args)
            return psum[:, nums[0] * BANK_F32:(nums[-1] + 1) * BANK_F32]

        def banks(lo, hi):
            return psum[:, lo * BANK_F32:hi * BANK_F32]

        scratch = nc.dram_tensor("kv_last_scratch", (P, 2 * D), F32, kind="Internal").ap()

        STORED_BEHIND = -next(off for kind, _, off in ORDERS["dve"] if kind == "3j")

        w_kv32 = pf[:].rearrange("p a b c -> p (a b c)")
        pairs = H // 2
        w2q32 = arg[:].rearrange("p a b c d -> p (a b c d)")[:, 0:pairs * D].rearrange("p (h n) -> p h n", h=pairs)
        w2k32 = featT[:].rearrange("p a b c d -> p (a b c d)")[:, 0:pairs * D].rearrange("p (h n) -> p h n", h=pairs)
        kq32 = v1[:, 0:E2].rearrange("p (h n) -> p h n", h=pairs)
        kk32 = y[:].rearrange("p (h n) -> p h n", h=pairs)
        wv232 = ctx_in[:].rearrange("p a b c -> p (a b c)")
        w132 = om[:].rearrange("p a b -> p (a b)")[:, 0:4 * P]
        whh32 = gu[:].rearrange("p a b -> p (a b)").rearrange("p (k n) -> p k n", k=KD)
        bk_row = xn3
        same_q = hT[:, 0:SQ]
        wv3 = rz[:, 0].rearrange("p (k n) -> p k n", k=KD)
        wo3 = rz[:, 1].rearrange("p (k n) -> p k n", k=KD)
        ctl = abn[:].rearrange("p a b -> p (a b)")
        hsT = at_m[:].rearrange("p a b c -> p (a b c)")[:, 0:KD * P]
        small = sb("small", [P, 16])
        rows = [prod, wv_l, attn]
        bih_r = at_m[:].rearrange("p a b c -> p (a b c)")[:, 512:1024]
        kvl_sb = s_new[:].rearrange("p a b -> p (a b)")

        w_in = sem("weights_in")
        x_ld = sem("x_loaded")
        kv_ld = sem("kv_last_loaded")
        ctx_ld = [sem(f"ctx_loaded_{b}") for b in range(BT)]
        out_st = sem("out_stored")
        scr_st = sem("scratch_stored")
        prep = {e: sem(f"prep_{e}") for e in ("pe", "act", "dve", "pool")}

        passed = {e: sem(f"passed_waits_{e}") for e in ("pool", "dve")}

        at_of = {e: {s: Progress(sem(f"{e}_{s}"), e, s) for s in ("P", "S1", "S2", "S3")} for e in STEPS}
        pe_at, act_at, dve_at, pool_at = (at_of[e] for e in ("pe", "act", "dve", "pool"))

        def block_diagonal(engine, n):
            q4 = qs[n][:].rearrange("p g (b q) -> p (g b) q", b=BT)
            return engine.tensor_tensor(BD[n][:].rearrange("p g b h q -> p (g b) h q"),
                                        q4.unsqueeze(2).to_broadcast([P, 2 * BT, 8, SQ]),
                                        mask8[:].unsqueeze(1).to_broadcast([P, 2 * BT, 8, SQ]), ALU.mult)

        def bank_read(item, turn):
            order = ORDERS["pe"]
            here = order.index(item)
            waits = {}
            for bank_no in banks_of(*item[:2]):
                for back in range(1, 2 * len(order)):
                    pos, turns_back = (here - back) % len(order), -((here - back) // len(order))
                    kind, args, off = order[pos]
                    t = turn.shifted(off - turns_back)
                    if bank_no in banks_of(kind, args) and t.exists(tiles):
                        waits[kind, args] = t
                        break
            return [at_of[LAST_READER[kind][0]][stage_of(kind)].after(t, LAST_READER[kind][1], *args)
                    for (kind, args), t in waits.items()]

        feature_loads = [(w2q32, a["aWq"]), (w2k32, a["aWk"])]
        for k32, name in ((kq32, "aKq"), (kk32, "aKk")):
            for n in range(2):
                rows_, cols = slice(n * HD, (n + 1) * HD), slice(n * HD, (n + 1) * HD)
                feature_loads.append((k32[rows_, :, cols], a[name][rows_]))
        features_in = sem("feature_weights_in")
        loads = [
            (w_kv32[:, 0:512].rearrange("p (k n) -> p k n", k=KD), a["xWk"]),
            (w_kv32[:, 512:1024].rearrange("p (k n) -> p k n", k=KD), a["xWv"]),
            (w_kv32[:, 1024:1536].rearrange("p (k n) -> p k n", k=KD), a["xWq"]),
            (w_kv32[:, 1536:2048].rearrange("p (k n) -> p k n", k=KD), a["xWo"]),
            (ctl.rearrange("p (k n) -> p k n", k=KD), a["ctx_last"]),
            (bk_row[:], a["xbk"].partition_broadcast(P)),
            (wv3, a["fWv"]),
            (wo3, a["fWo"]),
            (hs[0:SLOTS], a["slot_init"]),
            (hs[SLOTS:P], a["slot_init"]),
            (small[:, 0:2], a["xbv"]),
            (small[:, 2:4], a["fbv"]),
            (small[:, 6:7], a["tau"].partition_broadcast(P)),
            (small[0:SLOTS, 7:8], a["slot_scale"]),
            (small[SLOTS:P, 7:8], a["slot_scale"]),
            (small[:, 8:10], a["xbq_col"]),
            (bkc[:], a["xbk_col"]),
            (small[:, 10:11], a["fb1"]),
            (rows[0][:], a["xbo"].partition_broadcast(P)),
            (rows[1][:], a["fbo"].partition_broadcast(P)),
        ]
        wo232 = arg[:].rearrange("p a b c d -> p (a b c d)")[:, pairs * D:2 * pairs * D]\
            .rearrange("p (k n) -> p k n", k=8)
        wih32 = featT[:].rearrange("p a b c d -> p (a b c d)")[:, pairs * D:pairs * D + 6 * D]\
            .rearrange("p (k n) -> p k n", k=KD)
        late_loads = [
            (wv232.rearrange("p (k n) -> p k n", k=KD), a["aWv"]),
            (w132.rearrange("p (k n) -> p k n", k=4), a["fw1"]),
            (w2[:], a["fw2"]),
            (whh32, a["fwhh"]),
            (rows[2][:], a["fbhh"][2 * D:3 * D].partition_broadcast(P)),
            (bih_r, a["fbih"][0:2 * D].partition_broadcast(P)),
            (c_rz[:], a["fbhh"][0:2 * D].partition_broadcast(P)),
            (bihn[:], a["fbih"][2 * D:3 * D].partition_broadcast(P)),
            (b2r[:], a["fb2"].partition_broadcast(P)),
            (wo232, a["aWo"]),
            (wih32, a["fwih"]),
        ]
        late_in = sem("late_weights_in")
        POOL_ZEROED = 2
        POOL_CONSTANTS = 16
        POOL_PREP = 22
        ACT_FEATURES = 4
        ACT_ATTENTION = 8
        ACT_PREP = 13

        block = ctx.enter_context(nc.Block())

        def turns(engine, eng, run):
            def turn(n, reg=None):
                for item in ORDERS[engine]:
                    kind, args, off = item
                    t = Tile(reg, n + off)
                    if t.exists(tiles):
                        run(item, t)

            for n in range(-AHEAD, BEHIND + 1):
                turn(n)
            with eng.Fori(BEHIND + 1, tiles - AHEAD) as reg:
                turn(0, reg)
            for n in range(tiles - AHEAD, tiles + BEHIND):
                turn(n)

        @block.sync
        def _(sp):
            def start(dst, src, sm):
                sp.dma_start(dst, src).then_inc(sm, 16)

            for dst, src in feature_loads[:2]:
                start(dst, src, features_in)
            sp.wait_ge(prep["pool"], POOL_ZEROED)
            for dst, src in feature_loads[2:]:
                start(dst, src, features_in)
            for dst, src in loads:
                start(dst, src, w_in)
            for dst, src in late_loads:
                start(dst, src, late_in)
            sp.dma_start(x_in[:], a["x"][0]).then_inc(x_ld, 16)
            sp.wait_ge(prep["dve"], KVL_DONE)
            sp.dma_start(scratch, kvl_sb).then_inc(scr_st, 16)
            sp.wait_ge(scr_st, 16)

            def load_x(t):
                if not t.first:
                    sp.wait_ge(*pool_at["P"].after(t.shifted(-1), "xres"))
                    sp.wait_ge(*dve_at["P"].after(t.shifted(-1), "xn"))
                sp.dma_start(x_in[:], a["x"][t.times(1)]).then_inc(x_ld, 16)

            def load_kv(t):
                if not t.first:
                    sp.wait_ge(*pool_at["S1"].after(t.shifted(-1), "sum"))
                for b in range(BT):
                    sp.dma_start(kv_last[SQ * b:SQ * (b + 1), :],
                                 scratch[t.times(BT, b)].partition_broadcast(SQ)).then_inc(kv_ld, 16)

            def load_ctx(t, b):
                if not t.first:
                    sp.wait_ge(*pool_at["S1"].after(t.shifted(-1), "clo", b))
                sp.dma_start(ctx_in[:, b, :, :], a["ctx"][t.times(BT, b)]).then_inc(ctx_ld[b], 16)

            def store(t):
                sp.wait_ge(*dve_at["S3"].after(t, "out"))
                sp.dma_start(a["out"][t.times(1)], y_out[:]).then_inc(out_st, 16)

            first = Tile(None, 0)
            sp.wait_ge(prep["act"], ACT_PREP)
            sp.wait_ge(prep["dve"], WV2_DONE)
            for b in range(BT):
                load_ctx(first, b)
            load_kv(first)
            load_x(Tile(None, 1))

            def turn(t):
                if t.shifted(-STORED_BEHIND).exists(tiles):
                    store(t.shifted(-STORED_BEHIND))
                if t.shifted(1).exists(tiles):
                    for b in range(BT):
                        load_ctx(t.shifted(1), b)
                    load_kv(t.shifted(1))
                if t.shifted(2).exists(tiles):
                    load_x(t.shifted(2))

            peeled = STORED_BEHIND + 1
            for n in range(peeled):
                turn(Tile(None, n))
            with sp.Fori(peeled, tiles - 2) as reg:
                turn(Tile(reg, 0))
            for n in range(tiles - 2, tiles + STORED_BEHIND):
                turn(Tile(None, n))
            sp.wait_ge(out_st, 16 * tiles)

        @block.gpsimd
        def _(pool):
            g = nc.gpsimd

            def before():
                n = [0]

                def link(ins):
                    n[0] += 1
                    ins.then_inc(prep["pool"], 1)
                    pool.wait_ge(prep["pool"], n[0])

                link(g.memset(kq32, 0.0))
                link(g.memset(kk32, 0.0))
                assert n[0] == POOL_ZEROED
                link(g.memset(ident[:], 0.0))
                link(g.affine_select(out=ident[:], in_=ident[:], compare_op=ALU.not_equal, fill=1.0, base=0,
                                     pattern=[[-1, P]], channel_multiplier=1))
                link(g.tensor_copy(identb[:], ident[:]))
                link(g.memset(mask8[:], 1.0))
                link(g.affine_select(out=mask8[:], in_=mask8[:], compare_op=ALU.is_ge, fill=0.0, base=0,
                                     pattern=[[-DK, 8], [0, SQ]], channel_multiplier=1))
                link(g.affine_select(out=mask8[:], in_=mask8[:], compare_op=ALU.is_ge, fill=0.0, base=DK - 1,
                                     pattern=[[DK, 8], [0, SQ]], channel_multiplier=-1))
                link(g.memset(mask_o[:], 1.0))
                link(g.affine_select(out=mask_o[:], in_=mask_o[:], compare_op=ALU.is_ge, fill=0.0, base=0,
                                     pattern=[[-SQ, 4], [0, DK]], channel_multiplier=1))
                link(g.affine_select(out=mask_o[:], in_=mask_o[:], compare_op=ALU.is_ge, fill=0.0, base=SQ - 1,
                                     pattern=[[SQ, 4], [0, DK]], channel_multiplier=-1))
                mc = mask_c[:].rearrange("p (c r) -> p c r", c=4)
                link(g.memset(mask_c[:], 1.0))
                link(g.affine_select(out=mc, in_=mc, compare_op=ALU.is_ge, fill=0.0, base=0,
                                     pattern=[[-SQ, 4], [0, SQ]], channel_multiplier=1))
                link(g.affine_select(out=mc, in_=mc, compare_op=ALU.is_ge, fill=0.0, base=0,
                                     pattern=[[SQ, 4], [1, SQ]], channel_multiplier=-1))
                link(g.memset(collapse[:], 0.0))
                link(g.memset(half[:], -0.5))
                assert n[0] == POOL_CONSTANTS, n[0]
                pool.wait_ge(prep["act"], ACT_ATTENTION)
                kv4 = w_kv32.rearrange("p (w k n) -> p w k n", w=4, k=KD)
                for w, w32 in ((WK, kv4[:, 0]), (WV, kv4[:, 1]), (WQ, kv4[:, 2]), (WO, kv4[:, 3])):
                    link(g.tensor_tensor(w[1][:], w32, w[0][:], ALU.subtract))
                pool.wait_ge(prep["act"], ACT_PREP)
                for w, w32 in ((W1, w132.rearrange("p (k n) -> p k n", k=4)[:, 0:KD]), (WO2, wo232)):
                    link(g.tensor_tensor(w[1][:], w32, w[0][:], ALU.subtract))
                assert n[0] == POOL_PREP, n[0]

            def apart(*waits):
                for sm, val in waits:
                    pool.wait_ge(sm, val)
                pool.sem_inc(passed["pool"], 1)

            def power(stage, t, name, n):
                pool.wait_ge(*dve_at[stage].after(t, "eps"))
                g.tensor_tensor(rstd[:, n:n + 1], vareps[:, n:n + 1], half[:], ALU.pow)\
                 .then_inc(*pool_at[stage].step(name))

            def run(item, t):
                kind, arg_, off = item
                stage = stage_of(kind)
                prev = t.shifted(-1)
                if kind == "P0":
                    power("P", t, "rstd", 0)
                elif kind == "L2a":
                    power("S2", t, "rstd", 1)
                elif kind == "P2":
                    pool.wait_ge(*act_at["P"].after(t, "qhi"))
                    if not t.first:
                        pool.wait_ge(*pool_at["P"].after(prev, "bdlo"))
                    g.tensor_tensor(qs[1][:], qf[:], qs[0][:], ALU.subtract).then_inc(*pool_at["P"].step("qlo"))
                elif kind == "P3":
                    pool.wait_ge(*pool_at["P"].after(t, "qlo"))
                    if not t.first:
                        pool.wait_ge(*pe_at["S1"].after(prev, "ST", BT - 1))
                    block_diagonal(g, 1).then_inc(*pool_at["P"].step("bdlo"))
                elif kind == "P4":
                    pool.wait_ge(x_ld, t.times(16, 16))
                    if not t.first:
                        pool.wait_ge(*dve_at["S1"].after(prev, "x1"))
                    g.tensor_tensor(xres[:], x_in[:], b_o1[:], ALU.add).then_inc(*pool_at["P"].step("xres"))
                elif kind == "CS":
                    b, = arg_
                    pool.wait_ge(*act_at["S1"].after(t, "chi", b))
                    g.tensor_tensor(cs[1][:, b % 2], ctx_in[:, b], cs[0][:, b % 2], ALU.subtract)\
                     .then_inc(*pool_at["S1"].step("clo", b))
                elif kind == "ST":
                    b, = arg_
                    pool.wait_ge(*act_at["S1"].after(t, "pf", b))
                    if b >= 2:
                        pool.wait_ge(*pe_at["S1"].after(t, "PV", b - 2))
                    elif not t.first:
                        pool.wait_ge(*pe_at["S1"].after(prev, "PV", b + 2))
                    g.tensor_tensor(ps[1][:, b % 2], pf[:, b % 2], ps[0][:, b % 2], ALU.subtract)\
                     .then_inc(*pool_at["S1"].step("plo", b))
                elif kind == "PV":
                    b, = arg_
                    pool.wait_ge(*act_at["S1"].after(t, "ohi", b))
                    g.tensor_tensor(oms[1][:, b], om[:, b % 2], oms[0][:, b], ALU.subtract)\
                     .then_inc(*pool_at["S1"].step("olo", b))
                elif kind == "C1e":
                    pool.wait_ge(*dve_at["S1"].after(t, "at"))
                    pool.wait_ge(*pool_at["S1"].after(t, "wv"))
                    g.tensor_tensor(wv_l[:], wv_l[:], attn[:], ALU.add).then_inc(*pool_at["S1"].step("sum"))
                elif kind == "C1":
                    pool.wait_ge(*dve_at["S1"].after(t, "ea"))
                    g.tensor_tensor(wv_l[:].rearrange("p (h d) -> p h d", h=H),
                                    kv_last[:, D:2 * D].rearrange("p (h d) -> p h d", h=H),
                                    lk2[:].unsqueeze(2).to_broadcast([P, H, DK]), ALU.mult)\
                     .then_inc(*pool_at["S1"].step("wv"))
                elif kind == "N":
                    c, = arg_
                    pool.wait_ge(*dve_at["S2"].after(t, "rs", c))
                    f = arg[:, c].rearrange("p h s f -> p (h s) f")
                    g.tensor_tensor(f, f, fsum[:, c, 1].rearrange("p h s -> p (h s)").unsqueeze(2)
                                    .to_broadcast([P, 16, HD]), ALU.mult).then_inc(*pool_at["S2"].step("norm", c))
                elif kind == "3a":
                    pool.wait_ge(*dve_at["S2"].after(t, "x2"))
                    if not t.first:
                        pool.wait_ge(*dve_at["S3"].after(prev, "out"))
                    g.tensor_tensor(x2b[:], x2[:], b_o3[:], ALU.add).then_inc(*pool_at["S3"].step("x2b"))
                elif kind == "3x":
                    power("S3", t, "rstd", 2)
                elif kind == "3h":
                    n, = arg_
                    pool.wait_ge(*act_at["S3"].after(t, "tanh", n))
                    g.tensor_tensor(gu[:, 1], rz[:, n, 0:D], hn_half[:], ALU.mult)\
                     .then_inc(*pool_at["S3"].step("v", n))
                    pool.wait_ge(*dve_at["S3"].after(t, "u", n))
                    pool.wait_ge(*pool_at["S3"].after(t, "v", n))
                    g.tensor_tensor(gu[:, 2], gu[:, 0], gu[:, 1], ALU.add).then_inc(*pool_at["S3"].step("w", n))
                elif kind == "3S":
                    n, = arg_
                    pool.wait_ge(*act_at["S3"].after(t, "n", n))
                    g.tensor_tensor(gu[:, 4], hs[:], gu[:, 3], ALU.subtract).then_inc(*pool_at["S3"].step("d", n))

            before()
            turns("pool", pool, run)

        @block.scalar
        def _(act):
            s = nc.scalar

            def before():
                n = [0]

                def done(ins):
                    n[0] += 1
                    ins.then_inc(prep["act"], 1)

                act.wait_ge(prep["pe"], 1)
                for w, lo in ((FQ, 0), (FK, 4)):
                    for k in range(KD):
                        done(s.copy(w[0][:, k], banks(lo + 2 * k, lo + 2 * k + 2)))
                assert n[0] == ACT_FEATURES
                act.wait_ge(w_in, 16 * len(loads))
                kv4 = w_kv32.rearrange("p (w k n) -> p w k n", w=4, k=KD)
                for i, w in enumerate((WK, WV, WQ, WO)):
                    done(s.copy(w[0][:], kv4[:, i]))
                assert n[0] == ACT_ATTENTION
                done(s.mul(bq4c[:], small[:, 8:10], 0.25))
                act.wait_ge(late_in, 16 * len(late_loads))
                done(s.copy(WV2[0][:], wv232.rearrange("p (k n) -> p k n", k=KD)))
                done(s.copy(W1[0][:], w132.rearrange("p (k n) -> p k n", k=4)[:, 0:KD]))
                done(s.copy(WO2[0][:], wo232))
                done(s.copy(WIH[0][:], wih32))
                assert n[0] == ACT_PREP, n[0]

            def run(item, t):
                kind, arg_, off = item
                stage = stage_of(kind)
                prev = t.shifted(-1)
                if kind in ("P1", "L2b", "3b"):
                    xT = {"P1": x1T, "L2b": x2T, "3b": x3T}[kind]
                    act.wait_ge(*pe_at[stage].after(t, "xT"))
                    s.copy(xT[0][:].rearrange("p k n -> p (k n)"), bank(kind, *arg_)[:, 0:D])\
                     .then_inc(*act_at[stage].step("xhi"))
                elif kind == "P2":
                    act.wait_ge(*pe_at["P"].after(t, "q"))
                    if not t.first:
                        act.wait_ge(*pool_at["P"].after(prev, "qlo"))
                        act.wait_ge(*pe_at["P"].after(prev, "qn"))
                    for n in range(2):
                        s.activation(qf[:, n], bank("P2")[:, n * P:(n + 1) * P], ACT.Identity, bias=bq4c[:, n:n + 1],
                                     scale=0.25).then_inc(*act_at["P"].step(f"qf{n}"))
                    act.wait_ge(*act_at["P"].after(t, "qf1"))
                    if not t.first:
                        act.wait_ge(*dve_at["P"].after(prev, "bdhi"))
                    s.copy(qs[0][:], qf[:]).then_inc(*act_at["P"].step("qhi"))
                elif kind == "CS":
                    b, = arg_
                    act.wait_ge(ctx_ld[b], t.times(16, 16))
                    if b >= 2:
                        act.wait_ge(*pe_at["S1"].after(t, "v", b - 2))
                    elif not t.first:
                        act.wait_ge(*pe_at["S1"].after(prev, "v", b + 2))
                    s.copy(cs[0][:, b % 2], ctx_in[:, b]).then_inc(*act_at["S1"].step("chi", b))
                elif kind == "K":
                    b, = arg_
                    act.wait_ge(*pe_at["S1"].after(t, "kT", b))
                    if b >= 2:
                        act.wait_ge(*pe_at["S1"].after(t, "ST", b - 2))
                    elif not t.first:
                        act.wait_ge(*pe_at["S1"].after(prev, "ST", b + 2))
                    for n in range(2):
                        s.activation(ks[0][:, b % 2, n], bank("K", b)[:, n * SK:(n + 1) * SK], ACT.Identity,
                                     bias=bkc[:, n:n + 1]).then_inc(*act_at["S1"].step(f"kh{n}", b))
                elif kind == "VB":
                    b, = arg_
                    act.wait_ge(*pe_at["S1"].after(t, "v", b))
                    if not t.first:
                        act.wait_ge(*pe_at["S1"].after(prev, "PV", b))
                    s.copy(vs[0][:, b, :, :, 0:4 * DK].rearrange("p k j d -> p (k j) d"),
                           bank("VB", b).rearrange("p (k d) -> p k d", d=4 * DK))\
                     .then_inc(*act_at["S1"].step("vh", b))
                elif kind == "ST":
                    b, = arg_
                    act.wait_ge(*pe_at["S1"].after(t, "ST", b))
                    if b >= 2:
                        act.wait_ge(*pool_at["S1"].after(t, "plo", b - 2))
                        act.wait_ge(*pe_at["S1"].after(t, "PV", b - 2))
                    elif not t.first:
                        act.wait_ge(*pool_at["S1"].after(prev, "plo", b + 2))
                        act.wait_ge(*pe_at["S1"].after(prev, "PV", b + 2))
                    s.activation(ps[0][:, b % 2].rearrange("p k n -> p (k n)"), bank("ST", b), ACT.Exp)\
                     .then_inc(*act_at["S1"].step("ph", b))
                    s.activation(pf[:, b % 2].rearrange("p k n -> p (k n)"), bank("ST", b), ACT.Exp)\
                     .then_inc(*act_at["S1"].step("pf", b))
                elif kind == "PV":
                    b, = arg_
                    act.wait_ge(*dve_at["S1"].after(t, "mx", b))
                    if not t.first:
                        act.wait_ge(*pe_at["S1"].after(prev, "X"))
                    s.copy(oms[0][:, b], om[:, b % 2]).then_inc(*act_at["S1"].step("ohi", b))
                elif kind == "C1":
                    act.wait_ge(*dve_at["S1"].after(t, "te"))
                    s.activation(lk[:, 3:5, :].rearrange("p a b -> p (a b)"),
                                 lk[:, 1:3, :].rearrange("p a b -> p (a b)"), ACT.Exp)\
                     .then_inc(*act_at["S1"].step("ae"))
                elif kind == "C2":
                    act.wait_ge(*pe_at["S1"].after(t, "aT"))
                    s.copy(attT[0][:].rearrange("p k n -> p (k n)"), bank("C2")[:, 0:D])\
                     .then_inc(*act_at["S1"].step("ahi"))
                elif kind == "F":
                    c, = arg_
                    act.wait_ge(*dve_at["S2"].after(t, "subp", c))
                    for h in range(8):
                        last = s.activation(arg[:, c, h, 1], bank("F", c)[:, h * HD:(h + 1) * HD], ACT.Exp,
                                            bias=fmx[:, c, 1, h:h + 1], scale=-1.0, accum_out=fsum[:, c, 0, h, 1:2])
                    last.then_inc(*act_at["S2"].step("expm", c))
                    f = arg[:, c, :, 0]
                    s.activation(f, f, ACT.Exp).then_inc(*act_at["S2"].step("expp", c))
                elif kind == "V":
                    n, = arg_
                    act.wait_ge(*pe_at["S2"].after(t, "v", n))
                    if not t.first:
                        act.wait_ge(*pe_at["S2"].after(prev, "AV", 2 * n + 1))
                    w = (HD + 1) * 8
                    s.copy(v1[:, n * w:(n + 1) * w].rearrange("p (h d) -> p h d", h=8)[:, :, 0:HD],
                           bank("V", n).rearrange("p (h d) -> p h d", h=8))\
                     .then_inc(*act_at["S2"].step("v", n))
                elif kind == "T":
                    c, i = arg_
                    act.wait_ge(*pe_at["S2"].after(t, "T", c, i))
                    if not t.first:
                        act.wait_ge(*pe_at["S2"].after(prev, "AT", c // 2 * 2 + i))
                    s.copy(featT[:, c, i].rearrange("p h n -> p (h n)"), bank("T", c, i))\
                     .then_inc(*act_at["S2"].step("feat", c, i))
                elif kind == "Y":
                    n, = arg_
                    act.wait_ge(*pe_at["S2"].after(t, "Y", n))
                    if not t.first and n == 0:
                        act.wait_ge(*pe_at["S2"].after(prev, "W"))
                    s.copy(yT[0][:, 4 * n:4 * n + 4].rearrange("p h n -> p (h n)"), bank("Y", n))\
                     .then_inc(*act_at["S2"].step("yhi", n))
                elif kind == "3c":
                    act.wait_ge(*pe_at["S3"].after(t, "h"))
                    s.activation(hT[:], bank(kind, *arg_)[:, 0:P], ACT.Gelu, bias=c_h[:, 0:1])\
                     .then_inc(*act_at["S3"].step("gelu"))
                elif kind == "3d":
                    act.wait_ge(*dve_at["S3"].after(t, "nmax"))
                    s.activation(lg[:, 4], lg[:, 1], ACT.Exp, bias=sc3[:, 8:9]).then_inc(*act_at["S3"].step("e"))
                elif kind == "3e":
                    act.wait_ge(*pe_at["S3"].after(t, "si"))
                    s.copy(siT[0][:].rearrange("p k n -> p (k n)"), bank("3e"))\
                     .then_inc(*act_at["S3"].step("sihi"))
                elif kind == "3f":
                    act.wait_ge(*pe_at["S3"].after(t, "aT"))
                    s.copy(aT[:].rearrange("p k n -> p (k n)"), bank("3f")[:, 0:2 * P])\
                     .then_inc(*act_at["S3"].step("aT"))
                elif kind == "3g":
                    n, = arg_
                    act.wait_ge(*dve_at["S3"].after(t, "rz", n))
                    s.activation(rz[:, n], rz[:, n], ACT.Tanh, scale=0.5).then_inc(*act_at["S3"].step("tanh", n))
                elif kind == "3h":
                    n, = arg_
                    act.wait_ge(*pool_at["S3"].after(t, "w", n))
                    s.activation(gu[:, 3], gu[:, 2], ACT.Tanh).then_inc(*act_at["S3"].step("n", n))
                elif kind == "3i":
                    act.wait_ge(*pe_at["S3"].after(t, "as"))
                    s.copy(asT[:].rearrange("p k n -> p (k n)"), bank("3i")[:, 0:D])\
                     .then_inc(*act_at["S3"].step("as"))

            before()
            turns("act", act, run)

        @block.vector
        def _(dve):
            v = nc.vector

            def before():
                n = [0]

                def link(ins):
                    n[0] += 1
                    ins.then_inc(prep["dve"], 1)
                    dve.wait_ge(prep["dve"], n[0])

                for m, (w, lo) in enumerate(((FQ, 0), (FK, 4))):
                    for k in range(KD):
                        dve.wait_ge(prep["act"], 2 * m + k + 1)
                        link(v.tensor_tensor(w[1][:, k], banks(lo + 2 * k, lo + 2 * k + 2), w[0][:, k],
                                             ALU.subtract))
                    assert n[0] == (FQ_DONE, FK_DONE)[m]
                dve.wait_ge(prep["pool"], POOL_CONSTANTS)
                link(v.memset(vs[0][:, :, :, :, 4 * DK:4 * DK + 1], 1.0))
                link(v.memset(vs[1][:, :, :, :, 4 * DK:4 * DK + 1], 0.0))
                link(v.memset(v1[:], 1.0))
                link(v.tensor_reduce(same_q, ident[:].rearrange("p (h r) -> p r h", h=4), AX.X, ALU.add))
                for b in range(BT):
                    link(v.tensor_copy(collapse[:, b, SQ * b:SQ * (b + 1)], same_q))
                link(v.tensor_copy(same_b[:].rearrange("p (b q) -> p b q", b=BT),
                                   mask_o[:, :, 0].unsqueeze(2).to_broadcast([P, BT, SQ])))
                dve.wait_ge(w_in, 16 * len(loads))
                link(v.tensor_scalar(hs[:], hs[:], small[:, 7:8], None, ALU.mult))
                assert n[0] == HS_DONE
                dve.wait_ge(prep["pe"], 2)
                link(v.tensor_copy(hsT, banks(2, 3)[:, 0:D]))
                assert n[0] == HST_DONE
                link(v.tensor_tensor(kvl_sb[:, 0:D], banks(0, 1)[:, 0:D], bk_row[:], ALU.add))
                link(v.tensor_copy(kvl_sb[:, D:2 * D], banks(0, 1)[:, D:2 * D]))
                assert n[0] == KVL_DONE
                link(v.tensor_reduce(small[:, 4:6], hsT.rearrange("p (k n) -> p k n", k=KD)[:, :, 0:SLOTS], AX.X,
                                     ALU.add))
                link(v.tensor_scalar(small[:, 4:6], small[:, 4:6], 1.0 / SLOTS, None, ALU.mult))
                assert n[0] == MEAN_DONE
                link(v.tensor_tensor(b_o1[:], banks(1, 2)[:, 0:D], rows[0][:], ALU.add))
                link(v.tensor_tensor(b_o3[:], banks(1, 2)[:, D:2 * D], rows[1][:], ALU.add))
                link(v.tensor_copy(gvo[:].rearrange("p k n -> p (k n)"), banks(3, 4)))
                link(v.tensor_scalar(small[:, 11:12], small[:, 6:7], -1.0, None, ALU.mult))
                link(v.tensor_tensor(small[:, 12:13], small[:, 6:7], small[:, 11:12], ALU.max))
                link(v.tensor_scalar(small[:, 13:14], small[:, 12:13], 0.1, None, ALU.add))
                link(v.reciprocal(tinv[:], small[:, 13:14]))
                dve.wait_ge(prep["act"], ACT_PREP)
                link(v.tensor_tensor(WV2[1][:], wv232.rearrange("p (k n) -> p k n", k=KD), WV2[0][:], ALU.subtract))
                assert n[0] == WV2_DONE
                link(v.tensor_tensor(WIH[1][:], wih32, WIH[0][:], ALU.subtract))
                dve.wait_ge(prep["pe"], 3)
                link(v.tensor_tensor(c_h[:], banks(6, 7)[:, 0:1], small[:, 10:11], ALU.add))
                link(v.tensor_tensor(c_rz[:], banks(4, 5), c_rz[:], ALU.add))
                link(v.tensor_tensor(c_rz[:], c_rz[:], bih_r, ALU.add))
                link(v.tensor_tensor(hn_half[:], banks(5, 6)[:, 0:D], rows[2][:], ALU.add))
                link(v.tensor_scalar(hn_half[:], hn_half[:], 0.5, None, ALU.mult))
                link(v.tensor_tensor(bihn[:], bihn[:], hn_half[:], ALU.add))
                assert n[0] == DVE_PREP, n[0]

            def apart(*waits):
                for sm, val in waits:
                    dve.wait_ge(sm, val)
                dve.sem_inc(passed["dve"], 1)

            def norm_stats(stage, t, src, n):
                v.bn_stats(st6[:, n, :], src).then_inc(*dve_at[stage].step("stats"))
                apart(dve_at[stage].after(t, "stats"))
                v.bn_aggr(mv[:, n, :], st6[:, n, :]).then_inc(*dve_at[stage].step("aggr"))
                dve.wait_ge(*dve_at[stage].after(t, "aggr"))
                v.tensor_scalar(vareps[:, n:n + 1], mv[:, n, 1:2], LN_EPS, None, ALU.add)\
                 .then_inc(*dve_at[stage].step("eps"))

            def normed(stage, t, src, dst, n):
                dve.wait_ge(*pool_at[stage].after(t, "rstd"))
                v.tensor_scalar(dst, src, mv[:, n, 0:1], rstd[:, n:n + 1], ALU.subtract, ALU.mult)\
                 .then_inc(*dve_at[stage].step("xn"))

            def run(item, t):
                kind, arg_, off = item
                stage = stage_of(kind)
                prev = t.shifted(-1)
                if kind == "P0":
                    dve.wait_ge(x_ld, t.times(16, 16))
                    norm_stats("P", t, x_in[:], 0)
                elif kind == "P0x":
                    if not t.first:
                        dve.wait_ge(*pe_at["P"].after(prev, "xT"))
                    normed("P", t, x_in[:], xn1[:], 0)
                elif kind == "L2a":
                    dve.wait_ge(*dve_at["S1"].after(t, "x1"))
                    norm_stats("S2", t, x1[:], 1)
                elif kind == "L2x":
                    normed("S2", t, x1[:], xn2[:], 1)
                elif kind == "3a":
                    dve.wait_ge(*dve_at["S2"].after(t, "x2"))
                    norm_stats("S3", t, x2[:], 2)
                elif kind == "3x":
                    if not t.first:
                        dve.wait_ge(*pe_at["S3"].after(prev, "si"))
                    normed("S3", t, x2[:], xn3[:], 2)
                elif kind in ("P1", "L2b", "3b"):
                    xT = {"P1": x1T, "L2b": x2T, "3b": x3T}[kind]
                    dve.wait_ge(*act_at[stage].after(t, "xhi"))
                    v.tensor_tensor(xT[1][:].rearrange("p k n -> p (k n)"), bank(kind, *arg_)[:, 0:D],
                                    xT[0][:].rearrange("p k n -> p (k n)"), ALU.subtract)\
                     .then_inc(*dve_at[stage].step("xlo"))
                elif kind == "P3":
                    dve.wait_ge(*act_at["P"].after(t, "qhi"))
                    if not t.first:
                        dve.wait_ge(*pe_at["S1"].after(prev, "ST", BT - 1))
                    block_diagonal(v, 0).then_inc(*dve_at["P"].step("bdhi"))
                elif kind == "P4":
                    dve.wait_ge(*pe_at["P"].after(t, "qn"))
                    dve.wait_ge(kv_ld, t.times(64, 64))
                    if not t.first:
                        dve.wait_ge(*dve_at["P"].after(prev, "slast"))
                    v.tensor_tensor(prod[:], bank("P4")[:, 0:D], kv_last[:, 0:D], ALU.mult)\
                     .then_inc(*dve_at["P"].step("prod"))
                    dve.wait_ge(*dve_at["P"].after(t, "prod"))
                    v.tensor_reduce(s_last[:], prod[:].rearrange("p (h d) -> p h d", h=H), AX.X, ALU.add)\
                     .then_inc(*dve_at["P"].step("slast"))
                elif kind == "K":
                    b, = arg_
                    dve.wait_ge(*act_at["S1"].after(t, "kh1", b))
                    for n in range(2):
                        v.scalar_tensor_tensor(ks[1][:, b % 2, n], bank("K", b)[:, n * SK:(n + 1) * SK], bkc[:, n:n + 1],
                                               ks[0][:, b % 2, n], ALU.add, ALU.subtract)\
                         .then_inc(*dve_at["S1"].step(f"kl{n}", b))
                elif kind == "VB":
                    b, = arg_
                    dve.wait_ge(*act_at["S1"].after(t, "vh", b))
                    v.tensor_tensor(vs[1][:, b, :, :, 0:4 * DK].rearrange("p k j d -> p (k j) d"),
                                    bank("VB", b).rearrange("p (k d) -> p k d", d=4 * DK),
                                    vs[0][:, b, :, :, 0:4 * DK].rearrange("p k j d -> p (k j) d"), ALU.subtract)\
                     .then_inc(*dve_at["S1"].step("vl", b))
                elif kind == "A":
                    b, = arg_
                    dve.wait_ge(*pe_at["S1"].after(t, "A", b))
                    if not t.first:
                        dve.wait_ge(*pe_at["S1"].after(prev, "ST", b))
                        dve.wait_ge(*dve_at["S1"].after(prev, "mx", b))
                    v.tensor_reduce(nmax[:, b, :], bank("A", b).rearrange("p (j n) -> p j n", j=NQ), AX.X, ALU.max,
                                    negate=True).then_inc(*dve_at["S1"].step("max", b))
                elif kind == "PV":
                    b, = arg_
                    dve.wait_ge(*pe_at["S1"].after(t, "PV", b))
                    if b >= 2:
                        dve.wait_ge(*pool_at["S1"].after(t, "olo", b - 2))
                    elif not t.first:
                        dve.wait_ge(*pool_at["S1"].after(prev, "olo", b + 2))
                    o4 = bank("PV", b)[:, 0:NQ * 65].rearrange("p (j d) -> p j d", j=NQ)
                    mo = mask_o[:].rearrange("p a b -> p (a b)")
                    v.tensor_tensor(om[:, b % 2, 0:D].rearrange("p (j d) -> p j d", j=NQ), o4[:, :, 0:64],
                                    mo.unsqueeze(1).to_broadcast([P, NQ, 64]), ALU.mult)\
                     .then_inc(*dve_at["S1"].step("om", b))
                    m4 = mask_o[:, :, 0].unsqueeze(1).to_broadcast([P, NQ, 4])
                    v.tensor_tensor(om[:, b % 2, D:D + H].rearrange("p (j h) -> p j h", j=NQ),
                                    o4[:, :, 64:65].to_broadcast([P, NQ, 4]), m4, ALU.mult)\
                     .then_inc(*dve_at["S1"].step("zx", b))
                    v.tensor_tensor(om[:, b % 2, D + H:D + 2 * H].rearrange("p (j h) -> p j h", j=NQ),
                                    nmax[:, b, :].unsqueeze(2).to_broadcast([P, NQ, 4]), m4, ALU.mult)\
                     .then_inc(*dve_at["S1"].step("mx", b))
                elif kind == "C1":
                    dve.wait_ge(*pe_at["S1"].after(t, "X"))
                    dve.wait_ge(*dve_at["P"].after(t, "slast"))
                    at = dve_at["S1"]
                    v.tensor_tensor(lk[:, 0], bank("C1")[:, D + H:D + 2 * H], s_last[:], ALU.add)\
                     .then_inc(*at.step("d"))
                    dve.wait_ge(*at.after(t, "d"))
                    v.tensor_scalar(lk[:, 1], lk[:, 0], -1.0, 0.0, ALU.mult, ALU.min).then_inc(*at.step("ta"))
                    v.tensor_scalar(lk[:, 2], lk[:, 0], 0.0, None, ALU.min).then_inc(*at.step("te"))
                elif kind == "C1e":
                    at = dve_at["S1"]
                    dve.wait_ge(*act_at["S1"].after(t, "ae"))
                    v.tensor_tensor(lk[:, 5], bank("C1")[:, D:D + H], lk[:, 3], ALU.mult).then_inc(*at.step("za"))
                    dve.wait_ge(*at.after(t, "za"))
                    v.tensor_tensor(lk[:, 6], lk[:, 5], lk[:, 4], ALU.add).then_inc(*at.step("zt"))
                    dve.wait_ge(*at.after(t, "zt"))
                    v.reciprocal(lk[:, 7], lk[:, 6]).then_inc(*at.step("rz"))
                    dve.wait_ge(*at.after(t, "rz"))
                    v.tensor_tensor(lk2[:], lk[:, 4], lk[:, 7], ALU.mult).then_inc(*at.step("ea"))
                    v.scalar_tensor_tensor(lk[:, 5], lk[:, 3], 1.0, lk[:, 7], ALU.mult, ALU.mult)\
                     .then_inc(*at.step("at0"))
                    dve.wait_ge(*at.after(t, "at0"))
                    v.tensor_tensor(attn[:].rearrange("p (h d) -> p h d", h=H),
                                    bank("C1")[:, 0:D].rearrange("p (h d) -> p h d", h=H),
                                    lk[:, 5].unsqueeze(2).to_broadcast([P, H, DK]), ALU.mult)\
                     .then_inc(*at.step("at"))
                elif kind == "C2":
                    dve.wait_ge(*act_at["S1"].after(t, "ahi"))
                    v.tensor_tensor(attT[1][:].rearrange("p k n -> p (k n)"), bank("C2")[:, 0:D],
                                    attT[0][:].rearrange("p k n -> p (k n)"), ALU.subtract)\
                     .then_inc(*dve_at["S1"].step("alo"))
                elif kind == "C3":
                    dve.wait_ge(*pe_at["S1"].after(t, "o"))
                    if not t.first:
                        dve.wait_ge(*dve_at["S2"].after(prev, "x2"))
                    v.tensor_tensor(x1[:], bank("C3")[:, 0:D], xres[:], ALU.add).then_inc(*dve_at["S1"].step("x1"))
                elif kind == "F":
                    c, = arg_
                    at = dve_at["S2"]
                    dve.wait_ge(*pe_at["S2"].after(t, "f", c))
                    if not t.first:
                        dve.wait_ge(*pe_at["S2"].after(prev, "T", c, 1))
                    f = bank("F", c).rearrange("p (h f) -> p h f", h=8)
                    v.tensor_reduce(fmx[:, c, 0], f, AX.X, ALU.max).then_inc(*at.step("max", c))
                    v.tensor_reduce(fmx[:, c, 1], f, AX.X, ALU.min).then_inc(*at.step("min", c))
                    dve.wait_ge(*at.after(t, "max", c))
                    v.tensor_tensor(arg[:, c, :, 0, :], f, fmx[:, c, 0].unsqueeze(2).to_broadcast([P, 8, HD]),
                                    ALU.subtract).then_inc(*at.step("subp", c))
                elif kind == "G":
                    c, = arg_
                    at = dve_at["S2"]
                    dve.wait_ge(*act_at["S2"].after(t, "expp", c))
                    v.tensor_reduce(fsum[:, c, 0, :, 0], arg[:, c, :, 0], AX.X, ALU.add).then_inc(*at.step("sum", c))
                    dve.wait_ge(*at.after(t, "sum", c))
                    v.reciprocal(fsum[:, c, 1], fsum[:, c, 0]).then_inc(*at.step("rs", c))
                elif kind == "N":
                    c, = arg_
                    at = dve_at["S2"]
                    dve.wait_ge(*pool_at["S2"].after(t, "norm", c))
                    fl = arg[:, c].rearrange("p h s f -> p (h s f)")
                    v.tensor_scalar(fl, fl, FEAT_EPS, None, ALU.max).then_inc(*at.step("clamp", c))
                elif kind == "AT":
                    g4, = arg_
                    dve.wait_ge(*pe_at["S2"].after(t, "AT", g4))
                    if g4 >= 2:
                        dve.wait_ge(*pe_at["S2"].after(t, "AV", g4 - 2))
                    elif not t.first:
                        dve.wait_ge(*pe_at["S2"].after(prev, "AV", g4 + 2))
                    v.tensor_tensor(at_m[:, g4 % 2],
                                    bank("AT", g4).rearrange("p (h n) -> p h n", h=4),
                                    mask_c[:].unsqueeze(1).to_broadcast([P, 4, P]), ALU.mult)\
                     .then_inc(*dve_at["S2"].step("mask", g4))
                elif kind == "AV":
                    g4, = arg_
                    at = dve_at["S2"]
                    dve.wait_ge(*pe_at["S2"].after(t, "AV", g4))
                    if not t.first:
                        dve.wait_ge(*pe_at["S2"].after(prev, "Y", g4 // 2))
                    o = bank("AV", g4)[:, 0:384].rearrange("p (h d) -> p h d", h=4)
                    v.tensor_scalar(zr[:, g4, 0], o[:, :, HD], FEAT_EPS, None, ALU.add).then_inc(*at.step("z", g4))
                    dve.wait_ge(*at.after(t, "z", g4))
                    v.reciprocal(zr[:, g4, 1], zr[:, g4, 0]).then_inc(*at.step("rz", g4))
                    dve.wait_ge(*at.after(t, "rz", g4))
                    v.tensor_tensor(y[:, g4 * 256:(g4 + 1) * 256].rearrange("p (h d) -> p h d", h=4), o[:, :, 0:HD],
                                    zr[:, g4, 1].unsqueeze(2).to_broadcast([P, 4, HD]), ALU.mult)\
                     .then_inc(*at.step("y", g4))
                elif kind == "Y":
                    n, = arg_
                    dve.wait_ge(*act_at["S2"].after(t, "yhi", n))
                    v.tensor_tensor(yT[1][:, 4 * n:4 * n + 4].rearrange("p h n -> p (h n)"), bank("Y", n),
                                    yT[0][:, 4 * n:4 * n + 4].rearrange("p h n -> p (h n)"), ALU.subtract)\
                     .then_inc(*dve_at["S2"].step("ylo", n))
                elif kind == "W":
                    dve.wait_ge(*pe_at["S2"].after(t, "W"))
                    if not t.first:
                        dve.wait_ge(*pool_at["S3"].after(prev, "x2b"))
                        dve.wait_ge(*dve_at["S3"].after(prev, "xn"))
                    v.tensor_tensor(x2[:], bank("W")[:, 0:D], x1[:], ALU.add).then_inc(*dve_at["S2"].step("x2"))
                elif kind == "3d":
                    at = dve_at["S3"]
                    dve.wait_ge(*pe_at["S3"].after(t, "lg"))
                    v.tensor_tensor(lg[:, 0], bank("3d")[:, 0:SLOTS], b2r[:], ALU.add).then_inc(*at.step("lb"))
                    dve.wait_ge(*at.after(t, "lb"))
                    v.tensor_scalar(lg[:, 1], lg[:, 0], tinv[:, 0:1], None, ALU.mult).then_inc(*at.step("lg"))
                    apart(at.after(t, "lg"))
                    v.max(sc3[:, 0:8], lg[:, 1]).then_inc(*at.step("top"))
                    apart(at.after(t, "top"))
                    v.match_replace(lg[:, 2], sc3[:, 0:8], lg[:, 1], NEG).then_inc(*at.step("repl"))
                    dve.wait_ge(*at.after(t, "repl"))
                    v.tensor_tensor(lg[:, 3], lg[:, 2], lg[:, 1], ALU.not_equal).then_inc(*at.step("sel"))
                    v.tensor_scalar(sc3[:, 8:9], sc3[:, 0:1], -1.0, None, ALU.mult).then_inc(*at.step("nmax"))
                elif kind == "3w":
                    at = dve_at["S3"]
                    dve.wait_ge(*act_at["S3"].after(t, "e"))
                    dve.wait_ge(*at.after(t, "sel"))
                    v.scalar_tensor_tensor(lg[:, 5], lg[:, 4], 1.0, lg[:, 3], ALU.mult, ALU.mult,
                                           accum_out=sc3[:, 9:10]).then_inc(*at.step("ea"))
                    dve.wait_ge(*at.after(t, "ea"))
                    v.reciprocal(sc3[:, 10:11], sc3[:, 9:10]).then_inc(*at.step("rs"))
                    dve.wait_ge(*at.after(t, "rs"))
                    v.tensor_scalar(lg[:, 0], lg[:, 5], sc3[:, 10:11], None, ALU.mult).then_inc(*at.step("al"))
                    dve.wait_ge(*at.after(t, "al"))
                    if not t.first:
                        dve.wait_ge(*pe_at["S3"].after(prev, "aT"))
                    v.tensor_tensor(abd[:], lg[:, 0].unsqueeze(1).to_broadcast([P, BT, SLOTS]),
                                    mask_o[:, :, 0].unsqueeze(2).to_broadcast([P, BT, SLOTS]), ALU.mult)\
                     .then_inc(*at.step("abd"))
                elif kind == "3s":
                    at = dve_at["S3"]
                    dve.wait_ge(*pe_at["S3"].after(t, "ws"))
                    v.tensor_scalar(rw[:, 0], bank("3s")[:, 0:SLOTS], WSUM_EPS, None, ALU.add)\
                     .then_inc(*at.step("ws"))
                    dve.wait_ge(*at.after(t, "ws"))
                    v.reciprocal(rw[:, 1], rw[:, 0]).then_inc(*at.step("rw"))
                    dve.wait_ge(*at.after(t, "rw"))
                    v.tensor_tensor(rw[:, 2], lg[:, 0], rw[:, 1], ALU.mult).then_inc(*at.step("an"))
                    dve.wait_ge(*at.after(t, "an"))
                    v.tensor_tensor(abn[:], rw[:, 2].unsqueeze(1).to_broadcast([P, BT, SLOTS]),
                                    mask_o[:, :, 0].unsqueeze(2).to_broadcast([P, BT, SLOTS]), ALU.mult)\
                     .then_inc(*at.step("abn"))
                elif kind == "3e":
                    dve.wait_ge(*act_at["S3"].after(t, "sihi"))
                    v.tensor_tensor(siT[1][:].rearrange("p k n -> p (k n)"), bank("3e"),
                                    siT[0][:].rearrange("p k n -> p (k n)"), ALU.subtract)\
                     .then_inc(*dve_at["S3"].step("silo"))
                elif kind == "3g":
                    n, = arg_
                    dve.wait_ge(*pe_at["S3"].after(t, "rz", n))
                    v.tensor_tensor(rz[:, n], bank("3g", n), c_rz[:], ALU.add)\
                     .then_inc(*dve_at["S3"].step("rz", n))
                elif kind == "3h":
                    n, = arg_
                    at = dve_at["S3"]
                    dve.wait_ge(*pe_at["S3"].after(t, "n", n))
                    if n == 1:
                        dve.wait_ge(*pool_at["S3"].after(t, "w", 0))
                    v.tensor_tensor(gu[:, 0], bank("3h", n)[:, 0:D], bihn[:], ALU.add)\
                     .then_inc(*at.step("u", n))
                elif kind == "3S":
                    n, = arg_
                    at = dve_at["S3"]
                    dve.wait_ge(*pool_at["S3"].after(t, "d", n))
                    v.scalar_tensor_tensor(gu[:, 5], rz[:, n, D:2 * D], 1.0, gu[:, 4], ALU.add, ALU.mult)\
                     .then_inc(*at.step("q", n))
                    dve.wait_ge(*at.after(t, "q", n))
                    v.scalar_tensor_tensor(s_new[:, n], gu[:, 5], 0.5, gu[:, 3], ALU.mult, ALU.add)\
                     .then_inc(*at.step("S", n))
                elif kind == "3j":
                    dve.wait_ge(*pe_at["S3"].after(t, "y"))
                    if not t.first:
                        dve.wait_ge(out_st, t.times(16, 0))
                    v.tensor_tensor(y_out[:], bank(kind, *arg_)[:, 0:D], x2b[:], ALU.add)\
                     .then_inc(*dve_at["S3"].step("out"))

            before()
            turns("dve", dve, run)

        @block.tensor
        def _(pe):
            def mm(out, lhsT, rhs, start, stop):
                return pe.matmul(out, lhsT, rhs, start=start, stop=stop, skip_group_check=True)

            def split_product(out, terms, start=True, stop=True):
                last = None
                for n, (lh, ll, rh, rl) in enumerate(terms):
                    end = stop and n == len(terms) - 1
                    mm(out, lh, rh, start and n == 0, False)
                    mm(out, lh, rl, False, False)
                    last = mm(out, ll, rh, False, end)
                return last

            def before():
                def features(w32, k32, lo):
                    for k in range(KD):
                        for h in range(pairs):
                            last = mm(banks(lo + 2 * k, lo + 2 * k + 2)[:, h * P:(h + 1) * P],
                                      w32[:, h, k * P:(k + 1) * P], k32[:, h, :], True, True)
                    return last

                pe.wait_ge(features_in, 16 * len(feature_loads))
                features(w2q32, kq32, 0)
                features(w2k32, kk32, 4).then_inc(prep["pe"], 1)
                kv4 = w_kv32.rearrange("p (w k n) -> p w k n", w=4, k=KD)
                cl = ctl.rearrange("p (k n) -> p k n", k=KD)
                pe.wait_ge(w_in, 16 * len(loads))
                pe.wait_ge(prep["dve"], FQ_DONE)
                for w in range(2):
                    for k in range(KD):
                        mm(banks(0, 1)[:, w * D:(w + 1) * D], cl[:, k, :], kv4[:, w, k, :], k == 0, k == KD - 1)
                for w, wo in ((0, kv4[:, 3]), (1, wo3)):
                    for k in range(KD):
                        mm(banks(1, 2)[:, w * D:(w + 1) * D],
                           small[:, 2 * w + k:2 * w + k + 1].to_broadcast([P, P]), wo[:, k, :], k == 0, k == KD - 1)
                for m in range(KD):
                    for k in range(KD):
                        mm(banks(3, 4)[:, m * D:(m + 1) * D], wv3[:, k, m * P:(m + 1) * P], wo3[:, k, :], k == 0,
                           k == KD - 1)
                pe.wait_ge(prep["dve"], HS_DONE)
                for k in range(KD):
                    last = pe.transpose(banks(2, 3)[:, k * P:(k + 1) * P], hs[:, k * P:(k + 1) * P], ident[:])
                last.then_inc(prep["pe"], 1)
                pe.wait_ge(late_in, 16 * len(late_loads))
                pe.wait_ge(prep["dve"], MEAN_DONE)
                hT_ = hsT.rearrange("p (k n) -> p k n", k=KD)
                w1_ = w132.rearrange("p (k n) -> p k n", k=4)
                for bank_no, lo, n in ((4, 0, 512), (5, 512, 256)):
                    for k in range(KD):
                        mm(banks(bank_no, bank_no + 1)[:, 0:n], hT_[:, k, :], whh32[:, k, lo:lo + n], k == 0,
                           k == KD - 1)
                for k in range(KD):
                    last = mm(banks(6, 7)[:, 0:1], w1_[:, KD + k, :], small[:, 4 + k:5 + k], k == 0, k == KD - 1)
                last.then_inc(prep["pe"], 1)
                pe.wait_ge(prep["dve"], DVE_PREP)
                pe.wait_ge(prep["pool"], POOL_PREP)

            def wait_all(*needs):
                for n, need in enumerate(needs):
                    same = [(other.rank, m) for m, other in enumerate(needs) if other[0] is need[0]]
                    if max(same)[1] == n:
                        pe.wait_ge(*need)

            def transposed(stage, t, src, out):
                for k in range(KD):
                    last = pe.transpose(out[:, k * P:(k + 1) * P], src[:, k * P:(k + 1) * P], ident[:])
                last.then_inc(*pe_at[stage].step("xT"))

            def run(item, t):
                kind, arg_, off = item
                stage = stage_of(kind)
                out = bank(kind, *arg_)
                bank_free = bank_read(item, t.shifted(-off))
                if kind == "P1":
                    wait_all(*bank_free, dve_at["P"].after(t, "xn"))
                    transposed("P", t, xn1, out)
                elif kind == "L2b":
                    wait_all(*bank_free, dve_at["S2"].after(t, "xn"))
                    transposed("S2", t, xn2, out)
                elif kind == "3b":
                    wait_all(*bank_free, dve_at["S3"].after(t, "xn"))
                    transposed("S3", t, xn3, out)
                elif kind == "P2":
                    wait_all(*bank_free, dve_at["P"].after(t, "xlo"))
                    for g in range(2):
                        last = split_product(out[:, g * P:(g + 1) * P],
                                             [(WQ[0][:, k, g * P:(g + 1) * P], WQ[1][:, k, g * P:(g + 1) * P],
                                               x1T[0][:, k], x1T[1][:, k]) for k in range(KD)])
                    last.then_inc(*pe_at["P"].step("q"))
                elif kind == "P4":
                    wait_all(*bank_free, act_at["P"].after(t, "qf1"))
                    for n in range(2):
                        last = pe.transpose(out[:, n * P:(n + 1) * P], qf[:, n], ident[:])
                    last.then_inc(*pe_at["P"].step("qn"))
                elif kind == "K":
                    b, = arg_
                    wait_all(*bank_free, pool_at["S1"].after(t, "clo", b))
                    c = [cs[n][:, b % 2] for n in range(2)]
                    for g in range(2):
                        last = split_product(out[:, g * SK:(g + 1) * SK],
                                             [(WK[0][:, k, g * P:(g + 1) * P], WK[1][:, k, g * P:(g + 1) * P],
                                               c[0][:, k], c[1][:, k]) for k in range(KD)])
                    last.then_inc(*pe_at["S1"].step("kT", b))
                elif kind == "VB":
                    b, = arg_
                    wait_all(*bank_free, pool_at["S1"].after(t, "clo", b))
                    c = [cs[n][:, b % 2] for n in range(2)]
                    for m in range(2):
                        last = split_product(out[:, m * D:(m + 1) * D],
                                             [(c[0][:, k, m * P:(m + 1) * P], c[1][:, k, m * P:(m + 1) * P],
                                               WV[0][:, k], WV[1][:, k]) for k in range(KD)])
                    last.then_inc(*pe_at["S1"].step("v", b))
                elif kind == "A":
                    b, = arg_
                    queries = [dve_at["P"].after(t, "bdhi")] if b == 0 else []
                    wait_all(*bank_free, *queries, act_at["S1"].after(t, "kh1", b))
                    for j in range(NQ):
                        q = BD[0][:, j // 2, b].rearrange("p h q -> p (h q)")[:, j % 2 * P:(j % 2 + 1) * P]
                        last = mm(out[:, j * SK:(j + 1) * SK], q, ks[0][:, b % 2, j // 2], True, True)
                    last.then_inc(*pe_at["S1"].step("A", b))
                elif kind == "ST":
                    b, = arg_
                    queries = [pool_at["P"].after(t, "bdlo")] if b == 0 else []
                    wait_all(*bank_free, *queries, dve_at["S1"].after(t, "kl1", b))
                    for m in range(2):
                        for g in range(2):
                            k = [ks[n][:, b % 2, g, m * P:(m + 1) * P] for n in range(2)]
                            q = [BD[n][:, g, b].rearrange("p h q -> p (h q)") for n in range(2)]
                            split_product(out[:, m * 512 + g * 256:m * 512 + (g + 1) * 256],
                                          [(k[0], k[1], q[0], q[1])], start=(g == 0), stop=False)
                    pe.wait_ge(*dve_at["S1"].after(t, "max", b))
                    for m in range(2):
                        for j in range(NQ):
                            last = mm(out[:, m * 512 + j * P:m * 512 + (j + 1) * P],
                                      nmax[:, b, j:j + 1].to_broadcast([P, P]), identb[:], False, True)
                    last.then_inc(*pe_at["S1"].step("ST", b))
                elif kind == "PV":
                    b, = arg_
                    wait_all(*bank_free, pool_at["S1"].after(t, "plo", b), dve_at["S1"].after(t, "vl", b))
                    for j in range(NQ):
                        p = [[ps[n][:, b % 2, m, j * P:(j + 1) * P] for n in range(2)] for m in range(2)]
                        w = [[vs[n][:, b, m, j, :] for n in range(2)] for m in range(2)]
                        last = split_product(out[:, j * 65:(j + 1) * 65],
                                             [(p[m][0], p[m][1], w[m][0], w[m][1]) for m in range(2)])
                    last.then_inc(*pe_at["S1"].step("PV", b))
                elif kind == "C1":
                    wait_all(*bank_free, pool_at["S1"].after(t, "olo", BT - 1))
                    for b in range(BT):
                        for n in range(2):
                            last = mm(out[:, 0:D + 2 * H], collapse[:, b], oms[n][:, b], b == n == 0,
                                      n == 1 and b == BT - 1)
                    last.then_inc(*pe_at["S1"].step("X"))
                elif kind == "C2":
                    wait_all(*bank_free, pool_at["S1"].after(t, "sum"))
                    for k in range(KD):
                        last = pe.transpose(out[:, k * P:(k + 1) * P], wv_l[:, k * P:(k + 1) * P], ident[:])
                    last.then_inc(*pe_at["S1"].step("aT"))
                elif kind == "C3":
                    wait_all(*bank_free, dve_at["S1"].after(t, "alo"))
                    split_product(out[:, 0:D],
                                  [(attT[0][:, k], attT[1][:, k], WO[0][:, k], WO[1][:, k]) for k in range(KD)])\
                        .then_inc(*pe_at["S1"].step("o"))
                elif kind == "F":
                    c, = arg_
                    wait_all(*bank_free, dve_at["S2"].after(t, "xlo"))
                    w, lo = (FQ, FK)[c % 2], c // 2 * 512
                    split_product(out,
                                  [(x2T[0][:, k], x2T[1][:, k], w[0][:, k, lo:lo + 512], w[1][:, k, lo:lo + 512])
                                   for k in range(KD)]).then_inc(*pe_at["S2"].step("f", c))
                elif kind == "V":
                    n, = arg_
                    wait_all(*bank_free, dve_at["S2"].after(t, "xlo"))
                    split_product(out,
                                  [(x2T[0][:, k], x2T[1][:, k], WV2[0][:, k, n * 512:(n + 1) * 512],
                                    WV2[1][:, k, n * 512:(n + 1) * 512]) for k in range(KD)])\
                        .then_inc(*pe_at["S2"].step("v", n))
                elif kind == "T":
                    c, i = arg_
                    wait_all(*bank_free, dve_at["S2"].after(t, "clamp", c))
                    for h in range(4):
                        last = pe.transpose(out[:, h * P:(h + 1) * P],
                                            arg[:, c, 4 * i + h].rearrange("p s f -> p (s f)"), ident[:])
                    last.then_inc(*pe_at["S2"].step("T", c, i))
                elif kind == "AT":
                    g4, = arg_
                    c, i = g4 // 2 * 2, g4 % 2
                    wait_all(*bank_free, act_at["S2"].after(t, "feat", c, i), act_at["S2"].after(t, "feat", c + 1, i))
                    for h in range(4):
                        last = mm(out[:, h * P:(h + 1) * P], featT[:, c + 1, i, h],
                                  featT[:, c, i, h], True, True)
                    last.then_inc(*pe_at["S2"].step("AT", g4))
                elif kind == "AV":
                    g4, = arg_
                    wait_all(*bank_free, dve_at["S2"].after(t, "mask", g4),
                             act_at["S2"].after(t, "v", min(1, (g4 + 1) // 2)))
                    for h in range(4):
                        lo = (4 * g4 + h) * (HD + 1)
                        last = mm(out[:, h * 96:(h + 1) * 96], at_m[:, g4 % 2, h], v1[:, lo:lo + 96], True, True)
                    last.then_inc(*pe_at["S2"].step("AV", g4))
                elif kind == "Y":
                    n, = arg_
                    wait_all(*bank_free, dve_at["S2"].after(t, "y", 2 * n + 1))
                    for h in range(4):
                        last = pe.transpose(out[:, h * P:(h + 1) * P],
                                            y[:, (4 * n + h) * P:(4 * n + h + 1) * P], ident[:])
                    last.then_inc(*pe_at["S2"].step("Y", n))
                elif kind == "W":
                    wait_all(*bank_free, dve_at["S2"].after(t, "ylo", 1))
                    split_product(out[:, 0:D], [(yT[0][:, k], yT[1][:, k], WO2[0][:, k], WO2[1][:, k])
                                                for k in range(8)]).then_inc(*pe_at["S2"].step("W"))
                elif kind == "3c":
                    wait_all(*bank_free, dve_at["S3"].after(t, "xlo"))
                    split_product(out[:, 0:P],
                                  [(W1[0][:, k], W1[1][:, k], x3T[0][:, k], x3T[1][:, k]) for k in range(KD)])\
                        .then_inc(*pe_at["S3"].step("h"))
                elif kind == "3d":
                    wait_all(*bank_free, act_at["S3"].after(t, "gelu"))
                    mm(out[:, 0:SLOTS], hT[:], w2[:], True, True).then_inc(*pe_at["S3"].step("lg"))
                elif kind == "3s":
                    wait_all(*bank_free, dve_at["S3"].after(t, "al"))
                    mm(out[:, 0:SLOTS], same_b[:], lg[:, 0], True, True)\
                        .then_inc(*pe_at["S3"].step("ws"))
                elif kind == "3e":
                    wait_all(*bank_free, dve_at["S3"].after(t, "abn"))
                    for k in range(KD):
                        last = mm(out[:, k * D:(k + 1) * D], xn3[:, k * P:(k + 1) * P],
                                  abn[:].rearrange("p b s -> p (b s)"), True, True)
                    last.then_inc(*pe_at["S3"].step("si"))
                elif kind == "3f":
                    wait_all(*bank_free, dve_at["S3"].after(t, "abd"))
                    ab = abd[:].rearrange("p b s -> p (b s)")
                    for n in range(2):
                        last = pe.transpose(out[:, n * P:(n + 1) * P], ab[:, n * P:(n + 1) * P], ident[:])
                    last.then_inc(*pe_at["S3"].step("aT"))
                elif kind in ("3g", "3h"):
                    n, = arg_
                    lo, w, name = (0, 2 * D, "rz") if kind == "3g" else (2 * D, D, "n")
                    wait_all(*bank_free, dve_at["S3"].after(t, "silo"))
                    split_product(out[:, 0:w], [(siT[0][:, k, n * P:(n + 1) * P], siT[1][:, k, n * P:(n + 1) * P],
                                                 WIH[0][:, k, lo:lo + w], WIH[1][:, k, lo:lo + w])
                                                for k in range(KD)]).then_inc(*pe_at["S3"].step(name, n))
                elif kind == "3i":
                    wait_all(*bank_free, dve_at["S3"].after(t, "S", 1))
                    for k in range(KD):
                        for n in range(2):
                            last = mm(out[:, k * P:(k + 1) * P], s_new[:, n, k * P:(k + 1) * P], aT[:, n], n == 0,
                                      n == 1)
                    last.then_inc(*pe_at["S3"].step("as"))
                elif kind == "3j":
                    wait_all(*bank_free, act_at["S3"].after(t, "as"))
                    for k in range(KD):
                        last = mm(out[:, 0:D], asT[:, k], gvo[:, k], k == 0, k == KD - 1)
                    last.then_inc(*pe_at["S3"].step("y"))

            before()
            turns("pe", pe, run)


FQ_DONE, FK_DONE = 2, 4
HS_DONE = 14
HST_DONE = 15
KVL_DONE = 17
MEAN_DONE = 19
WV2_DONE = 27
DVE_PREP = 34


def kernel(**inputs):
    import numpy as _np
    import concourse.bacc as _bacc
    from concourse import mybir as _mybir
    from concourse.bass_utils import run_bass_kernel_spmd as _run

    i = {k: _np.asarray(v) for k, v in inputs.items()}
    n_b = i["x"].shape[0]
    tiles = n_b // BT

    def chunks(w):
        return _np.ascontiguousarray(w.reshape(-1, P, w.shape[1]).transpose(1, 0, 2))

    def column(b):
        return _np.ascontiguousarray(b.reshape(-1, P).T)

    def heads(w):
        return _np.ascontiguousarray(w.reshape(D, H // 2, P).transpose(2, 1, 0))

    def head_blocks(k):
        return _np.ascontiguousarray(k.reshape(H // 2, P, HD).transpose(1, 0, 2))

    c = i["ctx_1024"]
    arrays = {
        "x": i["x"].reshape(tiles, P, D),
        "ctx": _np.ascontiguousarray(c[:, :SK].reshape(n_b, SK, KD, P).transpose(0, 3, 2, 1)),
        "ctx_last": _np.ascontiguousarray(c[:, SK].reshape(n_b, KD, P).transpose(2, 1, 0)),
        "xWq": chunks(i["L0_xattn_Wq"].T), "xWk": chunks(i["L0_xattn_Wk"].T), "xWv": chunks(i["L0_xattn_Wv"].T),
        "xWo": chunks(i["L0_xattn_Wo"].T),
        "xbk": i["L0_xattn_bk"], "xbo": i["L0_xattn_bo"],
        "xbv": column(i["L0_xattn_bv"]), "xbq_col": column(i["L0_xattn_bq"]), "xbk_col": column(i["L0_xattn_bk"]),
        "aWq": heads(i["L0_attn_Wq"]), "aWk": heads(i["L0_attn_Wk"]), "aWv": chunks(i["L0_attn_Wv"]),
        "aWo": chunks(i["L0_attn_Wo"]),
        "aKq": head_blocks(i["L0_attn_Kq"]),
        "aKk": head_blocks(i["L0_attn_Kk"]),
        "slot_init": i["L0_ffn_slot_init"], "slot_scale": i["L0_ffn_slot_scale"],
        "fw1": chunks(i["L0_ffn_w1"].T), "fb1": column(i["L0_ffn_b1"]),
        "fw2": _np.ascontiguousarray(i["L0_ffn_w2"].T), "fb2": i["L0_ffn_b2"],
        "fwih": chunks(i["L0_ffn_gru_wih"].T), "fwhh": chunks(i["L0_ffn_gru_whh"].T),
        "fbih": i["L0_ffn_gru_bih"], "fbhh": i["L0_ffn_gru_bhh"],
        "fWv": chunks(i["L0_ffn_wv"]), "fbv": column(i["L0_ffn_bv"]),
        "fWo": chunks(i["L0_ffn_wo"].T), "fbo": i["L0_ffn_bo"], "tau": i["L0_ffn_tau"],
    }
    nc = _bacc.Bacc("TRN2", target_bir_lowering=False, num_devices=1)
    sent, aps = {}, {}
    for name, v in arrays.items():
        v = _np.ascontiguousarray(v)
        sent[f"in_{name}"] = v
        aps[name] = nc.dram_tensor(f"in_{name}", v.shape, _mybir.dt.from_np(v.dtype), kind="ExternalInput").ap()
    aps["out"] = nc.dram_tensor("out_0", (tiles, P, D), F32, kind="ExternalOutput").ap()
    bass_perceiver_layer(nc, aps, tiles)
    r = _run(nc, [sent], core_ids=[0])
    return r.results[0]["out_0"].reshape(n_b, SQ, D)
```
